# Optimizing a Trainium2 kernel written in Bass

```python
import numpy as np
import jax
import jax.numpy as jnp

def _softmax(x, axis=-1):
    return jax.nn.softmax(x, axis=axis)

def _gelu(x):
    return jax.nn.gelu(x, approximate=True)

def _silu(x):
    return jax.nn.silu(x)

def _sigmoid(x):
    return jax.nn.sigmoid(x)

def _layernorm(x, axis=-1, eps=1e-05):
    m = jnp.mean(x, axis=axis, keepdims=True)
    v = jnp.var(x, axis=axis, keepdims=True)
    return (x - m) / jnp.sqrt(v + eps)

def _scatter_add(tgt, idx, src, axis=0):
    return tgt.at[idx].add(src)

def _segment_sum(src, seg, n):
    return jax.ops.segment_sum(src, seg, n)
kernel_name = 'mk_adj_ffn_d4_adj_r2_7293e4'

def setup_inputs(seed: int=0):
    np.random.seed(seed)
    _w = jnp.asarray

    def _rec_inputs():
        import jax
        import jax.numpy as jnp
        _gk = jax.random.key(seed)
        x = -0.0001177 + 0.9999 * jax.random.normal(jax.random.fold_in(_gk, 1), (128, 40, 128), jnp.float32)
        _a = jax.random.bernoulli(jax.random.fold_in(_gk, 2), 0.1, (128, 40, 40))
        _a = jnp.logical_or(_a, jnp.swapaxes(_a, -1, -2))
        _a = jnp.logical_or(_a, jnp.eye(40, dtype=bool))
        _af = _a.astype(jnp.float32)
        _af = _af * jax.random.uniform(jax.random.fold_in(_gk, 3), (128, 40, 40), jnp.float32, 0.05, 0.999837)
        adj = _af
        _nm = jnp.ones((128, 40), dtype=bool)
        nodemask = jnp.where(_nm, 1.0, 0.0).astype(jnp.float32)
        return (x, adj, nodemask)
    x, adj, nodemask = _rec_inputs()

    def _L0_gnn_setup():
        import jax, jax.numpy as jnp
        import numpy as np
        EPS = 1e-05
        NBLK = 4
        BLK = 10
        key = jax.random.key(seed)
        k1, k2, k3 = jax.random.split(key, 3)
        B, N, Fin, Fout = (4096, 40, 128, 128)
        inp = jax.random.normal(k1, (B, N, Fin), dtype=jnp.float32)
        adj = jax.random.uniform(k2, (B, N, N), dtype=jnp.float32)
        stdv = 1.0 / np.sqrt(Fout)
        W = jax.random.uniform(k3, (Fin, Fout), dtype=jnp.float32, minval=-stdv, maxval=stdv)
        bn_gamma = jnp.ones((NBLK, N * Fout), dtype=jnp.float32)
        bn_beta = jnp.zeros((NBLK, N * Fout), dtype=jnp.float32)
        return {'input': inp, 'adj': adj, 'W': W, 'bn_gamma': bn_gamma, 'bn_beta': bn_beta}
    _L0_gnn_all = _L0_gnn_setup()
    _L0_gnn_in = {k: v for k, v in _L0_gnn_all.items() if k in ('W', 'bn_gamma', 'bn_beta')}
    del _L0_gnn_all

    def _L0_ffn_setup():
        import jax, jax.numpy as jnp
        import numpy as np
        H, P, G, NS, K = (8, 64, 64, 64, 3)
        D_INNER = H * P
        CONV_DIM = D_INNER + 2 * NS
        D_IN_PROJ = 2 * D_INNER + 2 * NS + 2 * H

        def _hydra(u, in_w, conv_w, conv_b, dt_bias, A_log, Dp, fcD_w, norm_w, out_w):
            Bt, L, _ = u.shape
            zxbcdt = u @ in_w.T
            z = zxbcdt[..., :D_INNER]
            xBC = zxbcdt[..., D_INNER:D_INNER + CONV_DIM]
            dt = zxbcdt[..., -2 * H:]
            dt = jnp.concatenate([dt[..., :H], jnp.flip(dt[..., H:], axis=1)], axis=0)
            dt = jax.nn.softplus(dt + dt_bias)
            xp = jnp.pad(xBC, ((0, 0), (K - 1, 0), (0, 0)))
            xBC = sum((xp[:, k:k + L, :] * conv_w[:, k] for k in range(K))) + conv_b
            xBC = jax.nn.silu(xBC)
            x = xBC[..., :D_INNER]
            Bm = xBC[..., D_INNER:D_INNER + NS]
            Cm = xBC[..., D_INNER + NS:]
            x_og = x
            x2 = jnp.concatenate([x, jnp.flip(x, 1)], 0).reshape(2 * Bt, L, H, P)
            B2 = jnp.concatenate([Bm, jnp.flip(Bm, 1)], 0)
            C2 = jnp.concatenate([Cm, jnp.flip(Cm, 1)], 0)
            dA = jnp.exp(dt * -jnp.exp(A_log))
            dBx = jnp.einsum('blh,bln,blhp->blhpn', dt, B2, x2)

            def step(h, inp):
                dA_t, dBx_t, C_t = inp
                h = h * dA_t[:, :, None, None] + dBx_t
                return (h, jnp.einsum('bhpn,bn->bhp', h, C_t))
            h0 = jnp.zeros((2 * Bt, H, P, NS), u.dtype)
            _, ys = jax.lax.scan(step, h0, (dA.transpose(1, 0, 2), dBx.transpose(1, 0, 2, 3, 4), C2.transpose(1, 0, 2)))
            y = ys.transpose(1, 0, 2, 3).reshape(2 * Bt, L, D_INNER)
            y_fw, y_bw = (y[:Bt], jnp.flip(y[Bt:], 1))
            y = jnp.pad(y_fw[:, :-1], ((0, 0), (1, 0), (0, 0))) + jnp.pad(y_bw[:, 1:], ((0, 0), (0, 1), (0, 0)))
            y = y + x_og * jnp.repeat(x_og @ fcD_w.T + Dp, P, axis=-1)
            yg = y * jax.nn.silu(z)
            yg = yg * jax.lax.rsqrt(jnp.mean(jnp.square(yg), -1, keepdims=True) + 1e-05) * norm_w
            return yg @ out_w.T
        key = jax.random.key(seed)
        ks = jax.random.split(key, 10)
        dim, Bsz, N = (128, 4, 4096)
        s = 0.02
        return {'x': jax.random.normal(ks[0], (Bsz, N, dim), jnp.float32), 'W_fx': jax.random.normal(ks[1], (D_INNER, dim), jnp.float32) * s, 'b_fx': jnp.zeros((D_INNER,), jnp.float32), 'W_x': jax.random.normal(ks[2], (D_INNER, dim), jnp.float32) * s, 'b_x': jnp.zeros((D_INNER,), jnp.float32), 'W_slice': jax.random.normal(ks[3], (G, P), jnp.float32) * s, 'b_slice': jnp.zeros((G,), jnp.float32), 'temperature': jnp.full((1, H, 1, 1), 0.5, jnp.float32), 'hy_in_w': jax.random.normal(ks[4], (D_IN_PROJ, D_INNER), jnp.float32) * s, 'hy_conv_w': jax.random.normal(ks[5], (CONV_DIM, K), jnp.float32) * s, 'hy_conv_b': jnp.zeros((CONV_DIM,), jnp.float32), 'hy_dt_bias': jnp.log(jnp.expm1(jnp.full((H,), 0.01, jnp.float32))), 'hy_A_log': jnp.log(jnp.linspace(1.0, 16.0, H)).astype(jnp.float32), 'hy_D': jnp.ones((H,), jnp.float32), 'hy_fcD_w': jax.random.normal(ks[6], (H, D_INNER), jnp.float32) * s, 'hy_norm_w': jnp.ones((D_INNER,), jnp.float32), 'hy_out_w': jax.random.normal(ks[7], (D_INNER, D_INNER), jnp.float32) * s, 'out_w': jax.random.normal(ks[8], (dim, D_INNER), jnp.float32) * s, 'out_b': jnp.zeros((dim,), jnp.float32)}
    _L0_ffn_all = _L0_ffn_setup()
    _L0_ffn_in = {k: v for k, v in _L0_ffn_all.items() if k in ('W_fx', 'b_fx', 'W_x', 'b_x', 'W_slice', 'b_slice', 'temperature', 'hy_in_w', 'hy_conv_w', 'hy_conv_b', 'hy_dt_bias', 'hy_A_log', 'hy_D', 'hy_fcD_w', 'hy_norm_w', 'hy_out_w', 'out_w', 'out_b')}
    del _L0_ffn_all

    def _L1_gnn_setup():
        import math
        import jax, jax.numpy as jnp
        import numpy as np
        B, N, DIN, DOUT = (64, 256, 128, 128)
        EPS = 1e-05
        key = jax.random.key(seed)
        k0, k1, k2, k3 = jax.random.split(key, 4)
        x = jax.random.normal(k0, (B, N, DIN), dtype=jnp.float32)
        adj = jax.random.uniform(k1, (B, N, N), dtype=jnp.float32) / N
        lengths = jax.random.randint(k2, (B,), N // 4, N + 1)
        mask = (jnp.arange(N)[None, :] < lengths[:, None]).astype(jnp.float32)
        std = math.sqrt(2.0 / (DIN + DOUT))
        weight = jax.random.normal(k3, (DIN, DOUT), dtype=jnp.float32) * std
        bias = jnp.zeros((DOUT,), dtype=jnp.float32)
        gamma = jnp.ones((DOUT,), dtype=jnp.float32)
        beta = jnp.zeros((DOUT,), dtype=jnp.float32)
        return {'x': x, 'adj': adj, 'mask': mask, 'weight': weight, 'bias': bias, 'gamma': gamma, 'beta': beta}
    _L1_gnn_all = _L1_gnn_setup()
    _L1_gnn_in = {k: v for k, v in _L1_gnn_all.items() if k in ('weight', 'bias', 'gamma', 'beta')}
    del _L1_gnn_all

    def _L1_ffn_setup():
        import jax, jax.numpy as jnp
        import numpy as np
        E = 8
        K = 2
        D = 128
        H = 256
        DOUT = 128
        EPS = 1e-05
        key = jax.random.key(seed)
        ks = jax.random.split(key, 9)
        s = 0.02
        return {'x': jax.random.normal(ks[0], (4, 4096, D), jnp.float32), 'gamma': 1.0 + 0.05 * jax.random.normal(ks[1], (D,), jnp.float32), 'beta': 0.05 * jax.random.normal(ks[2], (D,), jnp.float32), 'Wr': 0.01 * jax.random.normal(ks[3], (D, E), jnp.float32), 'br': jnp.zeros((E,), jnp.float32), 'W1': s * jax.random.normal(ks[4], (E, D, H), jnp.float32), 'b1': s * jax.random.normal(ks[5], (E, H), jnp.float32), 'W2': s * jax.random.normal(ks[6], (E, H, DOUT), jnp.float32), 'b2': s * jax.random.normal(ks[7], (E, DOUT), jnp.float32)}
    _L1_ffn_all = _L1_ffn_setup()
    _L1_ffn_in = {k: v for k, v in _L1_ffn_all.items() if k in ('gamma', 'beta', 'Wr', 'br', 'W1', 'b1', 'W2', 'b2')}
    del _L1_ffn_all

    def _L2_gnn_setup():
        import jax, jax.numpy as jnp
        import numpy as np
        HIDDEN = 128
        NEG_INF = -1e+30
        key = jax.random.key(seed)
        k1, k2, k3, k4 = jax.random.split(key, 4)
        B, S, H = (4, 2048, HIDDEN)
        matrix = jax.random.normal(k1, (B, S, H), dtype=jnp.float32)
        mask = jax.random.randint(k2, (B, S), 0, 2, dtype=jnp.int32)
        adj = jax.random.uniform(k3, (B, S, S), dtype=jnp.float32)
        limit = float(np.sqrt(6.0 / (H + H)))
        W = jax.random.uniform(k4, (H, H), dtype=jnp.float32, minval=-limit, maxval=limit)
        return {'matrix': matrix, 'mask': mask, 'adj': adj, 'W': W}
    _L2_gnn_all = _L2_gnn_setup()
    _L2_gnn_in = {k: v for k, v in _L2_gnn_all.items() if k in ('W',)}
    del _L2_gnn_all

    def _L2_ffn_setup():
        import jax, jax.numpy as jnp
        import numpy as np
        B, N, D = (16, 2048, 128)
        NUM_EXPERTS, TOP_K, HEADS = (4, 2, 4)
        N_EDGES = 524288
        LN_EPS = 1e-05

        def _layernorm(x, g, b):
            mu = x.mean(-1, keepdims=True)
            var = ((x - mu) ** 2).mean(-1, keepdims=True)
            return (x - mu) * jax.lax.rsqrt(var + LN_EPS) * g + b

        def _forward(x, edge_index, W_gat, att_src, att_dst, b_gat, ln_gamma, ln_beta, W1, b1, W2, b2):
            Bc, Nc, Dc = x.shape
            M = Bc * Nc
            x_flat = x.reshape(M, Dc)
            h = (x_flat @ W_gat).reshape(M, HEADS, NUM_EXPERTS)
            loops = jnp.arange(M, dtype=edge_index.dtype)
            src = jnp.concatenate([edge_index[0], loops])
            dst = jnp.concatenate([edge_index[1], loops])
            a_src = (h * att_src).sum(-1)
            a_dst = (h * att_dst).sum(-1)
            e = jax.nn.leaky_relu(a_src[src] + a_dst[dst], negative_slope=0.2)
            e_max = jax.ops.segment_max(e, dst, num_segments=M)
            ee = jnp.exp(e - e_max[dst])
            denom = jax.ops.segment_sum(ee, dst, num_segments=M)
            alpha = ee / (denom[dst] + 1e-16)
            msg = h[src] * alpha[:, :, None]
            agg = jax.ops.segment_sum(msg, dst, num_segments=M).reshape(M, HEADS * NUM_EXPERTS) + b_gat
            scores = _layernorm(agg, ln_gamma, ln_beta).reshape(M, HEADS, NUM_EXPERTS).mean(1)
            scores = scores.reshape(Bc, Nc, NUM_EXPERTS)
            topk_s, topk_i = jax.lax.top_k(scores, TOP_K)
            w = jax.nn.softmax(topk_s, axis=-1)
            out = jnp.zeros_like(x)
            for ei in range(NUM_EXPERTS):
                g = jnp.where(topk_i == ei, w, 0.0).sum(-1)
                hh = jax.nn.gelu(x @ W1[ei] + b1[ei], approximate=False)
                out = out + g[..., None] * (hh @ W2[ei] + b2[ei])
            return out
        key = jax.random.key(seed)
        ks = jax.random.split(key, 8)
        s = 0.05
        return {'x': jax.random.normal(ks[0], (B, N, D), jnp.float32), 'W_gat': jax.random.normal(ks[1], (D, HEADS * NUM_EXPERTS), jnp.float32) * s, 'att_src': jax.random.normal(ks[2], (HEADS, NUM_EXPERTS), jnp.float32) * s, 'att_dst': jax.random.normal(ks[3], (HEADS, NUM_EXPERTS), jnp.float32) * s, 'b_gat': jnp.zeros((HEADS * NUM_EXPERTS,), jnp.float32), 'ln_gamma': jnp.ones((HEADS * NUM_EXPERTS,), jnp.float32), 'ln_beta': jnp.zeros((HEADS * NUM_EXPERTS,), jnp.float32), 'W1': jax.random.normal(ks[4], (NUM_EXPERTS, D, 2 * D), jnp.float32) * s, 'b1': jnp.zeros((NUM_EXPERTS, 2 * D), jnp.float32), 'W2': jax.random.normal(ks[5], (NUM_EXPERTS, 2 * D, D), jnp.float32) * s, 'b2': jnp.zeros((NUM_EXPERTS, D), jnp.float32), 'edge_index': jax.random.randint(ks[6], (2, N_EDGES), 0, B * N, jnp.int32)}
    _L2_ffn_all = _L2_ffn_setup()
    _L2_ffn_in = {k: v for k, v in _L2_ffn_all.items() if k in ('W_gat', 'att_src', 'att_dst', 'b_gat', 'ln_gamma', 'ln_beta', 'W1', 'b1', 'W2', 'b2', 'edge_index')}
    del _L2_ffn_all

    def _L3_gnn_setup():
        import jax, jax.numpy as jnp
        import numpy as np
        DIM = 128
        HEADS = 8
        BS = 8
        N = 512
        NEG = -1000000000.0
        key = jax.random.key(seed)
        ks = jax.random.split(key, 8)
        feats = jax.random.normal(ks[0], (BS, N, DIM), dtype=jnp.float32)
        adj_mat = (jax.random.uniform(ks[1], (BS, N, N)) < 0.1).astype(jnp.float32)
        s = 1.0 / np.sqrt(DIM)
        fc_w = jax.random.normal(ks[2], (DIM, DIM * HEADS), dtype=jnp.float32) * s
        fc_b = jnp.zeros((DIM * HEADS,), dtype=jnp.float32)
        q_w = jax.random.normal(ks[3], (DIM, 1), dtype=jnp.float32) * s
        q_b = jnp.zeros((1,), dtype=jnp.float32)
        k_w = jax.random.normal(ks[4], (DIM, 1), dtype=jnp.float32) * s
        k_b = jnp.zeros((1,), dtype=jnp.float32)
        fp_w = jax.random.normal(ks[5], (DIM * HEADS, DIM), dtype=jnp.float32) * (1.0 / np.sqrt(DIM * HEADS))
        fp_b = jnp.zeros((DIM,), dtype=jnp.float32)
        return {'feats': feats, 'adj_mat': adj_mat, 'fc_w': fc_w, 'fc_b': fc_b, 'q_w': q_w, 'q_b': q_b, 'k_w': k_w, 'k_b': k_b, 'fp_w': fp_w, 'fp_b': fp_b}
    _L3_gnn_all = _L3_gnn_setup()
    _L3_gnn_in = {k: v for k, v in _L3_gnn_all.items() if k in ('fc_w', 'fc_b', 'q_w', 'q_b', 'k_w', 'k_b', 'fp_w', 'fp_b')}
    del _L3_gnn_all

    def _L3_ffn_setup():
        import jax, jax.numpy as jnp
        import numpy as np
        B, S, D, E, H, K = (4, 2048, 128, 8, 256, 2)
        key = jax.random.key(seed)
        ks = jax.random.split(key, 6)
        x = jax.random.normal(ks[0], (B, S, D), jnp.float32)
        Wg = jax.random.normal(ks[1], (D, E), jnp.float32) * 0.02
        bg = jnp.zeros((E,), jnp.float32)
        W1 = jax.random.normal(ks[2], (E, D, H), jnp.float32) * 0.02
        b1 = jnp.zeros((E, H), jnp.float32)
        W2 = jax.random.normal(ks[3], (E, H, D), jnp.float32) * 0.02
        b2 = jnp.zeros((E, D), jnp.float32)
        return {'x': x, 'Wg': Wg, 'bg': bg, 'W1': W1, 'b1': b1, 'W2': W2, 'b2': b2}
    _L3_ffn_all = _L3_ffn_setup()
    _L3_ffn_in = {k: v for k, v in _L3_ffn_all.items() if k in ('Wg', 'bg', 'W1', 'b1', 'W2', 'b2')}
    del _L3_ffn_all
    return {'x': x, 'adj': adj, 'nodemask': nodemask, 'L0_gnn_W': _L0_gnn_in['W'], 'L0_gnn_bn_gamma': _L0_gnn_in['bn_gamma'], 'L0_gnn_bn_beta': _L0_gnn_in['bn_beta'], 'L0_ffn_W_fx': _L0_ffn_in['W_fx'], 'L0_ffn_b_fx': _L0_ffn_in['b_fx'], 'L0_ffn_W_x': _L0_ffn_in['W_x'], 'L0_ffn_b_x': _L0_ffn_in['b_x'], 'L0_ffn_W_slice': _L0_ffn_in['W_slice'], 'L0_ffn_b_slice': _L0_ffn_in['b_slice'], 'L0_ffn_temperature': _L0_ffn_in['temperature'], 'L0_ffn_hy_in_w': _L0_ffn_in['hy_in_w'], 'L0_ffn_hy_conv_w': _L0_ffn_in['hy_conv_w'], 'L0_ffn_hy_conv_b': _L0_ffn_in['hy_conv_b'], 'L0_ffn_hy_dt_bias': _L0_ffn_in['hy_dt_bias'], 'L0_ffn_hy_A_log': _L0_ffn_in['hy_A_log'], 'L0_ffn_hy_D': _L0_ffn_in['hy_D'], 'L0_ffn_hy_fcD_w': _L0_ffn_in['hy_fcD_w'], 'L0_ffn_hy_norm_w': _L0_ffn_in['hy_norm_w'], 'L0_ffn_hy_out_w': _L0_ffn_in['hy_out_w'], 'L0_ffn_out_w': _L0_ffn_in['out_w'], 'L0_ffn_out_b': _L0_ffn_in['out_b'], 'L1_gnn_weight': _L1_gnn_in['weight'], 'L1_gnn_bias': _L1_gnn_in['bias'], 'L1_gnn_gamma': _L1_gnn_in['gamma'], 'L1_gnn_beta': _L1_gnn_in['beta'], 'L1_ffn_gamma': _L1_ffn_in['gamma'], 'L1_ffn_beta': _L1_ffn_in['beta'], 'L1_ffn_Wr': _L1_ffn_in['Wr'], 'L1_ffn_br': _L1_ffn_in['br'], 'L1_ffn_W1': _L1_ffn_in['W1'], 'L1_ffn_b1': _L1_ffn_in['b1'], 'L1_ffn_W2': _L1_ffn_in['W2'], 'L1_ffn_b2': _L1_ffn_in['b2'], 'L2_gnn_W': _L2_gnn_in['W'], 'L2_ffn_W_gat': _L2_ffn_in['W_gat'], 'L2_ffn_att_src': _L2_ffn_in['att_src'], 'L2_ffn_att_dst': _L2_ffn_in['att_dst'], 'L2_ffn_b_gat': _L2_ffn_in['b_gat'], 'L2_ffn_ln_gamma': _L2_ffn_in['ln_gamma'], 'L2_ffn_ln_beta': _L2_ffn_in['ln_beta'], 'L2_ffn_W1': _L2_ffn_in['W1'], 'L2_ffn_b1': _L2_ffn_in['b1'], 'L2_ffn_W2': _L2_ffn_in['W2'], 'L2_ffn_b2': _L2_ffn_in['b2'], 'L2_ffn_edge_index': _L2_ffn_in['edge_index'], 'L3_gnn_fc_w': _L3_gnn_in['fc_w'], 'L3_gnn_fc_b': _L3_gnn_in['fc_b'], 'L3_gnn_q_w': _L3_gnn_in['q_w'], 'L3_gnn_q_b': _L3_gnn_in['q_b'], 'L3_gnn_k_w': _L3_gnn_in['k_w'], 'L3_gnn_k_b': _L3_gnn_in['k_b'], 'L3_gnn_fp_w': _L3_gnn_in['fp_w'], 'L3_gnn_fp_b': _L3_gnn_in['fp_b'], 'L3_ffn_Wg': _L3_ffn_in['Wg'], 'L3_ffn_bg': _L3_ffn_in['bg'], 'L3_ffn_W1': _L3_ffn_in['W1'], 'L3_ffn_b1': _L3_ffn_in['b1'], 'L3_ffn_W2': _L3_ffn_in['W2'], 'L3_ffn_b2': _L3_ffn_in['b2']}

def reference(x, adj, nodemask, L0_gnn_W, L0_gnn_bn_gamma, L0_gnn_bn_beta, L0_ffn_W_fx, L0_ffn_b_fx, L0_ffn_W_x, L0_ffn_b_x, L0_ffn_W_slice, L0_ffn_b_slice, L0_ffn_temperature, L0_ffn_hy_in_w, L0_ffn_hy_conv_w, L0_ffn_hy_conv_b, L0_ffn_hy_dt_bias, L0_ffn_hy_A_log, L0_ffn_hy_D, L0_ffn_hy_fcD_w, L0_ffn_hy_norm_w, L0_ffn_hy_out_w, L0_ffn_out_w, L0_ffn_out_b, L1_gnn_weight, L1_gnn_bias, L1_gnn_gamma, L1_gnn_beta, L1_ffn_gamma, L1_ffn_beta, L1_ffn_Wr, L1_ffn_br, L1_ffn_W1, L1_ffn_b1, L1_ffn_W2, L1_ffn_b2, L2_gnn_W, L2_ffn_W_gat, L2_ffn_att_src, L2_ffn_att_dst, L2_ffn_b_gat, L2_ffn_ln_gamma, L2_ffn_ln_beta, L2_ffn_W1, L2_ffn_b1, L2_ffn_W2, L2_ffn_b2, L2_ffn_edge_index, L3_gnn_fc_w, L3_gnn_fc_b, L3_gnn_q_w, L3_gnn_q_b, L3_gnn_k_w, L3_gnn_k_b, L3_gnn_fp_w, L3_gnn_fp_b, L3_ffn_Wg, L3_ffn_bg, L3_ffn_W1, L3_ffn_b1, L3_ffn_W2, L3_ffn_b2):
    import jax
    import jax.numpy as jnp

    def _L0_gnn_ref(input, adj, W, bn_gamma, bn_beta):
        import jax, jax.numpy as jnp
        import numpy as np
        EPS = 1e-05
        NBLK = 4
        BLK = 10
        B, N, _ = input.shape
        Fout = W.shape[1]
        support = jnp.einsum('bnf,fo->bno', input, W)
        out = jnp.zeros((B, N, Fout), dtype=input.dtype)
        for i in range(NBLK):
            s, e = (i * BLK, (i + 1) * BLK)
            blk = jnp.einsum('bij,bjo->bio', adj[:, s:e, s:e], support[:, s:e, :])
            full = jnp.zeros((B, N, Fout), dtype=input.dtype).at[:, s:e, :].set(blk)
            flat = full.reshape(B, N * Fout)
            mean = jnp.mean(flat, axis=0)
            var = jnp.var(flat, axis=0)
            normed = (flat - mean) * jax.lax.rsqrt(var + EPS) * bn_gamma[i] + bn_beta[i]
            out = out + normed.reshape(B, N, Fout)
        return out

    def _L0_ffn_ref(x, W_fx, b_fx, W_x, b_x, W_slice, b_slice, temperature, hy_in_w, hy_conv_w, hy_conv_b, hy_dt_bias, hy_A_log, hy_D, hy_fcD_w, hy_norm_w, hy_out_w, out_w, out_b):
        import jax, jax.numpy as jnp
        import numpy as np
        H, P, G, NS, K = (8, 64, 64, 64, 3)
        D_INNER = H * P
        CONV_DIM = D_INNER + 2 * NS
        D_IN_PROJ = 2 * D_INNER + 2 * NS + 2 * H

        def _hydra(u, in_w, conv_w, conv_b, dt_bias, A_log, Dp, fcD_w, norm_w, out_w):
            Bt, L, _ = u.shape
            zxbcdt = u @ in_w.T
            z = zxbcdt[..., :D_INNER]
            xBC = zxbcdt[..., D_INNER:D_INNER + CONV_DIM]
            dt = zxbcdt[..., -2 * H:]
            dt = jnp.concatenate([dt[..., :H], jnp.flip(dt[..., H:], axis=1)], axis=0)
            dt = jax.nn.softplus(dt + dt_bias)
            xp = jnp.pad(xBC, ((0, 0), (K - 1, 0), (0, 0)))
            xBC = sum((xp[:, k:k + L, :] * conv_w[:, k] for k in range(K))) + conv_b
            xBC = jax.nn.silu(xBC)
            x = xBC[..., :D_INNER]
            Bm = xBC[..., D_INNER:D_INNER + NS]
            Cm = xBC[..., D_INNER + NS:]
            x_og = x
            x2 = jnp.concatenate([x, jnp.flip(x, 1)], 0).reshape(2 * Bt, L, H, P)
            B2 = jnp.concatenate([Bm, jnp.flip(Bm, 1)], 0)
            C2 = jnp.concatenate([Cm, jnp.flip(Cm, 1)], 0)
            dA = jnp.exp(dt * -jnp.exp(A_log))
            dBx = jnp.einsum('blh,bln,blhp->blhpn', dt, B2, x2)

            def step(h, inp):
                dA_t, dBx_t, C_t = inp
                h = h * dA_t[:, :, None, None] + dBx_t
                return (h, jnp.einsum('bhpn,bn->bhp', h, C_t))
            h0 = jnp.zeros((2 * Bt, H, P, NS), u.dtype)
            _, ys = jax.lax.scan(step, h0, (dA.transpose(1, 0, 2), dBx.transpose(1, 0, 2, 3, 4), C2.transpose(1, 0, 2)))
            y = ys.transpose(1, 0, 2, 3).reshape(2 * Bt, L, D_INNER)
            y_fw, y_bw = (y[:Bt], jnp.flip(y[Bt:], 1))
            y = jnp.pad(y_fw[:, :-1], ((0, 0), (1, 0), (0, 0))) + jnp.pad(y_bw[:, 1:], ((0, 0), (0, 1), (0, 0)))
            y = y + x_og * jnp.repeat(x_og @ fcD_w.T + Dp, P, axis=-1)
            yg = y * jax.nn.silu(z)
            yg = yg * jax.lax.rsqrt(jnp.mean(jnp.square(yg), -1, keepdims=True) + 1e-05) * norm_w
            return yg @ out_w.T
        B, N, _ = x.shape
        fx = (x @ W_fx.T + b_fx).reshape(B, N, H, P).transpose(0, 2, 1, 3)
        xm = (x @ W_x.T + b_x).reshape(B, N, H, P).transpose(0, 2, 1, 3)
        temp = jnp.maximum(temperature, 1e-06)
        sw = jax.nn.softmax((xm @ W_slice.T + b_slice) / temp, axis=-1)
        snorm = sw.sum(2)
        st = jnp.einsum('bhnc,bhng->bhgc', fx, sw) / (snorm + 1e-05)[..., None]
        st = st.transpose(0, 2, 1, 3).reshape(B, G, D_INNER)
        ot = _hydra(st, hy_in_w, hy_conv_w, hy_conv_b, hy_dt_bias, hy_A_log, hy_D, hy_fcD_w, hy_norm_w, hy_out_w)
        ot = ot.reshape(B, G, H, P).transpose(0, 2, 1, 3)
        out = jnp.einsum('bhgc,bhng->bhnc', ot, sw).transpose(0, 2, 1, 3).reshape(B, N, D_INNER)
        return out @ out_w.T + out_b

    def _L1_gnn_ref(x, adj, mask, weight, bias, gamma, beta):
        import math
        import jax, jax.numpy as jnp
        import numpy as np
        B, N, DIN, DOUT = (64, 256, 128, 128)
        EPS = 1e-05
        y = jnp.einsum('bnm,bmd->bnd', adj, x)
        y = jnp.einsum('bnd,de->bne', y, weight) + bias
        m = mask[:, :, None]
        n = jnp.sum(mask)
        mean = jnp.sum(y * m, axis=(0, 1)) / n
        var = jnp.sum((y - mean) ** 2 * m, axis=(0, 1)) / n
        y = ((y - mean) * jax.lax.rsqrt(var + EPS) * gamma + beta) * m
        return jax.nn.relu(y)

    def _L1_ffn_ref(x, gamma, beta, Wr, br, W1, b1, W2, b2):
        import jax, jax.numpy as jnp
        import numpy as np
        E = 8
        K = 2
        D = 128
        H = 256
        DOUT = 128
        EPS = 1e-05
        mu = jnp.mean(x, axis=-1, keepdims=True)
        var = jnp.mean(jnp.square(x - mu), axis=-1, keepdims=True)
        xn = (x - mu) * jax.lax.rsqrt(var + EPS) * gamma + beta
        logits = jnp.einsum('bsd,de->bse', xn, Wr) + br
        top_vals, top_idx = jax.lax.top_k(logits, K)
        w = jax.nn.softmax(top_vals, axis=-1)
        w_full = jnp.einsum('bsk,bske->bse', w, jax.nn.one_hot(top_idx, E, dtype=w.dtype))
        y = jnp.zeros(x.shape[:-1] + (DOUT,), x.dtype)
        for e in range(E):
            h = jax.nn.gelu(jnp.einsum('bsd,dh->bsh', xn, W1[e]) + b1[e], approximate=False)
            y_e = jnp.einsum('bsh,hd->bsd', h, W2[e]) + b2[e]
            y = y + y_e * w_full[..., e, None]
        return y

    def _L2_gnn_ref(matrix, mask, adj, W):
        import jax, jax.numpy as jnp
        import numpy as np
        HIDDEN = 128
        NEG_INF = -1e+30
        intermediate = jnp.einsum('bsh,hd->bsd', matrix, W)
        similarities = jnp.einsum('bsd,btd->bst', intermediate, matrix)
        similarities = similarities * adj
        key_mask = mask[:, None, :].astype(bool)
        masked = jnp.where(key_mask, similarities, NEG_INF)
        attn = jax.nn.softmax(masked, axis=-1)
        output = jnp.einsum('bst,bth->bsh', attn, matrix)
        return output

    def _L2_ffn_ref(x, W_gat, att_src, att_dst, b_gat, ln_gamma, ln_beta, W1, b1, W2, b2, edge_index):
        import jax, jax.numpy as jnp
        import numpy as np
        B, N, D = (16, 2048, 128)
        NUM_EXPERTS, TOP_K, HEADS = (4, 2, 4)
        N_EDGES = 524288
        LN_EPS = 1e-05

        def _layernorm(x, g, b):
            mu = x.mean(-1, keepdims=True)
            var = ((x - mu) ** 2).mean(-1, keepdims=True)
            return (x - mu) * jax.lax.rsqrt(var + LN_EPS) * g + b

        def _forward(x, edge_index, W_gat, att_src, att_dst, b_gat, ln_gamma, ln_beta, W1, b1, W2, b2):
            Bc, Nc, Dc = x.shape
            M = Bc * Nc
            x_flat = x.reshape(M, Dc)
            h = (x_flat @ W_gat).reshape(M, HEADS, NUM_EXPERTS)
            loops = jnp.arange(M, dtype=edge_index.dtype)
            src = jnp.concatenate([edge_index[0], loops])
            dst = jnp.concatenate([edge_index[1], loops])
            a_src = (h * att_src).sum(-1)
            a_dst = (h * att_dst).sum(-1)
            e = jax.nn.leaky_relu(a_src[src] + a_dst[dst], negative_slope=0.2)
            e_max = jax.ops.segment_max(e, dst, num_segments=M)
            ee = jnp.exp(e - e_max[dst])
            denom = jax.ops.segment_sum(ee, dst, num_segments=M)
            alpha = ee / (denom[dst] + 1e-16)
            msg = h[src] * alpha[:, :, None]
            agg = jax.ops.segment_sum(msg, dst, num_segments=M).reshape(M, HEADS * NUM_EXPERTS) + b_gat
            scores = _layernorm(agg, ln_gamma, ln_beta).reshape(M, HEADS, NUM_EXPERTS).mean(1)
            scores = scores.reshape(Bc, Nc, NUM_EXPERTS)
            topk_s, topk_i = jax.lax.top_k(scores, TOP_K)
            w = jax.nn.softmax(topk_s, axis=-1)
            out = jnp.zeros_like(x)
            for ei in range(NUM_EXPERTS):
                g = jnp.where(topk_i == ei, w, 0.0).sum(-1)
                hh = jax.nn.gelu(x @ W1[ei] + b1[ei], approximate=False)
                out = out + g[..., None] * (hh @ W2[ei] + b2[ei])
            return out
        return _forward(x, edge_index, W_gat, att_src, att_dst, b_gat, ln_gamma, ln_beta, W1, b1, W2, b2)

    def _L3_gnn_ref(feats, adj_mat, fc_w, fc_b, q_w, q_b, k_w, k_b, fp_w, fp_b):
        import jax, jax.numpy as jnp
        import numpy as np
        DIM = 128
        HEADS = 8
        BS = 8
        N = 512
        NEG = -1000000000.0
        bs, n, dim = feats.shape
        feat_proj = (feats @ fc_w + fc_b).reshape(bs, n, HEADS, dim).transpose(0, 2, 1, 3)
        q = feat_proj @ q_w + q_b
        k = feat_proj @ k_w + k_b
        logits = q + jnp.swapaxes(k, -1, -2)
        masked = logits + (1.0 - adj_mat[:, None]) * NEG
        masked = jax.nn.leaky_relu(masked, negative_slope=0.01)
        attn = jax.nn.softmax(masked, axis=-1)
        out = attn @ feat_proj
        out = out.transpose(0, 2, 1, 3).reshape(bs, n, HEADS * dim)
        out = out @ fp_w + fp_b + feats
        return jax.nn.sigmoid(out)

    def _L3_ffn_ref(x, Wg, bg, W1, b1, W2, b2):
        import jax, jax.numpy as jnp
        import numpy as np
        B, S, D, E, H, K = (4, 2048, 128, 8, 256, 2)
        Bv, Sv, Dv = x.shape
        gate_scores = x @ Wg + bg
        _, idx = jax.lax.top_k(gate_scores, K)
        mask = jax.nn.one_hot(idx, E, dtype=x.dtype).sum(axis=-2)
        xf = x.reshape(-1, Dv)
        mf = mask.reshape(-1, E)
        h = jax.nn.gelu(jnp.einsum('td,edh->teh', xf, W1) + b1[None], approximate=False)
        y = jnp.einsum('teh,ehd->ted', h, W2) + b2[None]
        out = jnp.einsum('ted,te->td', y, mf)
        return out.reshape(Bv, Sv, Dv)
    x = x + _L0_gnn_ref(_layernorm(x, axis=-1), adj, L0_gnn_W, L0_gnn_bn_gamma, L0_gnn_bn_beta)
    x = x + _L0_ffn_ref(_layernorm(x, axis=-1), L0_ffn_W_fx, L0_ffn_b_fx, L0_ffn_W_x, L0_ffn_b_x, L0_ffn_W_slice, L0_ffn_b_slice, L0_ffn_temperature, L0_ffn_hy_in_w, L0_ffn_hy_conv_w, L0_ffn_hy_conv_b, L0_ffn_hy_dt_bias, L0_ffn_hy_A_log, L0_ffn_hy_D, L0_ffn_hy_fcD_w, L0_ffn_hy_norm_w, L0_ffn_hy_out_w, L0_ffn_out_w, L0_ffn_out_b)
    x = x + _L1_gnn_ref(_layernorm(x, axis=-1), adj, nodemask, L1_gnn_weight, L1_gnn_bias, L1_gnn_gamma, L1_gnn_beta)
    x = x + _L1_ffn_ref(_layernorm(x, axis=-1), L1_ffn_gamma, L1_ffn_beta, L1_ffn_Wr, L1_ffn_br, L1_ffn_W1, L1_ffn_b1, L1_ffn_W2, L1_ffn_b2)
    x = x + _L2_gnn_ref(_layernorm(x, axis=-1), nodemask, adj, L2_gnn_W)
    x = x + _L2_ffn_ref(_layernorm(x, axis=-1), L2_ffn_W_gat, L2_ffn_att_src, L2_ffn_att_dst, L2_ffn_b_gat, L2_ffn_ln_gamma, L2_ffn_ln_beta, L2_ffn_W1, L2_ffn_b1, L2_ffn_W2, L2_ffn_b2, L2_ffn_edge_index)
    x = x + _L3_gnn_ref(_layernorm(x, axis=-1), adj, L3_gnn_fc_w, L3_gnn_fc_b, L3_gnn_q_w, L3_gnn_q_b, L3_gnn_k_w, L3_gnn_k_b, L3_gnn_fp_w, L3_gnn_fp_b)
    x = x + _L3_ffn_ref(_layernorm(x, axis=-1), L3_ffn_Wg, L3_ffn_bg, L3_ffn_W1, L3_ffn_b1, L3_ffn_W2, L3_ffn_b2)
    return x

_drawn_inputs = setup_inputs


def setup_inputs(seed=0):
    import zlib

    import numpy as np

    out = dict(_drawn_inputs(seed))
    spreads = {'L0_gnn_bn_gamma': (1.0, 0.2),
     'L0_gnn_bn_beta': (0.0, 0.1),
     'L0_ffn_b_fx': (0.0, 0.1),
     'L0_ffn_b_x': (0.0, 0.8),
     'L0_ffn_b_slice': (0.0, 0.8),
     'L0_ffn_temperature': (0.5, 0.6),
     'L0_ffn_hy_conv_b': (0.0, 0.1),
     'L0_ffn_hy_dt_bias': (-4.600166320800781, 0.6),
     'L0_ffn_hy_D': (1.0, 0.6),
     'L0_ffn_hy_norm_w': (1.0, 0.6),
     'L0_ffn_out_b': (0.0, 0.1),
     'L1_gnn_bias': (0.0, 2.0),
     'L1_gnn_gamma': (1.0, 0.2),
     'L1_gnn_beta': (0.0, 0.1),
     'L1_ffn_br': (0.0, 0.371),
     'L2_ffn_b_gat': (0.0, 0.413),
     'L2_ffn_ln_gamma': (1.0, 0.6),
     'L2_ffn_ln_beta': (0.0, 0.8),
     'L2_ffn_b1': (0.0, 0.435),
     'L2_ffn_b2': (0.0, 0.1),
     'L3_gnn_fc_b': (0.0, 0.765),
     'L3_gnn_fp_b': (0.0, 0.8),
     'L3_ffn_bg': (0.0, 0.1),
     'L3_ffn_b1': (0.0, 0.8),
     'L3_ffn_b2': (0.0, 0.1)}
    factors = {'L0_ffn_W_x': 8.0,
     'L0_ffn_W_slice': 8.0,
     'L0_ffn_hy_conv_w': 8.0,
     'L0_ffn_hy_A_log': 55.846,
     'L0_ffn_hy_fcD_w': 8.0,
     'L1_ffn_gamma': 8.0,
     'L1_ffn_beta': 8.0,
     'L1_ffn_Wr': 2.723,
     'L1_ffn_b1': 8.0,
     'L1_ffn_b2': 4.243,
     'L2_ffn_att_src': 22.656,
     'L2_ffn_att_dst': 27.146}
    for name, (base, spread) in spreads.items():
        noise = np.random.default_rng([zlib.crc32(name.encode()), seed]).standard_normal(out[name].shape)
        drawn = base * np.exp(spread * noise) if base else spread * noise
        out[name] = jnp.asarray(drawn.astype(out[name].dtype))
    for name, factor in factors.items():
        out[name] = (out[name] * factor).astype(out[name].dtype)
    return out
```

```python
import numpy as np
import concourse.bass as bass
from concourse import mybir
from contextlib import ExitStack

F32 = mybir.dt.float32
I32 = mybir.dt.int32
ALU = mybir.AluOpType
ACT = mybir.ActivationFunctionType
AX = mybir.AxisListType

B, N, D = 128, 40, 128
T = B * N
SLOT = 64
PAIRS = B // 2
CHG = 8
CH = CHG * N
NCH = B // CHG
CHP = CHG // 2
TT = T // 128


class Buffers:
    pass


def rows(j):
    return slice(SLOT * j, SLOT * j + N)


def load_x(nc, g):
    with nc.cleanup_on_exit(), ExitStack() as ctx:
        xin = ctx.enter_context(nc.sbuf_tensor("xin", [128, TT, D], F32))
        pst = [ctx.enter_context(nc.psum_tensor(f"pst{i}", [128, 512], F32)) for i in range(2)]
        sem = lambda name: nc.alloc_semaphore(name)
        zeroed, ident_ready, xt_ps, xt_out = map(sem, ("zeroed", "ident_ready", "xt_ps", "xt_out"))
        block = ctx.enter_context(nc.Block())
        PARTS = 5
        TP = TT // PARTS
        x_in = [sem(f"x_in{i}") for i in range(PARTS)]

        @block.sync
        def _(sp):
            x = g.x.rearrange("b n d -> (b n) d").rearrange("(t p) d -> p t d", p=128)
            for i in range(PARTS):
                sp.dma_start(xin[:, i * TP:(i + 1) * TP, :], x[:, i * TP:(i + 1) * TP, :]).then_inc(x_in[i], 16)

        @block.gpsimd
        def _(pool):
            pool.memset(g.ident[:], 0.0).then_inc(zeroed, 1)
            pool.memset(g.ones[:], 1.0)
            pool.memset(g.mean_w[:], 1.0 / D)
            pool.wait_ge(zeroed, 1)
            pool.affine_select(out=g.ident[:], in_=g.ident[:], compare_op=ALU.not_equal, fill=1.0, base=0,
                               pattern=[[-1, 128]], channel_multiplier=1).then_inc(ident_ready, 1)

        @block.tensor
        def _(pe):
            pe.wait_ge(ident_ready, 1)
            for c in range(TT // 4):
                if c % 2 == 0:
                    pe.wait_ge(x_in[c // 2], 16)
                if c >= 2:
                    pe.wait_ge(xt_out, c - 1)
                for k in range(4):
                    mm = pe.transpose(pst[c % 2][:, k * 128:(k + 1) * 128], xin[:, 4 * c + k, :], g.ident[:])
                mm.then_inc(xt_ps, 1)

        @block.scalar
        def _(act):
            for c in range(TT // 4):
                act.wait_ge(xt_ps, c + 1)
                act.activation(g.XT[:, c * 512:(c + 1) * 512], pst[c % 2][:], ACT.Copy).then_inc(xt_out, 1)

        @block.vector
        def _(dve):
            dve.memset(g.XNP[:], 0.0)
            dve.memset(g.eps[:], 1e-5)


def load_adjacency(nc, g, name, blocks):
    with nc.cleanup_on_exit(), ExitStack() as ctx:
        blk = ctx.enter_context(nc.sbuf_tensor(f"{name}_blk", [128, N], F32))
        psa = [[ctx.enter_context(nc.psum_tensor(f"{name}_ps{i}{j}", [128, CHP, N], F32)) for j in range(2)] for i in range(2)]
        sem = lambda s: nc.alloc_semaphore(f"{name}_{s}")
        adj_zero, adj_in, blk_ready, at_ps, at_out, steps = map(sem, ("adj_zero", "adj_in", "blk_ready", "at_ps", "at_out", "steps"))
        block = ctx.enter_context(nc.Block())

        @block.sync
        def _(sp):
            sp.wait_ge(adj_zero, 1)
            pairs = g.adj.rearrange("(q j) n m -> j n q m", j=2)
            for j in range(2):
                sp.dma_start(g.adjG[rows(j), :, :], pairs[j]).then_inc(adj_in, 16)

        @block.gpsimd
        def _(pool):
            pool.memset(blk[:], 1.0).then_inc(steps, 1)
            pool.wait_ge(steps, 1)
            if blocks:
                for j in range(2):
                    o = blk[SLOT * j:SLOT * j + SLOT, :].rearrange("p (a c) -> p a c", c=10)
                    pool.affine_select(out=o, in_=o, compare_op=ALU.is_ge, fill=0.0, base=0,
                                       pattern=[[-10, 4], [0, 10]], channel_multiplier=1).then_inc(steps, 1)
                    pool.wait_ge(steps, 2 + 2 * j)
                    pool.affine_select(out=o, in_=o, compare_op=ALU.is_ge, fill=0.0, base=9,
                                       pattern=[[10, 4], [0, 10]], channel_multiplier=-1).then_inc(steps, 1)
                    pool.wait_ge(steps, 3 + 2 * j)
            pool.nop().then_inc(blk_ready, 1)

        @block.tensor
        def _(pe):
            pe.wait_ge(adj_in, 32)
            for c in range(NCH):
                if c >= 2:
                    pe.wait_ge(at_out, c - 1)
                for q in range(CHP):
                    for j in range(2):
                        mm = pe.matmul(psa[c % 2][j][rows(j), q, :], g.adjG[rows(j), c * CHP + q, :],
                                       g.ident[rows(j), rows(j)], start=True, stop=True)
                mm.then_inc(at_ps, 1)

        @block.vector
        def _(dve):
            dve.memset(g.adjG[:], 0.0).then_inc(adj_zero, 1)
            dve.wait_ge(blk_ready, 1)
            for c in range(NCH):
                dve.wait_ge(at_ps, c + 1)
                for j in range(2):
                    o = g.adjT[rows(j), c * CHP:(c + 1) * CHP, :]
                    ps = psa[c % 2][j][rows(j), :, :]
                    if blocks:
                        ins = dve.tensor_tensor(o, ps, blk[rows(j), None, :].broadcast_to([N, CHP, N]), ALU.mult)
                    else:
                        ins = dve.tensor_copy(o, ps)
                ins.then_inc(at_out, 1)


def layer_norm(nc, g, src, slots=False, name="ln"):
    with nc.cleanup_on_exit(), ExitStack() as ctx:
        psm = [ctx.enter_context(nc.psum_tensor(f"{name}_m{i}", [128, CH], F32)) for i in range(2)]
        psv = [ctx.enter_context(nc.psum_tensor(f"{name}_v{i}", [128, CH], F32)) for i in range(2)]
        pst = [ctx.enter_context(nc.psum_tensor(f"{name}_t{i}", [128, CHP, 128], F32)) for i in range(2)]
        sq = ctx.enter_context(nc.sbuf_tensor(f"{name}_sq", [128, 2, CH], F32))
        sd = ctx.enter_context(nc.sbuf_tensor(f"{name}_sd", [128, 2, CH], F32))
        sem = lambda s: nc.alloc_semaphore(f"{name}_{s}")
        mean_ps, centred, squared, var_ps, root, normed, tr_ps, tr_out = map(sem, (
            "mean_ps", "centred", "squared", "var_ps", "root", "normed", "tr_ps", "tr_out"))
        block = ctx.enter_context(nc.Block())
        dst = lambda c: g.XNP[:, c * CHG:(c + 1) * CHG, 0:N]
        if src is g.XNP:
            inp = dst
        else:
            inp = lambda c: src[:, c * CH:(c + 1) * CH].rearrange("p (b n) -> p b n", n=N)
        v3 = lambda t: t.rearrange("p (b n) -> p b n", n=N)

        @block.tensor
        def _(pe):
            def var(c):
                pe.wait_ge(squared, c + 1)
                if c >= 2:
                    pe.wait_ge(root, c - 1)
                pe.matmul(psv[c % 2][:], g.mean_w[:], sq[:, c % 2, :], start=True, stop=True).then_inc(var_ps, 1)

            def turn(c):
                pe.wait_ge(normed, c + 1)
                if c >= 2:
                    pe.wait_ge(tr_out, c - 1)
                for q in range(CHP):
                    p = g.XNP[:, c * CHG + 2 * q:c * CHG + 2 * q + 2, :].rearrange("p b n -> p (b n)")
                    mm = pe.transpose(pst[c % 2][:, q, :], p, g.ident[:])
                mm.then_inc(tr_ps, 1)

            for c in range(NCH + 2):
                if c < NCH:
                    if c >= 2:
                        pe.wait_ge(centred, c - 1)
                    pe.matmul(psm[c % 2][:], g.mean_w[:], inp(c), start=True, stop=True).then_inc(mean_ps, 1)
                if 1 <= c <= NCH:
                    var(c - 1)
                if slots and c >= 2:
                    turn(c - 2)

        def turned(act, c):
            act.wait_ge(tr_ps, c + 1)
            act.activation(g.XNG[:, c * CHP:(c + 1) * CHP, :], pst[c % 2][:], ACT.Copy).then_inc(tr_out, 1)

        @block.scalar
        def _(act):
            for c in range(NCH + 1):
                if c < NCH:
                    act.wait_ge(centred, c + 1)
                    if c >= 2:
                        act.wait_ge(var_ps, c - 1)
                    act.activation(v3(sq[:, c % 2, :]), dst(c), ACT.Square).then_inc(squared, 1)
                if c >= 1:
                    k = c - 1
                    act.wait_ge(var_ps, k + 1)
                    if k >= 2:
                        act.wait_ge(normed, k - 1)
                    act.activation(sd[:, k % 2, :], psv[k % 2][:], ACT.Sqrt, bias=g.eps[:, 0:1]).then_inc(root, 1)
                if slots and c >= 3:
                    turned(act, c - 3)
            if slots:
                for c in range(NCH - 2, NCH):
                    turned(act, c)

        @block.vector
        def _(dve):
            for c in range(NCH + 2):
                if c < NCH:
                    dve.wait_ge(mean_ps, c + 1)
                    dve.tensor_tensor(dst(c), inp(c), v3(psm[c % 2][:]), ALU.subtract).then_inc(centred, 1)
                if c >= 2:
                    k = c - 2
                    dve.wait_ge(root, k + 1)
                    dve.reciprocal(sd[:, k % 2, :], sd[:, k % 2, :])
                    dve.drain()
                    dve.tensor_tensor(dst(k), dst(k), v3(sd[:, k % 2, :]), ALU.mult).then_inc(normed, 1)


def gnn_first(nc, g, name, AT, W, finish):
    with nc.cleanup_on_exit(), ExitStack() as ctx:
        psz = [[ctx.enter_context(nc.psum_tensor(f"{name}_z{i}{j}", [128, CHP, N], F32)) for j in range(2)] for i in range(2)]
        psy = [ctx.enter_context(nc.psum_tensor(f"{name}_y{i}", [128, CH], F32)) for i in range(2)]
        Z = ctx.enter_context(nc.sbuf_tensor(f"{name}_Z", [128, 2, CHP, 2, N], F32))
        Wt = ctx.enter_context(nc.sbuf_tensor(f"{name}_W", [D, D], F32))
        Y = ctx.enter_context(nc.sbuf_tensor(f"{name}_Y", [128, T], F32))
        sem = lambda s: nc.alloc_semaphore(f"{name}_{s}")
        w_in, z_ps, z_out, y_ps, y_out = map(sem, ("w_in", "z_ps", "z_out", "y_ps", "y_out"))
        loads, fin = finish(ctx, Y)
        block = ctx.enter_context(nc.Block())

        @block.sync
        def _(sp):
            sp.dma_start(Wt[:], W).then_inc(w_in, 16)
            loads(sp)

        @block.tensor
        def _(pe):
            def project(c):
                pe.wait_ge(z_out, c + 1)
                if c >= 2:
                    pe.wait_ge(y_out, c - 1)
                pe.matmul(psy[c % 2][:], Wt[:], Z[:, c % 2].rearrange("p q j n -> p (q j n)"),
                          start=True, stop=True).then_inc(y_ps, 1)

            pe.wait_ge(w_in, 16)
            for c in range(NCH + 1):
                if c < NCH:
                    if c >= 2:
                        pe.wait_ge(z_out, c - 1)
                    for q in range(CHP):
                        for j in range(2):
                            mm = pe.matmul(psz[c % 2][j][:, q, :], g.XNG[rows(j), c * CHP + q, :],
                                           AT[rows(j), c * CHP + q, :], start=True, stop=True)
                    mm.then_inc(z_ps, 1)
                if c >= 1:
                    project(c - 1)

        @block.scalar
        def _(act):
            for c in range(NCH):
                act.wait_ge(y_ps, c + 1)
                act.activation(Y[:, c * CH:(c + 1) * CH], psy[c % 2][:], ACT.Copy).then_inc(y_out, 1)
            fin["act"](act)

        @block.vector
        def _(dve):
            for c in range(NCH):
                dve.wait_ge(z_ps, c + 1)
                if c >= 2:
                    dve.wait_ge(y_ps, c - 1)
                dve.tensor_copy(Z[:, c % 2, :, 0, :], psz[c % 2][0][:])
                dve.tensor_copy(Z[:, c % 2, :, 1, :], psz[c % 2][1][:]).then_inc(z_out, 1)
            dve.wait_ge(y_out, NCH)
            fin["dve"](dve)


def l0_gnn(nc, g):
    def finish(ctx, Y):
        sb = lambda s, shape: ctx.enter_context(nc.sbuf_tensor(f"bn_{s}", shape, F32))
        sem = lambda s: nc.alloc_semaphore(f"bn_{s}")
        mean, var, sdv = sb("mean", [128, N]), sb("var", [128, N]), sb("sdv", [128, N])
        S = sb("S", [128, T])
        gam, bet, betas = sb("gam", [128, N]), sb("bet", [128, N]), sb("betas", [N, 4, D])
        gams, bsum = sb("gams", [N, D]), sb("bsum", [N, D])
        pin, vrd, sq, rt = sem("pin"), sem("vrd"), sem("sq"), sem("rt")
        g.bn = (gams, betas, gam, bet)
        nview = Y[:].rearrange("p (b n) -> p n b", n=N)
        sview = S[:].rearrange("p (b n) -> p n b", n=N)
        bc = lambda t: t[:, None, :].broadcast_to([128, B, N])
        y3, s3 = Y[:].rearrange("p (b n) -> p b n", n=N), S[:].rearrange("p (b n) -> p b n", n=N)

        def loads(sp):
            with nc.allow_non_contiguous_dma("small parameters, feature-major"):
                for n0 in range(0, N, 10):
                    i = n0 // 10
                    sp.dma_start(gam[:, n0:n0 + 10], g.L0_gnn_bn_gamma[i, n0 * D:(n0 + 10) * D].rearrange("(n d) -> d n", d=D),
                                 allow_slow_non_contiguous=True).then_inc(pin, 16)
                for i in range(4):
                    sp.dma_start(g.betaT[:, i, :], g.L0_gnn_bn_beta[i, :].rearrange("(n d) -> d n", d=D),
                                 allow_slow_non_contiguous=True).then_inc(pin, 16)

        def dve_part(dve):
            dve.tensor_reduce(mean[:], nview, AX.X, ALU.add)
            dve.drain()
            dve.tensor_scalar(mean[:], mean[:], 1.0 / B, None, ALU.mult)
            dve.drain()
            dve.tensor_tensor(y3, y3, bc(mean), ALU.subtract).then_inc(vrd, 1)
            dve.wait_ge(sq, 1)
            dve.tensor_reduce(var[:], sview, AX.X, ALU.add)
            dve.drain()
            dve.tensor_scalar(var[:], var[:], 1.0 / B, None, ALU.mult).then_inc(vrd, 1)
            dve.wait_ge(pin, 128)
            dve.tensor_tensor(bet[:], g.betaT[:, 0, :], g.betaT[:, 1, :], ALU.add)
            for i in (2, 3):
                dve.drain()
                dve.tensor_tensor(bet[:], bet[:], g.betaT[:, i, :], ALU.add)
            dve.wait_ge(rt, 1)
            dve.reciprocal(sdv[:], sdv[:])
            dve.drain()
            dve.tensor_tensor(sdv[:], sdv[:], gam[:], ALU.mult)
            dve.drain()
            dve.tensor_tensor(y3, y3, bc(sdv), ALU.mult)
            dve.drain()
            dve.tensor_tensor(y3, y3, bc(bet), ALU.add)
            dve.drain()
            dve.tensor_tensor(g.XT[:], g.XT[:], Y[:], ALU.add)

        def act_part(act):
            act.wait_ge(vrd, 1)
            act.activation(S[:], Y[:], ACT.Square).then_inc(sq, 1)
            act.wait_ge(vrd, 2)
            act.activation(sdv[:], var[:], ACT.Sqrt, bias=g.eps[:, 0:1]).then_inc(rt, 1)

        return loads, {"dve": dve_part, "act": act_part}
    gnn_first(nc, g, "g0", g.adjT, g.L0_gnn_W, finish)


def l1_gnn(nc, g):
    def finish(ctx, Y):
        sb = lambda s, shape: ctx.enter_context(nc.sbuf_tensor(f"mn_{s}", shape, F32))
        sem = lambda s: nc.alloc_semaphore(f"mn_{s}")
        S, M, par, st = sb("S", [128, T]), sb("M", [128, T]), sb("par", [128, 3]), sb("st", [128, 4])
        pin, vrd, rt = sem("pin"), sem("vrd"), sem("rt")

        def loads(sp):
            for i, p in enumerate((g.L1_gnn_bias, g.L1_gnn_gamma, g.L1_gnn_beta)):
                sp.dma_start(par[:, i:i + 1], p.rearrange("(d a) -> d a", a=1), allow_slow_non_contiguous=True).then_inc(pin, 16)
            sp.dma_start(M[:], g.nodemask.rearrange("b n -> (b n)")[None, :].broadcast_to([128, T])).then_inc(pin, 16)

        def dve_part(dve):
            dve.wait_ge(pin, 64)
            step = [lambda: dve.tensor_scalar(Y[:], Y[:], par[:, 0:1], None, ALU.add),
                    lambda: dve.tensor_reduce(st[:, 0:1], M[:], AX.X, ALU.add),
                    lambda: dve.tensor_tensor(S[:], Y[:], M[:], ALU.mult),
                    lambda: dve.tensor_reduce(st[:, 1:2], S[:], AX.X, ALU.add),
                    lambda: dve.reciprocal(st[:, 0:1], st[:, 0:1]),
                    lambda: dve.tensor_tensor(st[:, 1:2], st[:, 1:2], st[:, 0:1], ALU.mult),
                    lambda: dve.tensor_scalar(Y[:], Y[:], st[:, 1:2], None, ALU.subtract),
                    lambda: dve.tensor_tensor(S[:], Y[:], Y[:], ALU.mult),
                    lambda: dve.tensor_tensor(S[:], S[:], M[:], ALU.mult),
                    lambda: dve.tensor_reduce(st[:, 2:3], S[:], AX.X, ALU.add)]
            for s in step:
                s()
                dve.drain()
            dve.tensor_tensor(st[:, 2:3], st[:, 2:3], st[:, 0:1], ALU.mult).then_inc(vrd, 1)
            dve.wait_ge(rt, 1)
            dve.reciprocal(st[:, 3:4], st[:, 3:4])
            dve.drain()
            dve.tensor_tensor(st[:, 3:4], st[:, 3:4], par[:, 1:2], ALU.mult)
            dve.drain()
            dve.tensor_scalar(Y[:], Y[:], st[:, 3:4], par[:, 2:3], ALU.mult, ALU.add)
            dve.drain()
            dve.tensor_tensor(Y[:], Y[:], M[:], ALU.mult)
            dve.drain()
            dve.scalar_tensor_tensor(g.XT[:], Y[:], 0.0, g.XT[:], ALU.max, ALU.add)

        def act_part(act):
            act.wait_ge(vrd, 1)
            act.activation(st[:, 3:4], st[:, 2:3], ACT.Sqrt, bias=g.eps[:, 0:1]).then_inc(rt, 1)

        return loads, {"dve": dve_part, "act": act_part}
    gnn_first(nc, g, "g1", g.adjT, g.L1_gnn_weight, finish)


def store_output(nc, g, dst=None):
    with nc.cleanup_on_exit(), ExitStack() as ctx:
        xo = ctx.enter_context(nc.sbuf_tensor("xo", [128, TT, D], F32))
        pst = [ctx.enter_context(nc.psum_tensor(f"pso{i}", [128, 4, 128], F32)) for i in range(2)]
        sem = lambda name: nc.alloc_semaphore(name)
        out_ps, out_sb, stored = sem("out_ps"), sem("out_sb"), sem("stored")
        block = ctx.enter_context(nc.Block())

        @block.tensor
        def _(pe):
            for c in range(TT // 4):
                if c >= 2:
                    pe.wait_ge(out_sb, c - 1)
                for k in range(4):
                    t = 4 * c + k
                    mm = pe.transpose(pst[c % 2][:, k, :], g.XT[:, t * 128:(t + 1) * 128], g.ident[:])
                mm.then_inc(out_ps, 1)

        @block.scalar
        def _(act):
            for c in range(TT // 4):
                act.wait_ge(out_ps, c + 1)
                act.activation(xo[:, 4 * c:4 * c + 4, :], pst[c % 2][:], ACT.Copy).then_inc(out_sb, 1)

        @block.sync
        def _(sp):
            sp.wait_ge(out_sb, TT // 4)
            sp.dma_start((g.out if dst is None else dst).rearrange("b n d -> (b n) d").rearrange("(t p) d -> p t d", p=128), xo[:]).then_inc(stored, 16)
            sp.wait_ge(stored, 16)


def chunk_view(g, c):
    return g.XNP[:, bass.ds(c * CHG, CHG), 0:N]


def chunk_cols(t, c):
    return t[:, bass.ds(c * CH, CH)]


def affine_xn(nc, g, gamma, beta):
    with nc.cleanup_on_exit(), ExitStack() as ctx:
        par = ctx.enter_context(nc.sbuf_tensor("aff_par", [128, 2], F32))
        pin = nc.alloc_semaphore("aff_in")
        block = ctx.enter_context(nc.Block())

        @block.sync
        def _(sp):
            for i, p in enumerate((gamma, beta)):
                sp.dma_start(par[:, i:i + 1], p.rearrange("(d a) -> d a", a=1), allow_slow_non_contiguous=True).then_inc(pin, 16)

        @block.vector
        def _(dve):
            dve.wait_ge(pin, 32)
            x = g.XNP[:, :, 0:N]
            dve.tensor_scalar(x, x, par[:, 0:1], par[:, 1:2], ALU.mult, ALU.add)


def top2(dve, S, R, C, G, E):
    for i in range(E):
        si = lambda n: S[:, :, i:i + 1].broadcast_to([128, TT, n])
        if i:
            dve.tensor_tensor(C[:, :, 0:i], S[:, :, 0:i], si(i), ALU.is_ge)
        if i < E - 1:
            dve.tensor_tensor(C[:, :, i + 1:E], S[:, :, i + 1:E], si(E - 1 - i), ALU.is_gt)
        dve.memset(C[:, :, i:i + 1], 0.0)
        dve.drain()
        dve.tensor_reduce(R[:, :, i:i + 1], C[:], AX.X, ALU.add)
        dve.drain()
    dve.tensor_scalar(G[:], R[:], 1.5, None, ALU.is_lt)
    dve.drain()


def softmax_top2_before(dve, S, st):
    E = S.shape[2]
    dve.tensor_reduce(st[:, :, 0:1], S[:], AX.X, ALU.max)
    dve.drain()
    dve.tensor_tensor(S[:], S[:], st[:, :, 0:1].broadcast_to([128, TT, E]), ALU.subtract)


def softmax_top2_after(dve, S, G, st):
    E = S.shape[2]
    dve.tensor_tensor(G[:], G[:], S[:], ALU.mult)
    dve.drain()
    dve.tensor_reduce(st[:, :, 0:1], G[:], AX.X, ALU.add)
    dve.drain()
    dve.reciprocal(st[:, :, 0:1], st[:, :, 0:1])
    dve.drain()
    dve.tensor_tensor(G[:], G[:], st[:, :, 0:1].broadcast_to([128, TT, E]), ALU.mult)
    dve.drain()


def router(nc, g, name, E, Wr, br, soft):
    with nc.cleanup_on_exit(), ExitStack() as ctx:
        sb = lambda s, shape: ctx.enter_context(nc.sbuf_tensor(f"{name}_{s}", shape, F32))
        sem = lambda s: nc.alloc_semaphore(f"{name}_{s}")
        wr, brt, LT = sb("wr", [D, E]), sb("brt", [E, 1]), sb("LT", [E, T])
        S, R, C, G, st = (sb(s, [128, TT, E]) for s in ("S", "R", "C", "G", "st"))
        psl = [ctx.enter_context(nc.psum_tensor(f"{name}_l{i}", [E, CH], F32)) for i in range(2)]
        pss = ctx.enter_context(nc.psum_tensor(f"{name}_s", [128, TT, E], F32))
        psg = [ctx.enter_context(nc.psum_tensor(f"{name}_g{i}", [E, 512], F32)) for i in range(2)]
        w_in, l_ps, l_out, s_ps, shifted, expd, gated, g_ps, g_out = map(sem, (
            "w_in", "l_ps", "l_out", "s_ps", "shifted", "expd", "gated", "g_ps", "g_out"))
        block = ctx.enter_context(nc.Block())

        @block.sync
        def _(sp):
            sp.dma_start(wr[:], Wr).then_inc(w_in, 16)
            sp.dma_start(brt[:], br.rearrange("(e a) -> e a", a=1), allow_slow_non_contiguous=True).then_inc(w_in, 16)

        @block.tensor
        def _(pe):
            pe.wait_ge(w_in, 32)
            for c in range(NCH):
                if c >= 2:
                    pe.wait_ge(l_out, c - 1)
                pe.matmul(psl[c % 2][:], wr[:], chunk_view(g, c), start=True, stop=True).then_inc(l_ps, 1)
            pe.wait_ge(l_out, NCH)
            for t in range(TT):
                mm = pe.transpose(pss[:, t, :], LT[:, t * 128:(t + 1) * 128], g.ident[0:E, 0:E])
            mm.then_inc(s_ps, 1)
            pe.wait_ge(gated, 1)
            for c in range(TT // 4):
                if c >= 2:
                    pe.wait_ge(g_out, c - 1)
                for k in range(4):
                    mm = pe.transpose(psg[c % 2][:, k * 128:(k + 1) * 128], G[:, 4 * c + k, :], g.ident[:])
                mm.then_inc(g_ps, 1)

        @block.scalar
        def _(act):
            act.wait_ge(w_in, 32)
            for c in range(NCH):
                act.wait_ge(l_ps, c + 1)
                act.activation(LT[:, c * CH:(c + 1) * CH], psl[c % 2][:], ACT.Identity, bias=brt[:, 0:1]).then_inc(l_out, 1)
            if soft:
                act.wait_ge(shifted, 1)
                act.activation(S[:], S[:], ACT.Exp).then_inc(expd, 1)
            for c in range(TT // 4):
                act.wait_ge(g_ps, c + 1)
                act.activation(g.GT[0:E, c * 512:(c + 1) * 512], psg[c % 2][:], ACT.Copy).then_inc(g_out, 1)

        @block.vector
        def _(dve):
            dve.wait_ge(s_ps, 1)
            dve.tensor_copy(S[:], pss[:])
            dve.drain()
            top2(dve, S, R, C, G, E)
            if soft:
                softmax_top2_before(dve, S, st)
                dve.drain()
                dve.nop().then_inc(shifted, 1)
                dve.wait_ge(expd, 1)
                softmax_top2_after(dve, S, G, st)
            dve.nop().then_inc(gated, 1)


def moe(nc, g, name, E, W1, b1, W2, b2):
    H2 = W1.shape[2] // 128
    with nc.cleanup_on_exit(), ExitStack() as ctx:
        sb = lambda s, shape: ctx.enter_context(nc.sbuf_tensor(f"{name}_{s}", shape, F32))
        sem = lambda s: nc.alloc_semaphore(f"{name}_{s}")
        w1, b1t, w2, b2t = sb("w1", [D, E, H2 * 128]), sb("b1t", [128, E * H2]), sb("w2", [128, E * H2, D]), sb("b2t", [E, D])
        b1r = sb("b1r", [E * H2, 128])
        sel = sb("sel", [E, E, 128])
        hs, hg = sb("hs", [128, 2, H2, CH]), sb("hg", [128, 2, H2, CH])
        psg = [ctx.enter_context(nc.psum_tensor(f"{name}_pg{i}", [128, CH], F32)) for i in range(2)]
        psh = [[ctx.enter_context(nc.psum_tensor(f"{name}_ph{i}{k}", [128, CH], F32)) for k in range(H2)] for i in range(2)]
        pso = [ctx.enter_context(nc.psum_tensor(f"{name}_po{i}", [128, CH], F32)) for i in range(2)]
        w_in, b_in, b_ps, b_out, sel0, sel_ready, h_ps, h_out, hg_ready, out_done, o_ps, o_out = map(sem, (
            "w_in", "b_in", "b_ps", "b_out", "sel0", "sel_ready", "h_ps", "h_out", "hg_ready", "out_done", "o_ps", "o_out"))
        block = ctx.enter_context(nc.Block())

        def chunks(eng, chunk):
            chunk(0, 0)
            with eng.Fori(0, (NCH - 2) // 2) as i:
                chunk(2 * i + 1, 1)
                chunk(2 * i + 2, 0)
            chunk(NCH - 1, 1)

        @block.sync
        def _(sp):
            sp.dma_start(b1r[:], b1.rearrange("e (k p) -> (e k) p", p=128)).then_inc(b_in, 16)
            sp.dma_start(w1[:], W1.rearrange("e d h -> d e h")).then_inc(w_in, 16)
            sp.dma_start(w2[:], W2.rearrange("e (k p) d -> p (e k) d", p=128)).then_inc(w_in, 16)
            sp.dma_start(b2t[:], b2).then_inc(w_in, 16)

        @block.gpsimd
        def _(pool):
            pool.memset(sel[:], 0.0).then_inc(sel0, 1)
            pool.wait_ge(sel0, 1)
            pool.affine_select(out=sel[:], in_=sel[:], compare_op=ALU.not_equal, fill=1.0, base=0,
                               pattern=[[-1, E], [0, 128]], channel_multiplier=1).then_inc(sel_ready, 1)

        @block.tensor
        def _(pe):
            pe.wait_ge(b_in, 16)
            pe.transpose(psg[0][:, 0:E * H2], b1r[:], g.ident[0:E * H2, 0:E * H2]).then_inc(b_ps, 1)
            pe.wait_ge(b_out, 1)
            pe.wait_ge(w_in, 48)
            pe.wait_ge(sel_ready, 1)

            def hidden(c, e, s):
                if not (isinstance(c, int) and s < 2):
                    pe.wait_ge(h_out, s - 1)
                    pe.wait_ge(hg_ready, s - 1)
                for k in range(H2):
                    pe.matmul(psh[e % 2][k][:], w1[:, e, k * 128:(k + 1) * 128], chunk_view(g, c), start=True, stop=True)
                mm = pe.matmul(psg[e % 2][:], sel[:, e, :], chunk_cols(g.GT[0:E, :], c), start=True, stop=True)
                mm.then_inc(h_ps, 1)

            def chunk(c, par):
                for e in range(E):
                    s = c * E + e
                    if e < E - 1:
                        hidden(c, e + 1, s + 1)
                    elif not (isinstance(c, int) and c == NCH - 1):
                        hidden(c + 1, 0, s + 1)
                    if e == 0 and not (isinstance(c, int) and c < 2):
                        pe.wait_ge(o_out, c)
                    pe.wait_ge(hg_ready, s + 1)
                    for k in range(H2):
                        mm = pe.matmul(pso[par][:], w2[:, e * H2 + k, :], hg[:, e % 2, k, :], start=(e == 0 and k == 0), stop=False)
                    mm.then_inc(out_done, 1)
                pe.matmul(pso[par][:], b2t[:], chunk_cols(g.GT[0:E, :], c), start=False, stop=True).then_inc(o_ps, 1)

            hidden(0, 0, 0)
            chunks(pe, chunk)

        @block.scalar
        def _(act):
            act.wait_ge(b_ps, 1)
            act.activation(b1t[:], psg[0][:, 0:E * H2], ACT.Copy).then_inc(b_out, 1)
            act.drain()

            def chunk(c, par):
                for e in range(E):
                    s = c * E + e
                    act.wait_ge(h_ps, s + 1)
                    if not (isinstance(c, int) and s < 2):
                        act.wait_ge(hg_ready, s - 1)
                    for k in range(H2):
                        ins = act.activation(hs[:, e % 2, k, :], psh[e % 2][k][:], ACT.Gelu, bias=b1t[:, e * H2 + k:e * H2 + k + 1])
                    ins.then_inc(h_out, 1)
            chunks(act, chunk)

        @block.vector
        def _(dve):
            def add(c, par):
                dve.wait_ge(o_ps, c + 1)
                x = chunk_cols(g.XT, c)
                dve.tensor_tensor(x, x, pso[par][:], ALU.add).then_inc(o_out, 1)

            def chunk(c, par):
                for e in range(E):
                    s = c * E + e
                    dve.wait_ge(h_out, s + 1)
                    if not (isinstance(c, int) and s < 2):
                        dve.wait_ge(out_done, s - 1)
                    for k in range(H2):
                        ins = dve.tensor_tensor(hg[:, e % 2, k, :], hs[:, e % 2, k, :], psg[e % 2][:], ALU.mult)
                    ins.then_inc(hg_ready, 1)
                    if e == 1 and not (isinstance(c, int) and c == 0):
                        add(c - 1, 1 - par)
            dve.sem_inc(o_out, 1)
            chunks(dve, chunk)
            add(NCH - 1, 1)


def l2_gnn(nc, g):
    with nc.cleanup_on_exit(), ExitStack() as ctx:
        sb = lambda s, shape: ctx.enter_context(nc.sbuf_tensor(f"g2_{s}", shape, F32))
        sem = lambda s: nc.alloc_semaphore(f"g2_{s}")
        w, inter = sb("w", [D, D]), sb("inter", [128, 2, CHG, SLOT])
        P, key, hide, st = sb("P", [128, PAIRS, N]), sb("key", [128, PAIRS, N]), sb("hide", [128, PAIRS, N]), sb("st", [128, PAIRS])
        w_in, key_in, i_ps, i_out, s_ps, s_out, shifted, expd = map(sem, (
            "w_in", "key_in", "i_ps", "i_out", "s_ps", "s_out", "shifted", "expd"))
        with ExitStack() as first:
            psi = [first.enter_context(nc.psum_tensor(f"g2_i{i}", [128, CHG, SLOT], F32)) for i in range(2)]
            pss = [first.enter_context(nc.psum_tensor(f"g2_s{i}", [128, CHP, N], F32)) for i in range(2)]
            block = first.enter_context(nc.Block())

            @block.sync
            def _(sp):
                sp.dma_start(w[:], g.L2_gnn_W).then_inc(w_in, 16)
                masks = g.nodemask.rearrange("(q j) m -> j q m", j=2)
                for j in range(2):
                    sp.dma_start(key[SLOT * j:SLOT * (j + 1), :, :], masks[j][None, :, :].broadcast_to([SLOT, PAIRS, N])).then_inc(key_in, 16)

            @block.tensor
            def _(pe):
                def scores(c):
                    pe.wait_ge(i_out, c + 1)
                    if c >= 2:
                        pe.wait_ge(s_out, c - 1)
                    for q in range(CHP):
                        for j in range(2):
                            mm = pe.matmul(pss[c % 2][SLOT * j:SLOT * (j + 1), q, :], inter[:, c % 2, 2 * q + j, :],
                                           g.XNP[:, c * CHG + 2 * q + j, 0:N], start=True, stop=True)
                    mm.then_inc(s_ps, 1)

                pe.wait_ge(w_in, 16)
                for c in range(NCH + 1):
                    if c < NCH:
                        if c >= 2:
                            pe.wait_ge(i_out, c - 1)
                        pe.matmul(psi[c % 2][:].rearrange("p b n -> p (b n)"), w[:],
                                  g.XNP[:, c * CHG:(c + 1) * CHG, :].rearrange("p b n -> p (b n)"), start=True, stop=True).then_inc(i_ps, 1)
                    if c >= 1:
                        scores(c - 1)

            @block.scalar
            def _(act):
                for c in range(NCH):
                    act.wait_ge(i_ps, c + 1)
                    if c >= 2:
                        act.wait_ge(s_ps, c - 1)
                    act.activation(inter[:, c % 2], psi[c % 2][:], ACT.Copy).then_inc(i_out, 1)
                act.wait_ge(shifted, 1)
                act.activation(P[:], P[:], ACT.Exp).then_inc(expd, 1)

            @block.vector
            def _(dve):
                dve.wait_ge(key_in, 32)
                dve.tensor_scalar(key[:], key[:], 0.0, None, ALU.not_equal)
                dve.drain()
                dve.tensor_scalar(hide[:], key[:], 1.0, 1e30, ALU.subtract, ALU.mult)
                for c in range(NCH):
                    dve.wait_ge(s_ps, c + 1)
                    o = slice(c * CHP, (c + 1) * CHP)
                    dve.tensor_tensor(P[:, o, :], pss[c % 2][:], g.adjG[:, o, :], ALU.mult).then_inc(s_out, 1)
                dve.drain()
                dve.tensor_tensor(P[:], P[:], key[:], ALU.mult)
                dve.drain()
                dve.tensor_tensor(P[:], P[:], hide[:], ALU.add)
                dve.drain()
                dve.tensor_reduce(st[:], P[:], AX.X, ALU.max)
                dve.drain()
                dve.tensor_tensor(P[:], P[:], st[:, :, None].broadcast_to([128, PAIRS, N]), ALU.subtract).then_inc(shifted, 1)
                dve.wait_ge(expd, 1)
                dve.tensor_reduce(st[:], P[:], AX.X, ALU.add)
                dve.drain()
                dve.reciprocal(st[:], st[:])
                dve.drain()
                dve.tensor_tensor(P[:], P[:], st[:, :, None].broadcast_to([128, PAIRS, N]), ALU.mult)

        PT = sb("PT", [128, 2, CHP, N])
        pst = [[ctx.enter_context(nc.psum_tensor(f"g2_t{i}{j}", [128, CHP, N], F32)) for j in range(2)] for i in range(2)]
        psz = [[ctx.enter_context(nc.psum_tensor(f"g2_z{i}{j}", [128, CHP, N], F32)) for j in range(2)] for i in range(2)]
        t_ps, t_out, z_ps, z_out = map(sem, ("t_ps", "t_out", "z_ps", "z_out"))
        block = ctx.enter_context(nc.Block())

        @block.tensor
        def _(pe):
            for c in range(NCH + 1):
                if c < NCH:
                    if c >= 2:
                        pe.wait_ge(t_out, c - 1)
                    for q in range(CHP):
                        for j in range(2):
                            mm = pe.matmul(pst[c % 2][j][rows(j), q, :], P[rows(j), c * CHP + q, :], g.ident[rows(j), rows(j)],
                                           start=True, stop=True)
                    mm.then_inc(t_ps, 1)
                if c >= 1:
                    k = c - 1
                    pe.wait_ge(t_out, k + 1)
                    if k >= 2:
                        pe.wait_ge(z_out, k - 1)
                    for q in range(CHP):
                        for j in range(2):
                            mm = pe.matmul(psz[k % 2][j][:, q, :], g.XNG[rows(j), k * CHP + q, :], PT[rows(j), k % 2, q, :],
                                           start=True, stop=True)
                    mm.then_inc(z_ps, 1)

        @block.scalar
        def _(act):
            for c in range(NCH):
                act.wait_ge(t_ps, c + 1)
                if c >= 2:
                    act.wait_ge(z_ps, c - 1)
                for j in range(2):
                    ins = act.activation(PT[rows(j), c % 2], pst[c % 2][j][rows(j)], ACT.Copy)
                ins.then_inc(t_out, 1)

        @block.vector
        def _(dve):
            for c in range(NCH):
                dve.wait_ge(z_ps, c + 1)
                x = g.XT[:, c * CH:(c + 1) * CH].rearrange("p (q j n) -> p q j n", j=2, n=N)
                for j in range(2):
                    ins = dve.tensor_tensor(x[:, :, j, :], x[:, :, j, :], psz[c % 2][j][:], ALU.add)
                ins.then_inc(z_out, 1)


def l3_gnn(nc, g):
    HD = 8
    NEG = -1000000000.0
    with nc.cleanup_on_exit(), ExitStack() as ctx:
        sb = lambda s, shape: ctx.enter_context(nc.sbuf_tensor(f"g3_{s}", shape, F32))
        sem = lambda s: nc.alloc_semaphore(f"g3_{s}")
        wc, wq, wk = sb("wc", [D, HD, D]), sb("wq", [D, HD]), sb("wk", [D, HD, SLOT])
        obias, Q, neg = sb("obias", [D, 1]), sb("Q", [128, PAIRS, HD]), sb("neg", [128, PAIRS, N])
        with ExitStack() as first:
            fsb = lambda s, shape: first.enter_context(nc.sbuf_tensor(f"g3_{s}", shape, F32))
            fc, fcT, fp = fsb("fc", [D, HD, D]), fsb("fcT", [D, HD, D]), fsb("fp", [D, HD, D])
            qk, krep, qkrep, fcb, fcbT = fsb("qk", [D, 2]), fsb("krep", [D, SLOT]), fsb("qkrep", [D, 128]), fsb("fcb", [HD, D]), fsb("fcbT", [D, HD])
            qkb, fpb, cst = fsb("qkb", [128, 2]), fsb("fpb", [D, 1]), fsb("cst", [128, HD])
            ps = [first.enter_context(nc.psum_tensor(f"g3_p{i}", [128, 4, 128], F32)) for i in range(2)]
            pq = first.enter_context(nc.psum_tensor("g3_pq", [128, HD], F32))
            pk = first.enter_context(nc.psum_tensor("g3_pk", [128, HD, SLOT], F32))
            pb = first.enter_context(nc.psum_tensor("g3_pb", [128, HD], F32))
            po = first.enter_context(nc.psum_tensor("g3_po", [128, 1], F32))
            pQ = first.enter_context(nc.psum_tensor("g3_pQ", [128, PAIRS, HD], F32))
            w_in, rep, t_ps, t_out, c_ps, s_ps, folded, q_ps = map(sem, ("w_in", "rep", "t_ps", "t_out", "c_ps", "s_ps", "folded", "q_ps"))
            block = first.enter_context(nc.Block())
            LOADS = 16 * 8

            @block.sync
            def _(sp):
                col = lambda t: t.rearrange("(d a) -> d a", a=1)
                sp.dma_start(fc[:], g.L3_gnn_fc_w.rearrange("f (h d) -> f h d", h=HD)).then_inc(w_in, 16)
                sp.dma_start(fp[:], g.L3_gnn_fp_w.rearrange("(h d) o -> d h o", h=HD)).then_inc(w_in, 16)
                sp.dma_start(fcb[:], g.L3_gnn_fc_b.rearrange("(h d) -> h d", h=HD)).then_inc(w_in, 16)
                sp.dma_start(qk[:, 0:1], g.L3_gnn_q_w, allow_slow_non_contiguous=True).then_inc(w_in, 16)
                sp.dma_start(qk[:, 1:2], g.L3_gnn_k_w, allow_slow_non_contiguous=True).then_inc(w_in, 16)
                sp.dma_start(qkb[:, 0:1], g.L3_gnn_q_b[None, :].broadcast_to([128, 1]), allow_slow_non_contiguous=True).then_inc(w_in, 16)
                sp.dma_start(qkb[:, 1:2], g.L3_gnn_k_b[None, :].broadcast_to([128, 1]), allow_slow_non_contiguous=True).then_inc(w_in, 16)
                sp.dma_start(fpb[:], col(g.L3_gnn_fp_b), allow_slow_non_contiguous=True).then_inc(w_in, 16)

            @block.vector
            def _(dve):
                dve.wait_ge(w_in, LOADS)
                dve.tensor_scalar(krep[:], g.ones[:, 0:SLOT], qk[:, 1:2], None, ALU.mult)
                dve.tensor_scalar(qkrep[:], g.ones[:], qk[:, 0:1], qk[:, 1:2], ALU.mult, ALU.add).then_inc(rep, 1)
                dve.tensor_scalar(neg[:], g.adjG[:], -1.0, 1.0, ALU.mult, ALU.add)
                dve.drain()
                dve.tensor_scalar(neg[:], neg[:], NEG, None, ALU.mult)
                for i in range(2):
                    dve.wait_ge(t_ps, i + 1)
                    dve.tensor_copy(fcT[:, 4 * i:4 * i + 4, :], ps[i][:]).then_inc(t_out, 1)
                dve.wait_ge(t_ps, 3)
                dve.tensor_copy(fcbT[:], pb[:]).then_inc(t_out, 1)
                for i in range(2):
                    dve.wait_ge(c_ps, i + 1)
                    dve.tensor_copy(wc[:, 4 * i:4 * i + 4, :], ps[i][:])
                dve.wait_ge(s_ps, 1)
                dve.tensor_copy(wq[:], pq[:])
                dve.tensor_copy(wk[:], pk[:])
                dve.tensor_scalar(cst[:], pb[:], qkb[:, 0:1], qkb[:, 1:2], ALU.add, ALU.add)
                dve.tensor_scalar(obias[:], po[:], fpb[:, 0:1], None, ALU.add).then_inc(folded, 1)
                dve.wait_ge(q_ps, 1)
                dve.drain()
                dve.tensor_tensor(Q[:], pQ[:], cst[:, None, :].broadcast_to([128, PAIRS, HD]), ALU.add)

            @block.tensor
            def _(pe):
                pe.wait_ge(w_in, LOADS)
                for i in range(2):
                    for k in range(4):
                        mm = pe.transpose(ps[i][:, k, :], fc[:, 4 * i + k, :], g.ident[:])
                    mm.then_inc(t_ps, 1)
                pe.transpose(pb[:], fcb[:], g.ident[0:HD, 0:HD]).then_inc(t_ps, 1)
                pe.wait_ge(rep, 1)
                for i in range(2):
                    pe.wait_ge(t_out, i + 1)
                    for k in range(4):
                        mm = pe.matmul(ps[i][:, k, :], fcT[:, 4 * i + k, :], fp[:, 4 * i + k, :], start=True, stop=True)
                    mm.then_inc(c_ps, 1)
                for h in range(HD):
                    pe.matmul(pq[:, h:h + 1], fcT[:, h, :], qk[:, 0:1], start=True, stop=True)
                    pe.matmul(pk[:, h, :], fcT[:, h, :], krep[:], start=True, stop=True)
                pe.wait_ge(t_out, 3)
                pe.matmul(pb[:], qkrep[:], fcbT[:], start=True, stop=True)
                for h in range(HD):
                    mm = pe.matmul(po[:], fp[:, h, :], fcbT[:, h:h + 1], start=(h == 0), stop=(h == HD - 1))
                mm.then_inc(s_ps, 1)
                pe.wait_ge(folded, 1)
                for q in range(PAIRS):
                    mm = pe.matmul(pQ[:, q, :], g.XNP[:, 2 * q:2 * q + 2, :].rearrange("p b n -> p (b n)"), wq[:], start=True, stop=True)
                mm.then_inc(q_ps, 1)

        P, st = sb("P", [128, 2, HD, CHP, N]), sb("st", [128, HD, CHP])
        PT, Z, so = sb("PT", [128, 2, HD, N]), sb("Z", [128, 2, HD, CHG, N]), sb("so", [128, 2, CH])
        GR = [range(0, 3), range(3, 6), range(6, 8)]
        psk = [ctx.enter_context(nc.psum_tensor(f"g3_k{i}", [128, 3, CHP, N], F32)) for i in range(3)]
        pst = [ctx.enter_context(nc.psum_tensor(f"g3_t{j}", [128, HD, N], F32)) for j in range(2)]
        psz = [ctx.enter_context(nc.psum_tensor(f"g3_z{j}", [128, HD, N], F32)) for j in range(2)]
        psy = ctx.enter_context(nc.psum_tensor("g3_y", [128, CH], F32))
        k_ps, k_out, shifted, expd, attn, pt_ps, pt_out, z_ps, z_out, y_ps, y_pre, y_sig = map(sem, (
            "k_ps", "k_out", "shifted", "expd", "attn", "pt_ps", "pt_out", "z_ps", "z_out", "y_ps", "y_pre", "y_sig"))
        block = ctx.enter_context(nc.Block())

        @block.tensor
        def _(pe):
            def keys(c):
                if c >= 1:
                    pe.wait_ge(k_out, c)
                for i, hs in enumerate(GR):
                    for h in hs:
                        for j in range(2):
                            rhs = g.XNP[:, c * CHG + j:c * CHG + CHG:2, 0:N]
                            mm = pe.matmul(psk[i][SLOT * j:SLOT * (j + 1), h - hs[0], :, :], wk[:, h, :], rhs, start=True, stop=True)
                mm.then_inc(k_ps, 1)

            def product(n):
                pe.wait_ge(pt_out, n + 1)
                if n >= 1:
                    pe.wait_ge(z_out, n)
                for j in range(2):
                    mm = pe.matmul(psz[j][:].rearrange("p h n -> p (h n)"), g.XNG[rows(j), n, :],
                                   PT[rows(j), n % 2].rearrange("p h n -> p (h n)"), start=True, stop=True)
                mm.then_inc(z_ps, 1)

            def project(c):
                pe.wait_ge(z_out, CHP * (c + 1))
                if c >= 1:
                    pe.wait_ge(y_pre, c)
                for h in range(HD):
                    mm = pe.matmul(psy[:], wc[:, h, :], Z[:, c % 2, h].rearrange("p b n -> p (b n)"), start=(h == 0), stop=(h == HD - 1))
                mm.then_inc(y_ps, 1)

            keys(0)
            for c in range(NCH):
                if c < NCH - 1:
                    keys(c + 1)
                pe.wait_ge(attn, c + 1)
                for q in range(CHP):
                    n = c * CHP + q
                    if n >= 1:
                        pe.wait_ge(pt_out, n)
                    for j in range(2):
                        for h in range(HD):
                            mm = pe.matmul(pst[j][rows(j), h, :], P[rows(j), c % 2, h, q, :], g.ident[rows(j), rows(j)], start=True, stop=True)
                    mm.then_inc(pt_ps, 1)
                    if n >= 1:
                        product(n - 1)
                    if q == 1 and c >= 1:
                        project(c - 1)
            product(PAIRS - 1)
            project(NCH - 1)

        @block.scalar
        def _(act):
            def z_evac(n):
                act.wait_ge(z_ps, n + 1)
                c, q = n // CHP, n % CHP
                if q == 0 and c >= 2:
                    act.wait_ge(y_ps, c - 1)
                for j in range(2):
                    ins = act.activation(Z[:, c % 2, :, 2 * q + j, :], psz[j][:], ACT.Copy)
                ins.then_inc(z_out, 1)

            def sig(c):
                act.wait_ge(y_pre, c + 1)
                act.activation(so[:, c % 2, :], so[:, c % 2, :], ACT.Exp, scale=-1.0).then_inc(y_sig, 1)

            def exps(c):
                act.wait_ge(shifted, c + 1)
                act.activation(P[:, c % 2], P[:, c % 2], ACT.Exp).then_inc(expd, 1)

            exps(0)
            for c in range(NCH):
                if c < NCH - 1:
                    exps(c + 1)
                for q in range(CHP):
                    n = c * CHP + q
                    act.wait_ge(pt_ps, n + 1)
                    if n >= 2:
                        act.wait_ge(z_ps, n - 1)
                    for j in range(2):
                        ins = act.activation(PT[rows(j), n % 2], pst[j][rows(j)], ACT.Copy)
                    ins.then_inc(pt_out, 1)
                    if n >= 1:
                        z_evac(n - 1)
                    if q == 3 and c >= 1:
                        sig(c - 1)
            z_evac(PAIRS - 1)
            sig(NCH - 1)

        @block.vector
        def _(dve):
            def softmax(c):
                p = P[:, c % 2]
                o = slice(c * CHP, (c + 1) * CHP)
                dve.wait_ge(k_ps, c + 1)
                if c >= 2:
                    dve.wait_ge(pt_ps, CHP * (c - 1))
                for i, hs in enumerate(GR):
                    for h in hs:
                        ins = dve.tensor_tensor(p[:, h], psk[i][:, h - hs[0]], Q[:, o, h:h + 1].broadcast_to([128, CHP, N]), ALU.add)
                ins.then_inc(k_out, 1)
                dve.drain()
                m = neg[:, o, :].rearrange("p q m -> p (q m)")[:, None, :].broadcast_to([128, HD, CHP * N])
                p2 = p.rearrange("p h q m -> p h (q m)")
                dve.tensor_tensor(p2, p2, m, ALU.add)
                dve.drain()
                p1 = p.rearrange("p h q m -> p (h q m)")
                dve.scalar_tensor_tensor(p1, p1, 0.01, p1, ALU.mult, ALU.max)
                dve.drain()
                dve.tensor_reduce(st[:], p, AX.X, ALU.max)
                dve.drain()
                ph = p.rearrange("p h q m -> p (h q) m")
                sb_ = st[:].rearrange("p h q -> p (h q)")[:, :, None].broadcast_to([128, HD * CHP, N])
                dve.tensor_tensor(ph, ph, sb_, ALU.subtract).then_inc(shifted, 1)
                dve.wait_ge(expd, c + 1)
                dve.tensor_reduce(st[:], p, AX.X, ALU.add)
                dve.drain()
                dve.reciprocal(st[:], st[:])
                dve.drain()
                dve.tensor_tensor(ph, ph, sb_, ALU.mult).then_inc(attn, 1)

            def pre(c):
                dve.wait_ge(y_ps, c + 1)
                s3 = so[:, c % 2, :].rearrange("p (b n) -> p b n", n=N)
                dve.scalar_tensor_tensor(s3, psy[:].rearrange("p (b n) -> p b n", n=N), obias[:, 0:1],
                                         chunk_view(g, c), ALU.add, ALU.add).then_inc(y_pre, 1)

            def post(c):
                dve.wait_ge(y_sig, c + 1)
                s = so[:, c % 2, :]
                dve.tensor_scalar(s, s, 1.0, None, ALU.add)
                dve.drain()
                dve.reciprocal(s, s)
                dve.drain()
                x = g.XT[:, c * CH:(c + 1) * CH]
                dve.tensor_tensor(x, x, s, ALU.add)
                dve.drain()

            softmax(0)
            for c in range(NCH):
                if c < NCH - 1:
                    softmax(c + 1)
                if c >= 1:
                    pre(c - 1)
                    if c >= 2:
                        post(c - 2)
            pre(NCH - 1)
            post(NCH - 2)
            post(NCH - 1)


HEADS, EXP = 4, 4
HE = HEADS * EXP
V = HEADS + HE
EDGES = 524288
EC = EDGES // 128
BF16 = mybir.dt.bfloat16
VALID = 1 << 30
GRP = 8


def edge_keys(nc, g):
    with nc.cleanup_on_exit(), ExitStack() as ctx:
        sb = lambda s, shape, dt=F32: ctx.enter_context(nc.sbuf_tensor(f"ek_{s}", shape, dt))
        sem = lambda s: nc.alloc_semaphore(f"ek_{s}")
        lent = g.XNG[:].rearrange("p q d -> p (q d)").bitcast(I32)
        src, dst = lent[:, 0:EC], lent[:, EC:2 * EC]
        lent = g.XNP[:].rearrange("p b n -> p (b n)")
        keep, past = lent[:, 0:EC], lent[:, EC:2 * EC]
        mask = sb("mask", [128, EC], I32)
        dl, dh = sb("dl", [128, EC], BF16), sb("dh", [128, EC], BF16)
        iob = sb("iob", [128, 128], BF16)
        HG = 16
        OL, OH = sb("OL", [128, 2, HG, 128], BF16), sb("OH", [128, 2, HG, TT], BF16)
        zero = sb("zero", [128, 128], BF16)
        cnt, top = sb("cnt", [128, 1]), sb("top", [1, 1])
        pc = ctx.enter_context(nc.psum_tensor("ek_pc", [1, 128], F32))
        ph = ctx.enter_context(nc.psum_tensor("ek_ph", [128, TT], F32))
        e_in, counted, c_ps, hot, used, h_ps, io, zeroed = map(sem, ("e_in", "counted", "c_ps", "hot", "used", "h_ps", "io", "zeroed"))
        block = ctx.enter_context(nc.Block())

        @block.sync
        def _(sp):
            sp.dma_start(src, g.L2_ffn_edge_index[0].rearrange("(p c) -> p c", p=128)).then_inc(e_in, 16)
            sp.dma_start(dst, g.L2_ffn_edge_index[1].rearrange("(p c) -> p c", p=128)).then_inc(e_in, 16)

        @block.gpsimd
        def _(pool):
            pool.iota(iob[:], pattern=[[1, 128]], base=0, channel_multiplier=0, allow_small_or_imprecise_dtypes=True).then_inc(io, 1)
            pool.iota(g.iof[:], pattern=[[1, 128]], base=0, channel_multiplier=0, allow_small_or_imprecise_dtypes=True)
            pool.memset(zero[:], 0.0).then_inc(zeroed, 1)

        @block.vector
        def _(dve):
            dve.wait_ge(e_in, 32)
            w = g.work[:].bitcast(I32)
            dve.tensor_scalar(w, dst, 13, VALID, ALU.logical_shift_left, ALU.bitwise_or)
            dve.tensor_scalar(past, src, float(T - 1), None, ALU.is_ge)
            dve.tensor_scalar(keep, dst, float(T), None, ALU.is_lt)
            dve.drain()
            dve.tensor_tensor(w, w, src, ALU.bitwise_or)
            dve.tensor_tensor(past, past, keep, ALU.mult)
            dve.drain()
            dve.tensor_tensor(keep, keep, past, ALU.subtract)
            dve.drain()
            dve.tensor_copy(mask[:], keep)
            dve.tensor_reduce(cnt[:], keep, AX.X, ALU.add).then_inc(counted, 1)
            dve.drain()
            dve.tensor_scalar(mask[:], mask[:], 31, 31, ALU.logical_shift_left, ALU.arith_shift_right)
            dve.drain()
            dve.tensor_tensor(w, w, mask[:], ALU.bitwise_and)
            dve.drain()
            dve.tensor_scalar(mask[:], dst, 7, 255, ALU.logical_shift_right, ALU.bitwise_and) 
            dve.tensor_scalar(src, dst, 127, None, ALU.bitwise_and)
            dve.drain()
            dve.tensor_copy(dl[:], src)
            dve.scalar_tensor_tensor(keep, mask[:], 255.0, past, ALU.subtract, ALU.mult)
            dve.drain()
            dve.tensor_scalar(dh[:], keep, 255.0, None, ALU.add)
            dve.wait_ge(c_ps, 1)
            dve.tensor_reduce(top[:], pc[:], AX.X, ALU.max)
            dve.drain()
            dve.tensor_scalar(g.turns[:], top[:], float(GRP - 1), None, ALU.add)
            dve.drain()
            dve.tensor_scalar(g.turns[:], g.turns[:], 3, None, ALU.logical_shift_right)
            dve.wait_ge(io, 1)
            dve.drain()
            dve.nop().then_inc(used, 1)

            def one_hots(c, b):
                cols = bass.ds(c * HG, HG)
                i3 = lambda n: iob[:, None, 0:n].broadcast_to([128, HG, n])
                dve.tensor_tensor(OL[:, b], i3(128), dl[:, cols, None].broadcast_to([128, HG, 128]), ALU.is_equal)
                dve.tensor_tensor(OH[:, b], i3(TT), dh[:, cols, None].broadcast_to([128, HG, TT]), ALU.is_equal).then_inc(hot, 1)

            with dve.Fori(0, EC // HG // 2) as i:
                for b in range(2):
                    dve.wait_ge(h_ps, 2 * i + b + 1)
                    one_hots(2 * i + b, b)
            dve.wait_ge(h_ps, EC // HG + 3)
            dve.tensor_copy(g.cntB[:], ph[:])
            dve.memset(g.XNP[:], 0.0)

        @block.tensor
        def _(pe):
            pe.wait_ge(counted, 1)
            pe.transpose(pc[:], cnt[:], g.ident[:]).then_inc(c_ps, 1)
            pe.wait_ge(zeroed, 1)
            pe.wait_ge(used, 1)
            pe.matmul(ph[:], zero[:], zero[:, 0:TT], start=True, stop=False, skip_group_check=True).then_inc(h_ps, 2)

            def products(c, b):
                pe.wait_ge(hot, c + 1)
                for k in range(HG):
                    mm = pe.matmul(ph[:], OL[:, b, k, :], OH[:, b, k, :], start=False, stop=False, skip_group_check=True)
                mm.then_inc(h_ps, 1)

            with pe.Fori(0, EC // HG // 2) as i:
                for b in range(2):
                    products(2 * i + b, b)
            pe.matmul(ph[:], zero[:], zero[:, 0:TT], start=False, stop=True, skip_group_check=True).then_inc(h_ps, 1)


def leaky(dve, t, slope):
    dve.scalar_tensor_tensor(t, t, slope, t, ALU.mult, ALU.max)
    dve.drain()


def edge_router(nc, g):
    with nc.cleanup_on_exit(), ExitStack() as ctx:
        sb = lambda s, shape, dt=F32: ctx.enter_context(nc.sbuf_tensor(f"er_{s}", shape, dt))
        sem = lambda s: nc.alloc_semaphore(f"er_{s}")
        TS, TD, TM = sb("TS", [128, V, TT]), sb("TD", [128, HEADS, TT]), sb("TM", [128, HEADS, TT])
        amax = sb("amax", [128, HEADS])
        last = sb("last", [128, V])
        with ExitStack() as first:
            fsb = lambda s, shape: first.enter_context(nc.sbuf_tensor(f"er_{s}", shape, F32))
            wg, HT = fsb("wg", [D, HE]), fsb("HT", [HE, T])
            H, pr, att = fsb("H", [128, TT, HE]), fsb("pr", [128, TT, HE]), fsb("att", [128, 2, HE])
            mx, m4, dg, sel = fsb("mx", [128, HEADS]), fsb("m4", [HEADS, 1]), fsb("dg", [HEADS, HEADS]), fsb("sel", [128, 128])
            psl = [first.enter_context(nc.psum_tensor(f"er_l{i}", [HE, CH], F32)) for i in range(2)]
            psh = [first.enter_context(nc.psum_tensor(f"er_h{i}", [128, TT // 2, HE], F32)) for i in range(2)]
            psm = first.enter_context(nc.psum_tensor("er_m", [HEADS, 128], F32))
            psa = first.enter_context(nc.psum_tensor("er_a", [128, HEADS], F32))
            psv = first.enter_context(nc.psum_tensor("er_v", [128, V], F32))
            w_in, l_ps, l_out, h_ps, mxd, m_ps, dgd, a_ps, selr = map(sem, ("w_in", "l_ps", "l_out", "h_ps", "mxd", "m_ps", "dgd", "a_ps", "selr"))
            block = first.enter_context(nc.Block())

            @block.sync
            def _(sp):
                sp.dma_start(wg[:], g.L2_ffn_W_gat).then_inc(w_in, 16)
                for i, a in enumerate((g.L2_ffn_att_src, g.L2_ffn_att_dst)):
                    sp.dma_start(att[:, i, :], a.rearrange("h e -> (h e)")[None, :].broadcast_to([128, HE])).then_inc(w_in, 16)

            @block.gpsimd
            def _(pool):
                pool.affine_select(out=sel[:], in_=g.ones[:], compare_op=ALU.is_ge, fill=0.0, base=-127,
                                   pattern=[[0, 128]], channel_multiplier=1).then_inc(selr, 1)

            @block.tensor
            def _(pe):
                pe.wait_ge(w_in, 48)
                for c in range(NCH):
                    if c >= 2:
                        pe.wait_ge(l_out, c - 1)
                    pe.matmul(psl[c % 2][:], wg[:], chunk_view(g, c), start=True, stop=True).then_inc(l_ps, 1)
                pe.wait_ge(l_out, NCH)
                for t in range(TT):
                    mm = pe.transpose(psh[t // 20][:, t % 20, :], HT[:, t * 128:(t + 1) * 128], g.ident[0:HE, 0:HE])
                mm.then_inc(h_ps, 1)
                pe.wait_ge(mxd, 1)
                pe.transpose(psm[:], mx[:], g.ident[:]).then_inc(m_ps, 1)
                pe.wait_ge(dgd, 1)
                pe.wait_ge(selr, 1)
                pe.matmul(psv[:], sel[:], TS[:, :, TT - 1], start=True, stop=True)
                pe.matmul(psa[:], g.ones[0:HEADS, :], dg[:], start=True, stop=True).then_inc(a_ps, 1)

            @block.scalar
            def _(act):
                for c in range(NCH):
                    act.wait_ge(l_ps, c + 1)
                    act.activation(HT[:, c * CH:(c + 1) * CH], psl[c % 2][:], ACT.Copy).then_inc(l_out, 1)

            @block.vector
            def _(dve):
                dve.wait_ge(h_ps, 1)
                for i in range(2):
                    dve.tensor_copy(H[:, i * 20:(i + 1) * 20, :], psh[i][:])
                dve.drain()
                dve.tensor_copy(TS[:, HEADS:V, :].rearrange("p v t -> p t v"), H[:])
                for i, o in enumerate((TS[:, 0:HEADS, :], TD[:])):
                    dve.tensor_tensor(pr[:], H[:], att[:, i, None, :].broadcast_to([128, TT, HE]), ALU.mult)
                    dve.drain()
                    dve.tensor_reduce(o.rearrange("p h t -> p t h"), pr[:].rearrange("p t (h e) -> p t h e", h=HEADS), AX.X, ALU.add)
                    dve.drain()
                dve.tensor_reduce(mx[:], TS[:, 0:HEADS, :], AX.X, ALU.max).then_inc(mxd, 1)
                dve.wait_ge(m_ps, 1)
                dve.tensor_reduce(m4[:], psm[:], AX.X, ALU.max)
                dve.drain()
                dve.tensor_scalar(dg[:], g.ident[0:HEADS, 0:HEADS], m4[:, 0:1], None, ALU.mult).then_inc(dgd, 1)
                dve.wait_ge(a_ps, 1)
                dve.tensor_copy(amax[:], psa[:])
                dve.tensor_copy(last[:], psv[:])
                dve.drain()
                dve.tensor_tensor(TM[:], TD[:], amax[:, :, None].broadcast_to([128, HEADS, TT]), ALU.add)
                dve.drain()
                leaky(dve, TM[:], 0.2)

        k8, ki = sb("k8", [128, GRP]), sb("ki", [128, 4, GRP], I32)
        idx = sb("idx", [128, 4, GRP])
        OS, OD = sb("OS", [128, 2, 128]), sb("OD", [128, GRP, 128])
        SH, DH = sb("SH", [128, GRP, TT]), sb("DH", [128, GRP, TT])
        OT = sb("OT", [128, 2, 2, 128])
        G1, G2 = sb("G1", [128, V, TT]), sb("G2", [128, HEADS, TT])
        VS, VD, VM = sb("VS", [128, GRP, V]), sb("VD", [128, GRP, HEADS]), sb("VM", [128, GRP, HEADS])
        VW = sb("VW", [128, GRP, V])
        X = sb("X", [128, 2, V, TT])
        zero = sb("zero", [128, 128])
        A = sb("A", [128, V, TT])
        VH = V // 2
        pst = [ctx.enter_context(nc.psum_tensor(f"er_t{i}", [128, 2, 128], F32)) for i in range(2)]
        psg = [ctx.enter_context(nc.psum_tensor(f"er_g{i}", [128, VH, TT], F32)) for i in range(2)]
        psd = ctx.enter_context(nc.psum_tensor("er_d", [128, HEADS, TT], F32))
        acc = [ctx.enter_context(nc.psum_tensor(f"er_c{i}", [128, VH, TT], F32)) for i in range(2)]
        hot, t_ps, t_out, g_ps, g_use, scored, expd, x_ready, x_used, closed = map(sem, (
            "hot", "t_ps", "t_out", "g_ps", "g_use", "scored", "expd", "x_ready", "x_used", "closed"))

        def loop(eng):
            n = eng.value_load(g.turns[0:1, 0:1], min_val=0, max_val=EC // GRP)
            return eng.Fori(0, n)

        with nc.Block() as block:
            @block.vector
            def _(dve):
                dve.memset(zero[:], 0.0).then_inc(closed, 1)
                with loop(dve) as r:
                    dve.max(k8[:], g.work[:])
                    dve.drain()
                    dve.match_replace(g.work[:], k8[:], g.work[:], 0.0)
                    kb = k8[:].bitcast(I32)
                    dve.tensor_scalar(ki[:, 0], kb, 127, None, ALU.bitwise_and)
                    dve.tensor_scalar(ki[:, 1], kb, 7, 63, ALU.logical_shift_right, ALU.bitwise_and)
                    dve.tensor_scalar(ki[:, 2], kb, 13, 127, ALU.logical_shift_right, ALU.bitwise_and)
                    dve.tensor_scalar(ki[:, 3], kb, 20, None, ALU.logical_shift_right)
                    dve.drain()
                    dve.tensor_copy(idx[:], ki[:])
                    dve.drain()
                    dve.tensor_scalar(idx[:, 3], idx[:, 3], float(VALID >> 20), None, ALU.subtract)
                    dve.drain()
                    io = g.iof[:, None, 0:TT].broadcast_to([128, GRP, TT])
                    dve.tensor_tensor(SH[:], io, idx[:, 1, :, None].broadcast_to([128, GRP, TT]), ALU.is_equal)
                    dve.tensor_tensor(DH[:], io, idx[:, 3, :, None].broadcast_to([128, GRP, TT]), ALU.is_equal)
                    dve.drain()

                    def one_hot(u):
                        s = r * GRP + u
                        if u >= 2:
                            dve.wait_ge(t_ps, s - 1)
                        dve.tensor_scalar(OS[:, u % 2], g.iof[:], idx[:, 0, u:u + 1], None, ALU.is_equal)
                        dve.tensor_scalar(OD[:, u], g.iof[:], idx[:, 2, u:u + 1], None, ALU.is_equal).then_inc(hot, 1)

                    def select(u):
                        dve.wait_ge(g_ps, r * GRP + u + 1)
                        for i in range(2):
                            dve.tensor_tensor(G1[:, i * VH:(i + 1) * VH, :], psg[i][:], SH[:, u, None, :].broadcast_to([128, VH, TT]), ALU.mult)
                        dve.tensor_tensor(G2[:], psd[:], DH[:, u, None, :].broadcast_to([128, HEADS, TT]), ALU.mult).then_inc(g_use, 1)
                        dve.drain()
                        dve.tensor_reduce(VS[:, u, :], G1[:], AX.X, ALU.add)
                        dve.tensor_reduce(VD[:, u, :], G2[:], AX.X, ALU.add)
                        dve.drain()

                    one_hot(0)
                    for u in range(GRP):
                        if u + 1 < GRP:
                            one_hot(u + 1)
                        select(u)
                    am = amax[:, None, :].broadcast_to([128, GRP, HEADS])
                    w4 = VW[:, :, 0:HEADS]
                    dve.tensor_tensor(w4, VS[:, :, 0:HEADS], VD[:], ALU.add)
                    dve.tensor_tensor(VM[:], VD[:], am, ALU.add)
                    dve.drain()
                    leaky(dve, w4, 0.2)
                    leaky(dve, VM[:], 0.2)
                    dve.tensor_tensor(w4, w4, VM[:], ALU.subtract).then_inc(scored, 1)
                    dve.wait_ge(expd, r + 1)
                    hv = VS[:, :, HEADS:V].rearrange("p u (h e) -> p u h e", h=HEADS)
                    ov = VW[:, :, HEADS:V].rearrange("p u (h e) -> p u h e", h=HEADS)
                    dve.tensor_tensor(ov, hv, w4[:, :, :, None].broadcast_to([128, GRP, HEADS, EXP]), ALU.mult)
                    dve.drain()
                    for u in range(GRP):
                        if u >= 2:
                            dve.wait_ge(x_used, r * GRP + u - 1)
                        dve.tensor_tensor(X[:, u % 2], VW[:, u, :, None].broadcast_to([128, V, TT]),
                                          DH[:, u, None, :].broadcast_to([128, V, TT]), ALU.mult).then_inc(x_ready, 1)
                    dve.wait_ge(x_used, r * GRP + GRP)

            @block.scalar
            def _(act):
                with loop(act) as r:
                    for u in range(GRP):
                        s = r * GRP + u
                        act.wait_ge(t_ps, s + 1)
                        if u >= 2:
                            act.wait_ge(g_ps, s - 1)
                        act.activation(OT[:, u % 2], pst[u % 2][:], ACT.Copy).then_inc(t_out, 1)
                    act.wait_ge(scored, r + 1)
                    w4 = VW[:, :, 0:HEADS]
                    act.activation(w4, w4, ACT.Exp).then_inc(expd, 1)

            @block.tensor
            def _(pe):
                pe.wait_ge(closed, 1)
                for i in range(2):
                    a = acc[i][:].rearrange("p v t -> p (v t)")
                    pe.matmul(a, zero[:], TS[:, 0:VH, :].rearrange("p v t -> p (v t)"), start=True, stop=False, skip_group_check=True)
                with loop(pe) as r:
                    def turn(u):
                        s = r * GRP + u
                        pe.wait_ge(hot, s + 1)
                        if u >= 2:
                            pe.wait_ge(t_out, s - 1)
                        pe.transpose(pst[u % 2][:, 0, :], OS[:, u % 2], g.ident[:])
                        pe.transpose(pst[u % 2][:, 1, :], OD[:, u], g.ident[:]).then_inc(t_ps, 1)

                    def gather(u):
                        s = r * GRP + u
                        pe.wait_ge(t_out, s + 1)
                        if u >= 1:
                            pe.wait_ge(g_use, s)
                        for i in range(2):
                            pe.matmul(psg[i][:].rearrange("p v t -> p (v t)"), OT[:, u % 2, 0, :],
                                      TS[:, i * VH:(i + 1) * VH, :].rearrange("p v t -> p (v t)"), start=True, stop=True)
                        pe.matmul(psd[:].rearrange("p v t -> p (v t)"), OT[:, u % 2, 1, :], TD[:].rearrange("p v t -> p (v t)"),
                                  start=True, stop=True).then_inc(g_ps, 1)

                    turn(0)
                    for u in range(GRP):
                        if u + 1 < GRP:
                            turn(u + 1)
                        gather(u)
                    for u in range(GRP):
                        pe.wait_ge(x_ready, r * GRP + u + 1)
                        for i in range(2):
                            mm = pe.matmul(acc[i][:].rearrange("p v t -> p (v t)"), OD[:, u],
                                           X[:, u % 2, i * VH:(i + 1) * VH, :].rearrange("p v t -> p (v t)"),
                                           start=False, stop=False, skip_group_check=True)
                        mm.then_inc(x_used, 1)
                for i in range(2):
                    a = acc[i][:].rearrange("p v t -> p (v t)")
                    mm = pe.matmul(a, zero[:], TS[:, 0:VH, :].rearrange("p v t -> p (v t)"), start=False, stop=True, skip_group_check=True)
                mm.then_inc(closed, 1)

        W2_, bg, lg, lb = sb("W2", [128, 2, HEADS, TT]), sb("bg", [128, HE]), sb("lg", [128, HE]), sb("lb", [128, HE])
        tmp, st = sb("tmp", [128, HE, TT]), sb("st", [128, TT, 2])
        S, R, C, G = (sb(s, [128, TT, EXP]) for s in ("S", "R", "C", "G"))
        st4 = sb("st4", [128, TT, EXP])
        p_in, e1, e2, rt, rtd, sh, ex, gated, g_ps2, g_out = map(sem, ("p_in", "e1", "e2", "rt", "rtd", "sh", "ex", "gated", "gp2", "g_out"))
        block = ctx.enter_context(nc.Block())
        psr = [t[:].rearrange("p a b -> p (a b)") for t in psg]

        @block.sync
        def _(sp):
            for t, p in ((bg, g.L2_ffn_b_gat), (lg, g.L2_ffn_ln_gamma), (lb, g.L2_ffn_ln_beta)):
                sp.dma_start(t[:], p[None, :].broadcast_to([128, HE])).then_inc(p_in, 16)

        @block.vector
        def _(dve):
            bct = lambda t: t[:, :, None].broadcast_to([128, HE, TT])
            dve.tensor_tensor(W2_[:, 0], TS[:, 0:HEADS, :], TD[:], ALU.add)
            dve.tensor_tensor(W2_[:, 1], TD[:], last[:, 0:HEADS, None].broadcast_to([128, HEADS, TT]), ALU.add)
            for i in range(2):
                dve.tensor_copy(A[:, i * VH:(i + 1) * VH, :], acc[i][:])
            dve.drain()
            leaky(dve, W2_[:], 0.2)
            for i in range(2):
                dve.tensor_tensor(W2_[:, i], W2_[:, i], TM[:], ALU.subtract)
            dve.drain()
            dve.nop().then_inc(e1, 1)
            dve.wait_ge(e2, 1)
            dve.tensor_tensor(W2_[:, 1], W2_[:, 1], g.cntB[:, None, :].broadcast_to([128, HEADS, TT]), ALU.mult)
            dve.drain()
            t4 = tmp[:].rearrange("p (h e) t -> p h e t", h=HEADS)
            for i in range(2):
                dve.tensor_tensor(A[:, 0:HEADS, :], A[:, 0:HEADS, :], W2_[:, i], ALU.add)
                for h in range(HEADS):
                    w = W2_[:, i, h, None, :].broadcast_to([128, EXP, TT])
                    if i == 0:
                        v = TS[:, HEADS + h * EXP:HEADS + (h + 1) * EXP, :]
                    else:
                        v = last[:, HEADS + h * EXP:HEADS + (h + 1) * EXP, None].broadcast_to([128, EXP, TT])
                    dve.tensor_tensor(t4[:, h], v, w, ALU.mult)
                dve.drain()
                dve.tensor_tensor(A[:, HEADS:V, :], A[:, HEADS:V, :], tmp[:], ALU.add)
                dve.drain()
            dve.tensor_scalar(A[:, 0:HEADS, :], A[:, 0:HEADS, :], 1e-30, None, ALU.add)
            dve.drain()
            dve.reciprocal(A[:, 0:HEADS, :], A[:, 0:HEADS, :])
            dve.drain()
            M = A[:, HEADS:V, :]
            for h in range(HEADS):
                mh = A[:, HEADS + h * EXP:HEADS + (h + 1) * EXP, :]
                dve.tensor_tensor(mh, mh, A[:, h:h + 1, :].broadcast_to([128, EXP, TT]), ALU.mult)
            dve.wait_ge(p_in, 48)
            dve.drain()
            dve.tensor_tensor(M, M, bct(bg), ALU.add)
            dve.drain()
            bst = lambda k: st[:, :, k:k + 1].rearrange("p t a -> p a t").broadcast_to([128, HE, TT])
            dve.tensor_reduce(st[:, :, 0:1], M.rearrange("p v t -> p t v"), AX.X, ALU.add)
            dve.drain()
            dve.tensor_scalar(st[:, :, 0:1], st[:, :, 0:1], 1.0 / HE, None, ALU.mult)
            dve.drain()
            dve.tensor_tensor(M, M, bst(0), ALU.subtract)
            dve.drain()
            dve.tensor_tensor(tmp[:], M, M, ALU.mult)
            dve.drain()
            dve.tensor_reduce(st[:, :, 1:2], tmp[:].rearrange("p v t -> p t v"), AX.X, ALU.add)
            dve.drain()
            dve.tensor_scalar(st[:, :, 1:2], st[:, :, 1:2], 1.0 / HE, None, ALU.mult)
            dve.drain()
            dve.nop().then_inc(rt, 1)
            dve.wait_ge(rtd, 1)
            dve.reciprocal(st[:, :, 1:2], st[:, :, 1:2])
            dve.drain()
            dve.tensor_tensor(M, M, bst(1), ALU.mult)
            dve.drain()
            dve.tensor_tensor(M, M, bct(lg), ALU.mult)
            dve.drain()
            dve.tensor_tensor(M, M, bct(lb), ALU.add)
            dve.drain()
            dve.tensor_reduce(S[:], M.rearrange("p (h e) t -> p t e h", h=HEADS), AX.X, ALU.add)
            dve.drain()
            dve.tensor_scalar(S[:], S[:], 1.0 / HEADS, None, ALU.mult)
            dve.drain()
            top2(dve, S, R, C, G, EXP)
            softmax_top2_before(dve, S, st4)
            dve.drain()
            dve.nop().then_inc(sh, 1)
            dve.wait_ge(ex, 1)
            softmax_top2_after(dve, S, G, st4)
            dve.nop().then_inc(gated, 1)

        @block.scalar
        def _(act):
            act.wait_ge(e1, 1)
            act.activation(W2_[:], W2_[:], ACT.Exp).then_inc(e2, 1)
            act.wait_ge(rt, 1)
            act.activation(st[:, :, 1:2], st[:, :, 1:2], ACT.Sqrt, bias=g.eps[:, 0:1]).then_inc(rtd, 1)
            act.wait_ge(sh, 1)
            act.activation(S[:], S[:], ACT.Exp).then_inc(ex, 1)
            for c in range(TT // 2):
                act.wait_ge(g_ps2, c + 1)
                act.activation(g.GT[0:EXP, c * 256:(c + 1) * 256], psr[c % 2][0:EXP, 0:256], ACT.Copy).then_inc(g_out, 1)

        @block.tensor
        def _(pe):
            pe.wait_ge(gated, 1)
            for c in range(TT // 2):
                if c >= 2:
                    pe.wait_ge(g_out, c - 1)
                for k in range(2):
                    mm = pe.transpose(psr[c % 2][0:EXP, k * 128:(k + 1) * 128], G[:, 2 * c + k, :], g.ident[:])
                mm.then_inc(g_ps2, 1)


SH_, SP_, SG = 8, 64, 64
DI = SH_ * SP_
KT = DI // 128
SEQ = SG
CW = CHG * SG
XB = KT + 1
DTR = 40
IPM = 2 * KT + 2


def l0_ffn(nc, g):
    with nc.cleanup_on_exit(), ExitStack() as ctx:
        sb = lambda s, shape: ctx.enter_context(nc.sbuf_tensor(f"hy_{s}", shape, F32))
        sem = lambda s: nc.alloc_semaphore(f"hy_{s}")
        wfx, wlg, bfx, blg = sb("wfx", [D, DI]), sb("wlg", [D, DI]), sb("bfx", [128, DI]), sb("blg", [128, DI])
        win, wdt = sb("win", [128, KT, 2 * DI + 128]), sb("wdt", [128, KT, DTR])
        wo, wout, wfd = sb("wo", [128, KT, DI]), sb("wout", [128, KT, D]), sb("wfd", [128, KT, SH_])
        cw, cb = sb("cw", [128, XB, 3]), sb("cb", [128, XB])
        dtb, negA, outb, Dp = sb("dtb", [DTR, 1]), sb("negA", [DTR, 1]), sb("outb", [128, 1]), sb("Dp", [128, SH_])
        delta, selS, selB, rms_w = sb("delta", [128, SEQ]), sb("selS", [128, CHP, CHG]), sb("selB", [DTR, CHG, 128]), sb("rms_w", [128, 128])
        PS = [ctx.enter_context(nc.psum_tensor(f"hy_ps{i}", [128, 512], F32)) for i in range(8)]
        dA_dram = nc.dram_tensor("hy_decays", [2, 2, SH_, CHP, SEQ], F32).ap()

        with ExitStack() as first:
            fsb = lambda s, shape: first.enter_context(nc.sbuf_tensor(f"hy_{s}", shape, F32))
            raw_in, raw_dt = fsb("raw_in", [128, 2 * KT + 1, DI]), fsb("raw_dt", [DTR, DI])
            raw_o, raw_out, raw_fd = fsb("raw_o", [128, KT, DI]), fsb("raw_out", [128, DI]), fsb("raw_fd", [SH_, DI])
            raw_fx, raw_x, raw_sl = fsb("raw_fx", [128, KT, D]), fsb("raw_x", [128, KT, D]), fsb("raw_sl", [SG, SP_])
            slT, bx, bxr = fsb("slT", [128, SG]), fsb("bx", [128, KT]), fsb("bxr", [128, KT, 128])
            nw, tmp, bsl, sl2 = fsb("nw", [128, KT]), fsb("tmp", [128, SH_]), fsb("bsl", [128, SG]), fsb("sl2", [SG, 128])
            ws = {s: nc.alloc_semaphore(f"hyw_{s}") for s in ("w_in", "z", "sel", "t_ps", "t_out", "ready", "c_ps", "a1", "a2", "sl")}
            block = first.enter_context(nc.Block())
            slow = dict(allow_slow_non_contiguous=True)
            col = lambda t: t.rearrange("(d a) -> d a", a=1)
            tiles = lambda t: t.rearrange("(k p) -> p k", p=128)
            NLOAD = 26

            @block.sync
            def _(sp):
                def ld(dst, src, **kw):
                    sp.dma_start(dst, src, **kw).then_inc(ws["w_in"], 16)
                sp.wait_ge(ws["z"], 1)
                W = g.L0_ffn_hy_in_w
                ld(raw_in[:], W[0:2 * DI + 128, :].rearrange("(m p) k -> p m k", p=128))
                ld(raw_dt[0:SH_, :], W[2 * DI + 128:2 * DI + 128 + SH_, :])
                ld(raw_dt[32:32 + SH_, :], W[2 * DI + 128 + SH_:, :])
                ld(raw_o[:], g.L0_ffn_hy_out_w.rearrange("(m p) k -> p m k", p=128))
                ld(raw_out[:], g.L0_ffn_out_w)
                ld(raw_fd[:], g.L0_ffn_hy_fcD_w)
                ld(raw_fx[:], g.L0_ffn_W_fx.rearrange("(m p) k -> p m k", p=128))
                ld(raw_x[:], g.L0_ffn_W_x.rearrange("(m p) k -> p m k", p=128))
                ld(raw_sl[:], g.L0_ffn_W_slice)
                ld(bx[:], tiles(g.L0_ffn_b_x), **slow)
                ld(nw[:], tiles(g.L0_ffn_hy_norm_w), **slow)
                ld(bsl[:], g.L0_ffn_b_slice[None, :].broadcast_to([128, SG]))
                ld(bfx[:], g.L0_ffn_b_fx[None, :].broadcast_to([128, DI]))
                ld(tmp[:], g.L0_ffn_temperature.rearrange("a h b c -> a (h b c)").broadcast_to([128, SH_]))
                for i in range(3):
                    ld(cw[:, :, i], g.L0_ffn_hy_conv_w[:, i].rearrange("(k p) -> p k", p=128), **slow)
                ld(cb[:], tiles(g.L0_ffn_hy_conv_b), **slow)
                ld(dtb[0:SH_, :], col(g.L0_ffn_hy_dt_bias), **slow)
                ld(dtb[32:32 + SH_, :], col(g.L0_ffn_hy_dt_bias), **slow)
                ld(negA[0:SH_, :], col(g.L0_ffn_hy_A_log), **slow)
                ld(negA[32:32 + SH_, :], col(g.L0_ffn_hy_A_log), **slow)
                ld(outb[:], col(g.L0_ffn_out_b), **slow)
                ld(Dp[:], g.L0_ffn_hy_D[None, :].broadcast_to([128, SH_]))
                ld(sl2[:, 0:SP_], g.L0_ffn_W_slice)
                ld(sl2[:, SP_:], g.L0_ffn_W_slice)

            @block.gpsimd
            def _(pool):
                made = [0]

                def step(ins):
                    made[0] += 1
                    ins.then_inc(ws["sel"], 1)
                    pool.wait_ge(ws["sel"], made[0])

                step(pool.memset(delta[:], 0.0))
                step(pool.memset(selS[:], 1.0))
                step(pool.memset(selB[:], 0.0))
                step(pool.memset(rms_w[:], 1.0 / DI))
                for j in range(2):
                    h = slice(SLOT * j, SLOT * (j + 1))
                    step(pool.affine_select(out=delta[h, :], in_=delta[h, :], compare_op=ALU.not_equal, fill=1.0, base=0,
                                            pattern=[[-1, SEQ]], channel_multiplier=1))
                    step(pool.affine_select(out=selS[h], in_=selS[h], compare_op=ALU.is_ge, fill=0.0, base=N - 1,
                                            pattern=[[0, CHP], [0, CHG]], channel_multiplier=-1))
                    step(pool.affine_select(out=selS[h], in_=selS[h], compare_op=ALU.is_equal, fill=0.0, base=j,
                                            pattern=[[2, CHP], [-1, CHG]], channel_multiplier=0))
                    r = slice(32 * j, 32 * j + CHG)
                    o = selB[r, :, SLOT * j:SLOT * (j + 1)]
                    step(pool.affine_select(out=o, in_=o, compare_op=ALU.not_equal, fill=1.0, base=0,
                                            pattern=[[-1, CHG], [0, SLOT]], channel_multiplier=1))

            srcs = []
            for m in range(2 * KT + 1):
                srcs.append(([raw_in[:, m, k * 128:(k + 1) * 128] for k in range(KT)], 128, win[:, :, m * 128:(m + 1) * 128]))
            for m in range(KT):
                srcs.append(([raw_o[:, m, k * 128:(k + 1) * 128] for k in range(KT)], 128, wo[:, :, m * 128:(m + 1) * 128]))
            srcs.append(([raw_out[:, k * 128:(k + 1) * 128] for k in range(KT)], 128, wout[:]))
            srcs.append(([raw_fx[:, k, :] for k in range(KT)], 128, wfx[:].rearrange("p (k n) -> p k n", k=KT)))
            srcs.append(([raw_fd[:, k * 128:(k + 1) * 128] for k in range(KT)], SH_, wfd[:]))
            srcs.append(([raw_dt[:, k * 128:(k + 1) * 128] for k in range(KT)], DTR, wdt[:]))
            srcs.append(([sl2[:]], SG, slT[:, None, :]))
            NT = len(srcs)

            @block.tensor
            def _(pe):
                pe.wait_ge(ws["w_in"], 16 * NLOAD)
                for n, (ins_, w, _) in enumerate(srcs):
                    if n >= 2:
                        pe.wait_ge(ws["t_out"], n - 1)
                    for k, s in enumerate(ins_):
                        mm = pe.transpose(PS[n % 2][:, k * w:(k + 1) * w], s, g.ident[0:w, 0:w])
                    mm.then_inc(ws["t_ps"], 1)
                pe.wait_ge(ws["t_out"], NT)
                pe.wait_ge(ws["ready"], 1)
                for h in range(SH_):
                    r = slice(SLOT * (h % 2), SLOT * (h % 2) + SLOT)
                    o = slice((h // 2) * SG, (h // 2 + 1) * SG)
                    pe.matmul(PS[2 + h % 2][:, o], raw_x[r, h // 2, :], slT[r, :], start=True, stop=True)
                    mm = pe.matmul(PS[4 + h % 2][:, o], bxr[r, h // 2, :], slT[r, :], start=True, stop=True)
                mm.then_inc(ws["c_ps"], 1)

            @block.scalar
            def _(act):
                act.wait_ge(ws["a1"], 1)
                act.activation(negA[:], negA[:], ACT.Exp).then_inc(ws["a2"], 1)

            @block.vector
            def _(dve):
                dve.memset(raw_dt[:], 0.0)
                dve.memset(dtb[:], 0.0)
                dve.memset(negA[:], 0.0).then_inc(ws["z"], 1)
                dve.wait_ge(ws["w_in"], 16 * NLOAD)
                dve.tensor_scalar(negA[:], negA[:], 88.0, None, ALU.min).then_inc(ws["a1"], 1)
                for n, (ins_, w, dst) in enumerate(srcs):
                    dve.wait_ge(ws["t_ps"], n + 1)
                    dve.tensor_copy(dst, PS[n % 2][:, 0:len(ins_) * w].rearrange("p (k n) -> p k n", n=w)).then_inc(ws["t_out"], 1)
                dve.drain()
                for k in range(KT):
                    dve.tensor_scalar(bxr[:, k, :], g.ones[:], bx[:, k:k + 1], None, ALU.mult)
                    dve.tensor_scalar(wo[:, k, :], wo[:, k, :], nw[:, k:k + 1], None, ALU.mult)
                dve.tensor_scalar(tmp[:], tmp[:], 1e-6, None, ALU.max)
                dve.drain()
                dve.reciprocal(tmp[:], tmp[:])
                dve.wait_ge(ws["a2"], 1)
                dve.tensor_scalar(negA[:], negA[:], -1.0, None, ALU.mult)
                dve.drain()
                dve.nop().then_inc(ws["ready"], 1)
                dve.wait_ge(ws["c_ps"], 1)
                for par in range(2):
                    heads = lambda t: t[:].rearrange("p (k a n) -> p a k n", a=2, n=SG)[:, par]
                    ps = lambda i: PS[i + par][:, 0:KT * SG].rearrange("p (k n) -> p k n", k=KT)
                    it = tmp[:].rearrange("p (k a) -> p a k", a=2)[:, par][:, :, None].broadcast_to([128, KT, SG])
                    dve.tensor_tensor(heads(wlg), ps(2), it, ALU.mult)
                    dve.tensor_tensor(heads(blg), ps(4), bsl[:, None, :].broadcast_to([128, KT, SG]), ALU.add)
                    dve.drain()
                    dve.tensor_tensor(heads(blg), heads(blg), it, ALU.mult)

        lent = g.XNG[:].rearrange("p q d -> p (q d)")
        HQT = SH_ * CHP * SEQ
        dAb = lent[:, 0:2 * HQT].rearrange("p (a n) -> p a n", a=2)
        L = lent[:, 2 * HQT:4 * HQT].rearrange("p (a n) -> p a n", a=2)
        XC, fx, sw, sst = sb("XC", [128, CW]), sb("fx", [128, CHP, DI]), sb("sw", [128, CHP, DI]), sb("sst", [128, CHP * SH_])
        rn, rb, uT, swT = sb("rn", [DTR, KT * SG]), sb("rb", [128, 2, 512]), sb("uT", [128, KT, CW]), sb("swT", [128, CHP, SH_, N])
        zs, xr = sb("zs", [128, KT, CW]), sb("xr", [128, XB, CHG, SEQ + 2])
        xs, Bs, Cs = sb("xs", [128, XB, CW]), sb("Bs", [64, CW]), sb("Cs", [64, CW])
        dtv, dt1, dA = sb("dtv", [DTR, CW]), sb("dt1", [DTR, CW]), sb("dA", [DTR, CW])
        xt, dtc, Dc = sw, sb("dtc", [128, 2, SH_, CHP]), sb("Dc", [128, SH_, CHP])
        E, W, rr = fx[:].rearrange("p q n -> p (q n)"), dAb[:, 0].rearrange("p (h q t) -> p h q t", q=CHP, t=SEQ), sb("rr", [128, CW])
        yg, sq = xs[:, 0:KT, :], uT
        ot = xt
        oT = uT[:].rearrange("p k n -> p (k n)")[:, 0:KT * CH].rearrange("p (k q j n) -> p k q j n", q=CHP, j=2, n=N)
        s = {n: sem(n) for n in ("xc", "lf_ps", "lg_out", "smx", "sme", "smd", "sn_ps", "rn", "st_ps", "rb_out", "u_out", "sT_ps", "sT_out",
                                 "ip_ps", "ip_out", "cv", "xs", "dtab", "dtln", "dt_rdy", "da_exp", "da_rdy", "da_ld", "xt_ps", "xt_out",
                                 "g_ps", "w_rdy", "y_ps", "yg1", "sq", "r_ps", "rt", "yg2", "ot_ps", "ot_out", "o_ps", "oT_out", "f_ps", "done", "settled")}
        da_st = [sem(f"da_st{i}") for i in range(2)]
        block = ctx.enter_context(nc.Block())
        half = lambda j: slice(SLOT * j, SLOT * (j + 1))

        @block.sync
        def _(sp):
            with sp.Fori(0, NCH) as c:
                sp.wait_ge(s["da_rdy"], c + 1)
                for a in range(2):
                    src = dA[32 * a:32 * a + SH_, :].rearrange("h (q j t) -> h q j t", j=2, t=SEQ)
                    for j in range(2):
                        sp.dma_start(dA_dram[j, a], src[:, :, j, :]).then_inc(da_st[j], 16)
                for j in range(2):
                    sp.wait_ge(da_st[j], 32 * c + 32)
                    src = dA_dram[j].rearrange("a h q t -> (a h q t)")[None, :].broadcast_to([SLOT, 2 * HQT])
                    sp.dma_start(dAb[half(j)].rearrange("p a n -> p (a n)"), src).then_inc(s["da_ld"], 16)

        @block.tensor
        def _(pe):
            def settle(sem, value):
                pe.wait_ge(sem, value)
                pe.sem_inc(s["settled"], 1)

            with pe.Fori(0, NCH) as c:
                pe.wait_ge(s["done"], c + 1)
                pe.wait_ge(s["xc"], c + 1)
                for q in range(CHP):
                    if q >= 2:
                        pe.wait_ge(s["lg_out"], 4 * c + q - 1)
                    x = XC[:, q * 128:(q + 1) * 128]
                    pe.matmul(PS[q % 2][:], x, wlg[:], start=True, stop=True)
                    pe.matmul(PS[2 + q % 2][:], x, wfx[:], start=True, stop=True).then_inc(s["lf_ps"], 1)
                pe.wait_ge(s["smd"], c + 1)
                for par in range(2):
                    for q in range(CHP):
                        rhs = sw[:, q, :].rearrange("p (k a n) -> p a k n", a=2, n=SG)[:, par]
                        mm = pe.matmul(PS[4][32 * par:32 * par + CHG, 0:KT * SG].rearrange("p (k n) -> p k n", k=KT), selS[:, q, :], rhs,
                                       start=(q == 0), stop=(q == CHP - 1))
                mm.then_inc(s["sn_ps"], 1)
                for q in range(CHP):
                    if q >= 2:
                        settle(s["u_out"], 4 * c + q - 1)
                    for j in range(2):
                        for h in range(SH_):
                            o = (h // 2) * SG
                            pe.matmul(PS[2 * (q % 2) + j][half(h % 2), o:o + SG], fx[rows(j), q, h * 64:(h + 1) * 64],
                                      sw[rows(j), q, h * 64:(h + 1) * 64], start=True, stop=True)
                    if q == 0:
                        pe.wait_ge(s["rn"], c + 1)
                    for j in range(2):
                        mm = pe.matmul(PS[5 + q % 2][:, j * 256:(j + 1) * 256], selB[:, 2 * q + j, :], rn[:], start=True, stop=True)
                    mm.then_inc(s["st_ps"], 1)
                for q in range(CHP):
                    if q < 2:
                        settle(s["u_out"], 4 * c + q + 3)
                    else:
                        settle(s["sT_out"], 4 * c + q - 1)
                    for j in range(2):
                        for h in range(SH_):
                            mm = pe.matmul(PS[2 * (q % 2) + j][half(j), h * N:(h + 1) * N], sw[rows(j), q, h * 64:(h + 1) * 64],
                                           g.ident[rows(j), rows(j)], start=True, stop=True)
                    mm.then_inc(s["sT_ps"], 1)
                pe.wait_ge(s["u_out"], 4 * c + 4)
                for m in range(IPM):
                    if m >= 4:
                        pe.wait_ge(s["ip_out"], IPM * c + m - 3)
                    for k in range(KT):
                        if m < IPM - 1:
                            mm = pe.matmul(PS[4 + m % 4][:], win[:, k, m * 128:(m + 1) * 128], uT[:, k, :], start=(k == 0), stop=(k == KT - 1))
                        else:
                            mm = pe.matmul(PS[4 + m % 4][0:DTR, :], wdt[:, k, :], uT[:, k, :], start=(k == 0), stop=(k == KT - 1))
                    mm.then_inc(s["ip_ps"], 1)
                pe.wait_ge(s["xs"], XB * c + XB)
                for q in range(CHP):
                    if q >= 2:
                        pe.wait_ge(s["xt_out"], 4 * c + q - 1)
                    for k in range(KT):
                        mm = pe.transpose(PS[q % 2][:, k * 128:(k + 1) * 128], xs[:, k, q * 128:(q + 1) * 128], g.ident[:])
                    mm.then_inc(s["xt_ps"], 1)
                settle(s["ip_out"], IPM * c + IPM)
                for q in range(CHP):
                    for j in range(2):
                        b = slice((2 * q + j) * SEQ, (2 * q + j + 1) * SEQ)
                        pe.matmul(PS[6][half(j), q * SEQ:(q + 1) * SEQ], Bs[:, b], Cs[:, b], start=True, stop=True)
                    for k in range(KT):
                        pe.matmul(PS[7][:, 160 + 8 * q:168 + 8 * q], xs[:, k, q * 128:(q + 1) * 128], wfd[:, k, :], start=(k == 0), stop=(k == KT - 1))
                settle(s["dt_rdy"], c + 1)
                for q in range(CHP):
                    mm = pe.transpose(PS[7][:, DTR * q:DTR * (q + 1)], dtv[:, q * 128:(q + 1) * 128], g.ident[0:DTR, 0:DTR])
                mm.then_inc(s["g_ps"], 1)
                pe.wait_ge(s["w_rdy"], c + 1)
                pe.wait_ge(s["xt_out"], 4 * c + 4)
                settle(s["sT_out"], 4 * c + 4)
                for q in range(CHP):
                    for j in range(2):
                        for h in range(SH_):
                            o = (h // 2) * 128 + (q % 2) * SEQ
                            mm = pe.matmul(PS[2 + 2 * (q // 2) + j][half(h % 2), o:o + SEQ], xt[half(j), q, h * 64:(h + 1) * 64],
                                           W[half(j), h, q, :], start=True, stop=True)
                    if q % 2:
                        mm.then_inc(s["y_ps"], 1)
                pe.wait_ge(s["sq"], c + 1)
                for k in range(KT):
                    mm = pe.matmul(PS[0][:], rms_w[:], sq[:, k, :], start=(k == 0), stop=(k == KT - 1))
                mm.then_inc(s["r_ps"], 1)
                pe.wait_ge(s["yg2"], c + 1)
                for q in range(CHP):
                    if q >= 2:
                        pe.wait_ge(s["ot_out"], 4 * c + q - 1)
                    for k in range(KT):
                        mm = pe.matmul(PS[6 + q % 2][:], yg[:, k, q * 128:(q + 1) * 128], wo[:, k, :], start=(k == 0), stop=(k == KT - 1))
                    mm.then_inc(s["ot_ps"], 1)
                for q in range(CHP):
                    settle(s["ot_out"], 4 * c + q + 1)
                    if q >= 2:
                        settle(s["oT_out"], 4 * c + q - 1)
                    for j in range(2):
                        for h in range(SH_):
                            o = (h // 2) * N
                            mm = pe.matmul(PS[2 + 2 * (q % 2) + j][half(h % 2), o:o + N], ot[half(j), q, h * 64:(h + 1) * 64],
                                           swT[half(j), q, h, :], start=True, stop=True)
                    mm.then_inc(s["o_ps"], 1)
                pe.wait_ge(s["oT_out"], 4 * c + 4)
                for k in range(KT):
                    mm = pe.matmul(PS[1][:, 0:CH], wout[:, k, :], oT[:, k].rearrange("p q j n -> p (q j n)"), start=(k == 0), stop=(k == KT - 1))
                mm.then_inc(s["f_ps"], 1)

        @block.scalar
        def _(act):
            with act.Fori(0, NCH) as c:
                act.wait_ge(s["done"], c + 1)
                act.activation(XC[:].rearrange("p (b n) -> p b n", n=SLOT), g.XNP[:, bass.ds(c * CHG, CHG), :], ACT.Copy).then_inc(s["xc"], 1)
                act.wait_ge(s["smx"], c + 1)
                act.activation(sw[:], sw[:], ACT.Exp).then_inc(s["sme"], 1)
                for q in range(CHP):
                    act.wait_ge(s["st_ps"], 4 * c + q + 1)
                    if q >= 2:
                        act.wait_ge(s["u_out"], 4 * c + q - 1)
                    act.activation(rb[:, q % 2], PS[5 + q % 2][:], ACT.Copy).then_inc(s["rb_out"], 1)
                for q in range(CHP):
                    act.wait_ge(s["sT_ps"], 4 * c + q + 1)
                    for j in range(2):
                        ins = act.activation(swT[half(j), q].rearrange("p h n -> p (h n)"), PS[2 * (q % 2) + j][half(j), 0:SH_ * N], ACT.Copy)
                    ins.then_inc(s["sT_out"], 1)
                for m in range(IPM):
                    act.wait_ge(s["ip_ps"], IPM * c + m + 1)
                    p = PS[4 + m % 4]
                    if m < KT:
                        ins = act.activation(zs[:, m, :], p[:], ACT.Silu)
                    elif m < IPM - 1:
                        ins = act.activation(xr[:, m - KT, :, 2:], p[:].rearrange("p (b t) -> p b t", t=SEQ), ACT.Copy)
                    else:
                        ins = act.activation(dtv[:], p[0:DTR, :], ACT.Identity, bias=dtb[:, 0:1])
                    ins.then_inc(s["ip_out"], 1)
                for i in range(KT):
                    act.wait_ge(s["cv"], XB * c + i + 1)
                    act.activation(xs[:, i, :], xs[:, i, :], ACT.Silu).then_inc(s["xs"], 1)
                act.wait_ge(s["cv"], XB * c + XB)
                act.activation(Bs[:], xs[0:64, KT, :], ACT.Silu)
                act.activation(Cs[:], xs[64:128, KT, :], ACT.Silu).then_inc(s["xs"], 1)
                act.wait_ge(s["dtab"], c + 1)
                act.activation(dt1[:], dt1[:], ACT.Exp, scale=-1.0)
                act.drain()
                act.activation(dt1[:], dt1[:], ACT.Ln, bias=1.0).then_inc(s["dtln"], 1)
                act.wait_ge(s["dt_rdy"], c + 1)
                act.activation(dA[:], dtv[:], ACT.Exp, scale=negA[:, 0:1]).then_inc(s["da_exp"], 1)
                for q in range(CHP):
                    act.wait_ge(s["xt_ps"], 4 * c + q + 1)
                    act.activation(xt[:, q, :], PS[q % 2][:], ACT.Copy).then_inc(s["xt_out"], 1)
                act.wait_ge(s["yg1"], c + 1)
                act.activation(sq[:], yg, ACT.Square).then_inc(s["sq"], 1)
                act.wait_ge(s["r_ps"], c + 1)
                act.activation(rr[:], PS[0][:], ACT.Sqrt, bias=g.eps[:, 0:1]).then_inc(s["rt"], 1)
                for q in range(CHP):
                    act.wait_ge(s["ot_ps"], 4 * c + q + 1)
                    act.activation(ot[:, q, :], PS[6 + q % 2][:], ACT.Copy).then_inc(s["ot_out"], 1)

        @block.vector
        def _(dve):
            dve.memset(rn[:], 0.0)
            dve.memset(xr[:], 0.0)
            dve.drain()
            dve.nop().then_inc(s["done"], 1)
            with dve.Fori(0, NCH) as c:
                for q in range(CHP):
                    dve.wait_ge(s["lf_ps"], 4 * c + q + 1)
                    dve.tensor_tensor(sw[:, q, :], PS[q % 2][:], blg[:], ALU.add)
                    dve.tensor_tensor(fx[:, q, :], PS[2 + q % 2][:], bfx[:], ALU.add).then_inc(s["lg_out"], 1)
                dve.drain()
                sw3 = sw[:].rearrange("p q (h n) -> p (q h) n", n=SG)
                bc = sst[:, :, None].broadcast_to([128, CHP * SH_, SG])
                dve.tensor_reduce(sst[:], sw3, AX.X, ALU.max)
                dve.drain()
                dve.tensor_tensor(sw3, sw3, bc, ALU.subtract).then_inc(s["smx"], 1)
                dve.wait_ge(s["sme"], c + 1)
                dve.tensor_reduce(sst[:], sw3, AX.X, ALU.add)
                dve.drain()
                dve.reciprocal(sst[:], sst[:])
                dve.drain()
                dve.tensor_tensor(sw3, sw3, bc, ALU.mult).then_inc(s["smd"], 1)
                dve.wait_ge(s["sn_ps"], c + 1)
                for par in range(2):
                    r = slice(32 * par, 32 * par + CHG)
                    dve.tensor_scalar(rn[r, :], PS[4][r, 0:KT * SG], 1e-5, None, ALU.add)
                dve.drain()
                for par in range(2):
                    r = slice(32 * par, 32 * par + CHG)
                    ins = dve.reciprocal(rn[r, :], rn[r, :])
                ins.then_inc(s["rn"], 1)
                for q in range(CHP):
                    dve.wait_ge(s["rb_out"], 4 * c + q + 1)
                    for j in range(2):
                        o = uT[:, :, (2 * q + j) * SG:(2 * q + j + 1) * SG]
                        v = lambda t: t.rearrange("p (k n) -> p k n", n=SG)
                        ins = dve.tensor_tensor(o, v(PS[2 * (q % 2) + j][:, 0:256]), v(rb[:, q % 2, j * 256:(j + 1) * 256]), ALU.mult)
                    ins.then_inc(s["u_out"], 1)
                for i in range(XB):
                    dve.wait_ge(s["ip_out"], IPM * c + KT + i + 1)
                    o = xs[:, i, :].rearrange("p (b t) -> p b t", t=SEQ)
                    dve.tensor_scalar(o, xr[:, i, :, 2:], cw[:, i, 2:3], cb[:, i:i + 1], ALU.mult, ALU.add)
                    dve.drain()
                    dve.scalar_tensor_tensor(o, xr[:, i, :, 1:SEQ + 1], cw[:, i, 1:2], o, ALU.mult, ALU.add)
                    dve.drain()
                    dve.scalar_tensor_tensor(o, xr[:, i, :, 0:SEQ], cw[:, i, 0:1], o, ALU.mult, ALU.add).then_inc(s["cv"], 1)
                dve.wait_ge(s["ip_out"], IPM * c + IPM)
                dve.scalar_tensor_tensor(dt1[:], dtv[:], -1.0, dtv[:], ALU.mult, ALU.max).then_inc(s["dtab"], 1)
                dve.wait_ge(s["dtln"], c + 1)
                dve.scalar_tensor_tensor(dtv[:], dtv[:], 0.0, dt1[:], ALU.max, ALU.add).then_inc(s["dt_rdy"], 1)
                dve.wait_ge(s["da_exp"], c + 1)
                d4 = dA[:].rearrange("p (b t) -> p b t", t=SEQ)
                dve.memset(d4[0:SH_, :, 0:1], 0.0)
                dve.memset(d4[32:32 + SH_, :, SEQ - 1:SEQ], 0.0).then_inc(s["da_rdy"], 1)
                dve.wait_ge(s["g_ps"], c + 1)
                dts = PS[7][:, 0:CHP * DTR].rearrange("p (q r) -> p r q", r=DTR)
                for a in range(2):
                    dve.tensor_copy(dtc[:, a], dts[:, 32 * a:32 * a + SH_, :])
                dve.tensor_tensor(Dc[:], PS[7][:, 160:160 + CHP * SH_].rearrange("p (q h) -> p h q", h=SH_),
                                  Dp[:, :, None].broadcast_to([128, SH_, CHP]), ALU.add)
                dve.drain()
                dlt = delta[:, None, :].broadcast_to([128, SH_ * CHP, SEQ])
                per = lambda t: t.rearrange("p h q -> p (h q)")[:, :, None].broadcast_to([128, SH_ * CHP, SEQ])
                E3 = E.rearrange("p (r t) -> p r t", t=SEQ)
                for a in range(2):
                    dve.tensor_tensor(E3, dlt, per(dtc[:, a]), ALU.mult)
                    dve.drain()
                    if a == 0:
                        dve.wait_ge(s["da_ld"], 32 * c + 32)
                    st = slice(None) if a == 0 else slice(None, None, -1)
                    dve.tensor_tensor_scan(L[:, a][:, st], dAb[:, a][:, st], E[:, st], 0.0, ALU.mult, ALU.add)
                    dve.drain()
                    G = PS[6][:, None, 0:CHP * SEQ].broadcast_to([128, SH_, CHP * SEQ])
                    l3 = L[:, a].rearrange("p (h n) -> p h n", h=SH_)
                    dve.tensor_tensor(l3, l3, G, ALU.mult)
                W3 = W.rearrange("p h q t -> p (h q) t")
                dve.tensor_tensor(W3, dlt, per(Dc[:]), ALU.mult)
                dve.drain()
                L3 = lambda a: L[:, a].rearrange("p (r t) -> p r t", t=SEQ)
                dve.tensor_tensor(W3[:, :, 1:], W3[:, :, 1:], L3(0)[:, :, :SEQ - 1], ALU.add)
                dve.drain()
                dve.tensor_tensor(W3[:, :, :SEQ - 1], W3[:, :, :SEQ - 1], L3(1)[:, :, 1:], ALU.add).then_inc(s["w_rdy"], 1)
                y5 = yg.rearrange("p k (q j t) -> p k q j t", j=2, t=SEQ)
                z5 = zs[:].rearrange("p k (q j t) -> p k q j t", j=2, t=SEQ)
                for f in range(2):
                    dve.wait_ge(s["y_ps"], 2 * c + f + 1)
                    for q in range(2 * f, 2 * f + 2):
                        for j in range(2):
                            p = PS[2 + 2 * f + j][:].rearrange("p (k q t) -> p k q t", k=KT, q=2)[:, :, q % 2, :]
                            ins = dve.tensor_tensor(y5[:, :, q, j, :], p, z5[:, :, q, j, :], ALU.mult)
                ins.then_inc(s["yg1"], 1)
                dve.wait_ge(s["rt"], c + 1)
                dve.reciprocal(rr[:], rr[:])
                dve.drain()
                dve.tensor_tensor(yg, yg, rr[:, None, :].broadcast_to([128, KT, CW]), ALU.mult).then_inc(s["yg2"], 1)
                for q in range(CHP):
                    dve.wait_ge(s["o_ps"], 4 * c + q + 1)
                    for j in range(2):
                        p = PS[2 + 2 * (q % 2) + j][:, 0:160].rearrange("p (k n) -> p k n", n=N)
                        ins = dve.tensor_copy(oT[:, :, q, j, :], p)
                    ins.then_inc(s["oT_out"], 1)
                dve.wait_ge(s["f_ps"], c + 1)
                x = chunk_cols(g.XT, c)
                dve.scalar_tensor_tensor(x, PS[1][:, 0:CH], outb[:, 0:1], x, ALU.add, ALU.add).then_inc(s["done"], 1)


def graph_network(nc, g):
    with ExitStack() as ctx:
        sb = lambda name, shape, dt=F32: ctx.enter_context(nc.sbuf_tensor(name, shape, dt))
        g.XT, g.XNP, g.XNG = sb("XT", [128, T]), sb("XNP", [128, B, SLOT]), sb("XNG", [128, PAIRS, D])
        g.ident, g.ones, g.mean_w, g.eps = sb("ident", [128, 128]), sb("ones", [128, 128]), sb("mean_w", [128, 128]), sb("eps", [128, 1])
        load_x(nc, g)
        with nc.sbuf_tensor("adjG0", [128, PAIRS, N], F32) as adjG, nc.sbuf_tensor("adjT0", [128, PAIRS, N], F32) as adjT, \
                nc.sbuf_tensor("betaT", [128, 4, N], F32) as betaT:
            g.adjG, g.adjT, g.betaT = adjG, adjT, betaT
            load_adjacency(nc, g, "a0", True)
            layer_norm(nc, g, g.XT, True, "n0")
            l0_gnn(nc, g)
        layer_norm(nc, g, g.XT, False, "n1")
        l0_ffn(nc, g)

        g.GT, g.iof, g.work = sb("GT", [8, T]), sb("iof", [128, 128]), sb("work", [128, EC])
        g.turns, g.cntB = sb("turns", [1, 1], I32), sb("cntB", [128, TT])
        edge_keys(nc, g)
        g.adjG, g.adjT = sb("adjG", [128, PAIRS, N]), sb("adjT", [128, PAIRS, N])
        load_adjacency(nc, g, "a1", False)
        layer_norm(nc, g, g.XT, True, "n2")
        l1_gnn(nc, g)
        layer_norm(nc, g, g.XT, False, "n3")
        layer_norm(nc, g, g.XNP, False, "n4")
        affine_xn(nc, g, g.L1_ffn_gamma, g.L1_ffn_beta)
        router(nc, g, "r1", 8, g.L1_ffn_Wr, g.L1_ffn_br, True)
        moe(nc, g, "f1", 8, g.L1_ffn_W1, g.L1_ffn_b1, g.L1_ffn_W2, g.L1_ffn_b2)
        layer_norm(nc, g, g.XT, True, "n5")
        l2_gnn(nc, g)
        layer_norm(nc, g, g.XT, False, "n6")
        edge_router(nc, g)
        moe(nc, g, "f2", EXP, g.L2_ffn_W1, g.L2_ffn_b1, g.L2_ffn_W2, g.L2_ffn_b2)
        layer_norm(nc, g, g.XT, True, "n7")
        l3_gnn(nc, g)
        layer_norm(nc, g, g.XT, False, "n8")
        router(nc, g, "r3", 8, g.L3_ffn_Wg, g.L3_ffn_bg, False)
        moe(nc, g, "f3", 8, g.L3_ffn_W1, g.L3_ffn_b1, g.L3_ffn_W2, g.L3_ffn_b2)
        store_output(nc, g)


def build(nc, x, adj, nodemask, L0_gnn_W, L0_gnn_bn_gamma, L0_gnn_bn_beta, L0_ffn_W_fx, L0_ffn_b_fx, L0_ffn_W_x, L0_ffn_b_x, L0_ffn_W_slice, L0_ffn_b_slice, L0_ffn_temperature, L0_ffn_hy_in_w, L0_ffn_hy_conv_w, L0_ffn_hy_conv_b, L0_ffn_hy_dt_bias, L0_ffn_hy_A_log, L0_ffn_hy_D, L0_ffn_hy_fcD_w, L0_ffn_hy_norm_w, L0_ffn_hy_out_w, L0_ffn_out_w, L0_ffn_out_b, L1_gnn_weight, L1_gnn_bias, L1_gnn_gamma, L1_gnn_beta, L1_ffn_gamma, L1_ffn_beta, L1_ffn_Wr, L1_ffn_br, L1_ffn_W1, L1_ffn_b1, L1_ffn_W2, L1_ffn_b2, L2_gnn_W, L2_ffn_W_gat, L2_ffn_att_src, L2_ffn_att_dst, L2_ffn_b_gat, L2_ffn_ln_gamma, L2_ffn_ln_beta, L2_ffn_W1, L2_ffn_b1, L2_ffn_W2, L2_ffn_b2, L2_ffn_edge_index, L3_gnn_fc_w, L3_gnn_fc_b, L3_gnn_q_w, L3_gnn_q_b, L3_gnn_k_w, L3_gnn_k_b, L3_gnn_fp_w, L3_gnn_fp_b, L3_ffn_Wg, L3_ffn_bg, L3_ffn_W1, L3_ffn_b1, L3_ffn_W2, L3_ffn_b2, out):
    g = Buffers()
    g.x, g.adj, g.nodemask, g.L0_gnn_W = x, adj, nodemask, L0_gnn_W
    g.L0_gnn_bn_gamma, g.L0_gnn_bn_beta, g.L0_ffn_W_fx, g.L0_ffn_b_fx = L0_gnn_bn_gamma, L0_gnn_bn_beta, L0_ffn_W_fx, L0_ffn_b_fx
    g.L0_ffn_W_x, g.L0_ffn_b_x, g.L0_ffn_W_slice, g.L0_ffn_b_slice = L0_ffn_W_x, L0_ffn_b_x, L0_ffn_W_slice, L0_ffn_b_slice
    g.L0_ffn_temperature, g.L0_ffn_hy_in_w, g.L0_ffn_hy_conv_w, g.L0_ffn_hy_conv_b = L0_ffn_temperature, L0_ffn_hy_in_w, L0_ffn_hy_conv_w, L0_ffn_hy_conv_b
    g.L0_ffn_hy_dt_bias, g.L0_ffn_hy_A_log, g.L0_ffn_hy_D, g.L0_ffn_hy_fcD_w = L0_ffn_hy_dt_bias, L0_ffn_hy_A_log, L0_ffn_hy_D, L0_ffn_hy_fcD_w
    g.L0_ffn_hy_norm_w, g.L0_ffn_hy_out_w, g.L0_ffn_out_w, g.L0_ffn_out_b = L0_ffn_hy_norm_w, L0_ffn_hy_out_w, L0_ffn_out_w, L0_ffn_out_b
    g.L1_gnn_weight, g.L1_gnn_bias, g.L1_gnn_gamma, g.L1_gnn_beta = L1_gnn_weight, L1_gnn_bias, L1_gnn_gamma, L1_gnn_beta
    g.L1_ffn_gamma, g.L1_ffn_beta, g.L1_ffn_Wr, g.L1_ffn_br = L1_ffn_gamma, L1_ffn_beta, L1_ffn_Wr, L1_ffn_br
    g.L1_ffn_W1, g.L1_ffn_b1, g.L1_ffn_W2, g.L1_ffn_b2 = L1_ffn_W1, L1_ffn_b1, L1_ffn_W2, L1_ffn_b2
    g.L2_gnn_W, g.L2_ffn_W_gat, g.L2_ffn_att_src, g.L2_ffn_att_dst = L2_gnn_W, L2_ffn_W_gat, L2_ffn_att_src, L2_ffn_att_dst
    g.L2_ffn_b_gat, g.L2_ffn_ln_gamma, g.L2_ffn_ln_beta, g.L2_ffn_W1 = L2_ffn_b_gat, L2_ffn_ln_gamma, L2_ffn_ln_beta, L2_ffn_W1
    g.L2_ffn_b1, g.L2_ffn_W2, g.L2_ffn_b2, g.L2_ffn_edge_index = L2_ffn_b1, L2_ffn_W2, L2_ffn_b2, L2_ffn_edge_index
    g.L3_gnn_fc_w, g.L3_gnn_fc_b, g.L3_gnn_q_w, g.L3_gnn_q_b = L3_gnn_fc_w, L3_gnn_fc_b, L3_gnn_q_w, L3_gnn_q_b
    g.L3_gnn_k_w, g.L3_gnn_k_b, g.L3_gnn_fp_w, g.L3_gnn_fp_b = L3_gnn_k_w, L3_gnn_k_b, L3_gnn_fp_w, L3_gnn_fp_b
    g.L3_ffn_Wg, g.L3_ffn_bg, g.L3_ffn_W1, g.L3_ffn_b1 = L3_ffn_Wg, L3_ffn_bg, L3_ffn_W1, L3_ffn_b1
    g.L3_ffn_W2, g.L3_ffn_b2 = L3_ffn_W2, L3_ffn_b2
    g.out = out
    graph_network(nc, g)


_INS = ['x', 'adj', 'nodemask', 'L0_gnn_W', 'L0_gnn_bn_gamma', 'L0_gnn_bn_beta', 'L0_ffn_W_fx', 'L0_ffn_b_fx', 'L0_ffn_W_x', 'L0_ffn_b_x', 'L0_ffn_W_slice', 'L0_ffn_b_slice', 'L0_ffn_temperature', 'L0_ffn_hy_in_w', 'L0_ffn_hy_conv_w', 'L0_ffn_hy_conv_b', 'L0_ffn_hy_dt_bias', 'L0_ffn_hy_A_log', 'L0_ffn_hy_D', 'L0_ffn_hy_fcD_w', 'L0_ffn_hy_norm_w', 'L0_ffn_hy_out_w', 'L0_ffn_out_w', 'L0_ffn_out_b', 'L1_gnn_weight', 'L1_gnn_bias', 'L1_gnn_gamma', 'L1_gnn_beta', 'L1_ffn_gamma', 'L1_ffn_beta', 'L1_ffn_Wr', 'L1_ffn_br', 'L1_ffn_W1', 'L1_ffn_b1', 'L1_ffn_W2', 'L1_ffn_b2', 'L2_gnn_W', 'L2_ffn_W_gat', 'L2_ffn_att_src', 'L2_ffn_att_dst', 'L2_ffn_b_gat', 'L2_ffn_ln_gamma', 'L2_ffn_ln_beta', 'L2_ffn_W1', 'L2_ffn_b1', 'L2_ffn_W2', 'L2_ffn_b2', 'L2_ffn_edge_index', 'L3_gnn_fc_w', 'L3_gnn_fc_b', 'L3_gnn_q_w', 'L3_gnn_q_b', 'L3_gnn_k_w', 'L3_gnn_k_b', 'L3_gnn_fp_w', 'L3_gnn_fp_b', 'L3_ffn_Wg', 'L3_ffn_bg', 'L3_ffn_W1', 'L3_ffn_b1', 'L3_ffn_W2', 'L3_ffn_b2']
_OUTS = [((B, N, D), "float32")]


def kernel(**inputs):
    import numpy as _np
    import concourse.bacc as _bacc
    from concourse import mybir as _mybir
    from concourse.bass_utils import run_bass_kernel_spmd as _run

    nc = _bacc.Bacc("TRN2", target_bir_lowering=False, num_devices=1)
    arrays, args = {}, []
    for name in _INS:
        a = _np.ascontiguousarray(inputs[name])
        arrays[f"in_{name}_dram"] = a
        args.append(nc.dram_tensor(f"in_{name}_dram", a.shape, _mybir.dt.from_np(a.dtype), kind="ExternalInput").ap())
    for i, (shape, dtype) in enumerate(_OUTS):
        dt = _mybir.dt.from_np(_np.dtype(dtype))
        args.append(nc.dram_tensor(f"out_{i}_dram", shape, dt, kind="ExternalOutput").ap())
    build(nc, *args)
    r = _run(nc, [arrays], core_ids=[0])
    return r.results[0]["out_0_dram"]
```

```python
import numpy as np
import concourse.bass as bass
from concourse import mybir
from contextlib import ExitStack

F32 = mybir.dt.float32
I32 = mybir.dt.int32
BF16 = mybir.dt.bfloat16
ALU = mybir.AluOpType
ACT = mybir.ActivationFunctionType
AX = mybir.AxisListType

B, N, D = 128, 40, 128
T = B * N
SLOT = 64
PAIRS = B // 2
CHG = 8
CH = CHG * N
NCH = B // CHG
CHP = CHG // 2
TT = T // 128
LNR = NCH // 2


class Buffers:
    pass


def rows(j):
    return slice(SLOT * j, SLOT * j + N)


def load_x(nc, g):
    with nc.cleanup_on_exit(), ExitStack() as ctx:
        xin = ctx.enter_context(nc.sbuf_tensor("xin", [128, TT, D], F32))
        pst = [ctx.enter_context(nc.psum_tensor(f"pst{i}", [128, 512], F32)) for i in range(2)]
        sem = lambda name: nc.alloc_semaphore(name)
        zeroed, ident_ready, xt_ps, xt_out = map(sem, ("zeroed", "ident_ready", "xt_ps", "xt_out"))
        block = ctx.enter_context(nc.Block())
        PARTS = 5
        TP = TT // PARTS
        x_in = [sem(f"x_in{i}") for i in range(PARTS)]

        @block.sync
        def _(sp):
            x = g.x.rearrange("b n d -> (b n) d").rearrange("(t p) d -> p t d", p=128)
            for i in range(PARTS):
                sp.dma_start(xin[:, i * TP:(i + 1) * TP, :], x[:, i * TP:(i + 1) * TP, :]).then_inc(x_in[i], 16)

        @block.gpsimd
        def _(pool):
            pool.memset(g.ident[:], 0.0).then_inc(zeroed, 1)
            pool.memset(g.mean_w[:], 1.0 / D)
            pool.memset(g.mean_row[:], 1.0 / D).then_inc(zeroed, 1)
            pool.memset(g.row[:], 1.0).then_inc(zeroed, 1)
            pool.wait_ge(zeroed, 3)
            pool.affine_select(out=g.mean_row[:], in_=g.mean_row[:], compare_op=ALU.is_equal, fill=0.0, base=0,
                               pattern=[[-1, LNR], [1, LNR]], channel_multiplier=0).then_inc(zeroed, 1)
            pool.wait_ge(zeroed, 4)
            for i in range(3):
                r = g.row[32 * i:32 * i + 32]
                pool.affine_select(out=r, in_=r, compare_op=ALU.is_equal, fill=0.0, base=0,
                                   pattern=[[-1, LNR], [0, 128]], channel_multiplier=1).then_inc(zeroed, 1)
                pool.wait_ge(zeroed, 5 + i)
            pool.affine_select(out=g.ident[:], in_=g.ident[:], compare_op=ALU.not_equal, fill=1.0, base=0,
                               pattern=[[-1, 128]], channel_multiplier=1).then_inc(ident_ready, 1)

        @block.tensor
        def _(pe):
            pe.wait_ge(ident_ready, 1)
            for c in range(TT // 4):
                if c % 2 == 0:
                    pe.wait_ge(x_in[c // 2], 16)
                if c >= 2:
                    pe.wait_ge(xt_out, c - 1)
                for k in range(4):
                    mm = pe.transpose(pst[c % 2][:, k * 128:(k + 1) * 128], xin[:, 4 * c + k, :], g.ident[:])
                mm.then_inc(xt_ps, 1)

        @block.scalar
        def _(act):
            for c in range(TT // 4):
                act.wait_ge(xt_ps, c + 1)
                act.activation(g.XT[:, c * 512:(c + 1) * 512], pst[c % 2][:], ACT.Copy).then_inc(xt_out, 1)

        @block.vector
        def _(dve):
            dve.memset(g.XNP[:], 0.0)
            dve.memset(g.eps[:], 1e-5)
            dve.memset(g.inv[:], 0.0)


def load_adjacency(nc, g, name, blocks):
    with nc.cleanup_on_exit(), ExitStack() as ctx:
        blk = ctx.enter_context(nc.sbuf_tensor(f"{name}_blk", [128, N], F32))
        psa = [[ctx.enter_context(nc.psum_tensor(f"{name}_ps{i}{j}", [128, CHP, N], F32)) for j in range(2)] for i in range(2)]
        sem = lambda s: nc.alloc_semaphore(f"{name}_{s}")
        adj_zero, adj_in, blk_ready, at_ps, at_out, steps = map(sem, ("adj_zero", "adj_in", "blk_ready", "at_ps", "at_out", "steps"))
        block = ctx.enter_context(nc.Block())

        @block.sync
        def _(sp):
            sp.wait_ge(adj_zero, 1)
            pairs = g.adj.rearrange("(q j) n m -> j n q m", j=2)
            for j in range(2):
                sp.dma_start(g.adjG[rows(j), :, :], pairs[j]).then_inc(adj_in, 16)

        @block.gpsimd
        def _(pool):
            pool.memset(blk[:], 1.0).then_inc(steps, 1)
            pool.wait_ge(steps, 1)
            if blocks:
                for j in range(2):
                    o = blk[SLOT * j:SLOT * j + SLOT, :].rearrange("p (a c) -> p a c", c=10)
                    pool.affine_select(out=o, in_=o, compare_op=ALU.is_ge, fill=0.0, base=0,
                                       pattern=[[-10, 4], [0, 10]], channel_multiplier=1).then_inc(steps, 1)
                    pool.wait_ge(steps, 2 + 2 * j)
                    pool.affine_select(out=o, in_=o, compare_op=ALU.is_ge, fill=0.0, base=9,
                                       pattern=[[10, 4], [0, 10]], channel_multiplier=-1).then_inc(steps, 1)
                    pool.wait_ge(steps, 3 + 2 * j)
            pool.nop().then_inc(blk_ready, 1)

        @block.tensor
        def _(pe):
            pe.wait_ge(adj_in, 32)
            for c in range(NCH):
                if c >= 2:
                    pe.wait_ge(at_out, c - 1)
                for q in range(CHP):
                    for j in range(2):
                        mm = pe.matmul(psa[c % 2][j][rows(j), q, :], g.adjG[rows(j), c * CHP + q, :],
                                       g.ident[rows(j), rows(j)], start=True, stop=True)
                mm.then_inc(at_ps, 1)

        @block.vector
        def _(dve):
            dve.memset(g.adjG[:], 0.0).then_inc(adj_zero, 1)
            dve.wait_ge(blk_ready, 1)
            for c in range(NCH):
                dve.wait_ge(at_ps, c + 1)
                for j in range(2):
                    o = g.adjT[rows(j), c * CHP:(c + 1) * CHP, :]
                    ps = psa[c % 2][j][rows(j), :, :]
                    if blocks:
                        ins = dve.tensor_tensor(o, ps, blk[rows(j), None, :].broadcast_to([N, CHP, N]), ALU.mult)
                    else:
                        ins = dve.tensor_copy(o, ps)
                ins.then_inc(at_out, 1)


def split_parts(dve, value, parts, rest, low):
    for i, p in enumerate(parts):
        dve.tensor_copy(low, value)
        dve.drain()
        if i < 2:
            dve.tensor_tensor(rest, value, low, ALU.subtract)
        dve.tensor_copy(p, low)
        dve.drain()
        value = rest


def layer_norm(nc, g, src, slots=False, name="ln"):
    with nc.cleanup_on_exit(), ExitStack() as ctx:
        psm = [ctx.enter_context(nc.psum_tensor(f"{name}_m{i}", [128, CH], F32)) for i in range(2)]
        psv = [ctx.enter_context(nc.psum_tensor(f"{name}_v{i}", [LNR, CH], F32)) for i in range(2)]
        psr = [ctx.enter_context(nc.psum_tensor(f"{name}_r{i}", [128, CH], F32)) for i in range(2)]
        pst = [ctx.enter_context(nc.psum_tensor(f"{name}_t{i}", [128, CHP, 128], F32)) for i in range(2)]
        sq = ctx.enter_context(nc.sbuf_tensor(f"{name}_sq", [128, 3, CH], F32))
        low = ctx.enter_context(nc.sbuf_tensor(f"{name}_low", [LNR, CH], BF16))
        sd = ctx.enter_context(nc.sbuf_tensor(f"{name}_sd", [LNR, 2, CH], F32))
        sem = lambda s: nc.alloc_semaphore(f"{name}_{s}")
        mean_ps, centred, squared, var_ps, root, inverse, r_ps, normed, tr_ps, tr_out = map(sem, (
            "mean_ps", "centred", "squared", "var_ps", "root", "inverse", "r_ps", "normed", "tr_ps", "tr_out"))
        block = ctx.enter_context(nc.Block())
        dst = lambda c: g.XNP[:, c * CHG:(c + 1) * CHG, 0:N]
        if src is g.XNP:
            inp = dst
        else:
            inp = lambda c: src[:, c * CH:(c + 1) * CH].rearrange("p (b n) -> p b n", n=N)
        v3 = lambda t: t.rearrange("p (b n) -> p b n", n=N)

        @block.tensor
        def _(pe):
            def mean(c):
                if c >= 2:
                    pe.wait_ge(centred, c - 1)
                pe.matmul(psm[c % 2][:], g.mean_w[:], inp(c), start=True, stop=True).then_inc(mean_ps, 1)

            def var(c):
                pe.wait_ge(squared, c + 1)
                pe.matmul(psv[c // LNR][:], g.mean_row[:, c % LNR, :], sq[:, c % 3, :], start=(c % LNR == 0), stop=(c % LNR == LNR - 1)).then_inc(var_ps, 1)

            def spread(c):
                if c % LNR == 0:
                    pe.wait_ge(inverse, c // LNR + 1)
                if c >= 2:
                    pe.wait_ge(normed, c - 1)
                pe.matmul(psr[c % 2][:], g.row[:, c % LNR, :], g.inv[:, c // LNR, :], start=True, stop=True).then_inc(r_ps, 1)

            def turn(c):
                pe.wait_ge(normed, c + 1)
                if c >= 2:
                    pe.wait_ge(tr_out, c - 1)
                for q in range(CHP):
                    p = g.XNP[:, c * CHG + 2 * q:c * CHG + 2 * q + 2, :].rearrange("p b n -> p (b n)")
                    mm = pe.transpose(pst[c % 2][:, q, :], p, g.ident[:])
                mm.then_inc(tr_ps, 1)

            for c in range(NCH + LNR + 4):
                if c < NCH:
                    mean(c)
                if 2 <= c <= NCH + 1:
                    var(c - 2)
                k = c - LNR - 2
                if 0 <= k < NCH:
                    spread(k)
                if slots and 1 <= k <= NCH:
                    turn(k - 1)

        def turned(act, c):
            act.wait_ge(tr_ps, c + 1)
            act.activation(g.XNG[:, c * CHP:(c + 1) * CHP, :], pst[c % 2][:], ACT.Copy).then_inc(tr_out, 1)

        @block.scalar
        def _(act):
            for c in range(NCH + LNR + 4):
                if c < NCH:
                    act.wait_ge(centred, c + 1)
                    if c >= 3:
                        act.wait_ge(var_ps, c - 2)
                    act.activation(v3(sq[:, c % 3, :]), dst(c), ACT.Square).then_inc(squared, 1)
                if c % LNR == 0 and 0 < c <= NCH:
                    act.wait_ge(var_ps, c)
                    act.activation(sd[:, c // LNR - 1, :], psv[c // LNR - 1][:], ACT.Sqrt, bias=g.eps[0:LNR, 0:1]).then_inc(root, 1)
                k = c - LNR - 3
                if slots and 0 <= k < NCH:
                    turned(act, k)

        @block.vector
        def _(dve):
            for c in range(NCH + LNR + 3):
                if c < NCH:
                    dve.wait_ge(mean_ps, c + 1)
                    dve.tensor_tensor(dst(c), inp(c), v3(psm[c % 2][:]), ALU.subtract).then_inc(centred, 1)
                if c % LNR == 1 and 1 < c <= NCH + 1:
                    k = c // LNR - 1
                    dve.wait_ge(root, k + 1)
                    dve.reciprocal(sd[:, k, :], sd[:, k, :])
                    dve.drain()
                    split_parts(dve, sd[:, k, :], [g.inv[32 * i:32 * i + LNR, k, :] for i in range(3)], sd[:, k, :], low[:])
                    dve.nop().then_inc(inverse, 1)
                k = c - LNR - 2
                if 0 <= k < NCH:
                    dve.wait_ge(r_ps, k + 1)
                    dve.tensor_tensor(dst(k), dst(k), v3(psr[k % 2][:]), ALU.mult).then_inc(normed, 1)


def gnn_first(nc, g, name, AT, W, finish):
    with nc.cleanup_on_exit(), ExitStack() as ctx:
        psz = [[ctx.enter_context(nc.psum_tensor(f"{name}_z{i}{j}", [128, CHP, N], F32)) for j in range(2)] for i in range(2)]
        psy = [ctx.enter_context(nc.psum_tensor(f"{name}_y{i}", [128, CH], F32)) for i in range(2)]
        Z = ctx.enter_context(nc.sbuf_tensor(f"{name}_Z", [128, 2, CHP, 2, N], F32))
        Wt = ctx.enter_context(nc.sbuf_tensor(f"{name}_W", [D, D], F32))
        Y = ctx.enter_context(nc.sbuf_tensor(f"{name}_Y", [128, T], F32))
        sem = lambda s: nc.alloc_semaphore(f"{name}_{s}")
        w_in, z_ps, z_out, y_ps, y_out = map(sem, ("w_in", "z_ps", "z_out", "y_ps", "y_out"))
        loads, fin = finish(ctx, Y)
        block = ctx.enter_context(nc.Block())

        @block.sync
        def _(sp):
            sp.dma_start(Wt[:], W).then_inc(w_in, 16)
            loads(sp)

        @block.tensor
        def _(pe):
            def project(c):
                pe.wait_ge(z_out, c + 1)
                if c >= 2:
                    pe.wait_ge(y_out, c - 1)
                pe.matmul(psy[c % 2][:], Wt[:], Z[:, c % 2].rearrange("p q j n -> p (q j n)"),
                          start=True, stop=True).then_inc(y_ps, 1)

            pe.wait_ge(w_in, 16)
            for c in range(NCH + 1):
                if c < NCH:
                    if c >= 2:
                        pe.wait_ge(z_out, c - 1)
                    for q in range(CHP):
                        for j in range(2):
                            mm = pe.matmul(psz[c % 2][j][:, q, :], g.XNG[rows(j), c * CHP + q, :],
                                           AT[rows(j), c * CHP + q, :], start=True, stop=True)
                    mm.then_inc(z_ps, 1)
                if c >= 1:
                    project(c - 1)

        @block.scalar
        def _(act):
            for c in range(NCH):
                act.wait_ge(y_ps, c + 1)
                act.activation(Y[:, c * CH:(c + 1) * CH], psy[c % 2][:], ACT.Copy).then_inc(y_out, 1)
            fin["act"](act)

        @block.vector
        def _(dve):
            for c in range(NCH):
                dve.wait_ge(z_ps, c + 1)
                if c >= 2:
                    dve.wait_ge(y_ps, c - 1)
                dve.tensor_copy(Z[:, c % 2, :, 0, :], psz[c % 2][0][:])
                dve.tensor_copy(Z[:, c % 2, :, 1, :], psz[c % 2][1][:]).then_inc(z_out, 1)
            dve.wait_ge(y_out, NCH)
            fin["dve"](dve)


def l0_gnn(nc, g):
    def finish(ctx, Y):
        sb = lambda s, shape: ctx.enter_context(nc.sbuf_tensor(f"bn_{s}", shape, F32))
        sem = lambda s: nc.alloc_semaphore(f"bn_{s}")
        mean, var, sdv = sb("mean", [128, N]), sb("var", [128, N]), sb("sdv", [128, N])
        S = sb("S", [128, T])
        gam, bet = sb("gam", [128, N]), sb("bet", [128, N])
        pin, vrd, sq, rt = sem("pin"), sem("vrd"), sem("sq"), sem("rt")
        nview = Y[:].rearrange("p (b n) -> p n b", n=N)
        sview = S[:].rearrange("p (b n) -> p n b", n=N)
        bc = lambda t: t[:, None, :].broadcast_to([128, B, N])
        y3, s3 = Y[:].rearrange("p (b n) -> p b n", n=N), S[:].rearrange("p (b n) -> p b n", n=N)

        def loads(sp):
            with nc.allow_non_contiguous_dma("small parameters, feature-major"):
                for n0 in range(0, N, 10):
                    i = n0 // 10
                    sp.dma_start(gam[:, n0:n0 + 10], g.L0_gnn_bn_gamma[i, n0 * D:(n0 + 10) * D].rearrange("(n d) -> d n", d=D),
                                 allow_slow_non_contiguous=True).then_inc(pin, 16)
                for i in range(4):
                    sp.dma_start(g.betaT[:, i, :], g.L0_gnn_bn_beta[i, :].rearrange("(n d) -> d n", d=D),
                                 allow_slow_non_contiguous=True).then_inc(pin, 16)

        def dve_part(dve):
            dve.tensor_reduce(mean[:], nview, AX.X, ALU.add)
            dve.drain()
            dve.tensor_scalar(mean[:], mean[:], 1.0 / B, None, ALU.mult)
            dve.drain()
            dve.tensor_tensor(y3, y3, bc(mean), ALU.subtract).then_inc(vrd, 1)
            dve.wait_ge(sq, 1)
            dve.tensor_reduce(var[:], sview, AX.X, ALU.add)
            dve.drain()
            dve.tensor_scalar(var[:], var[:], 1.0 / B, None, ALU.mult).then_inc(vrd, 1)
            dve.wait_ge(pin, 128)
            dve.tensor_tensor(bet[:], g.betaT[:, 0, :], g.betaT[:, 1, :], ALU.add)
            for i in (2, 3):
                dve.drain()
                dve.tensor_tensor(bet[:], bet[:], g.betaT[:, i, :], ALU.add)
            dve.wait_ge(rt, 1)
            dve.reciprocal(sdv[:], sdv[:])
            dve.drain()
            dve.tensor_tensor(sdv[:], sdv[:], gam[:], ALU.mult)
            dve.drain()
            dve.tensor_tensor(y3, y3, bc(sdv), ALU.mult)
            dve.drain()
            dve.tensor_tensor(y3, y3, bc(bet), ALU.add)
            dve.drain()
            dve.tensor_tensor(g.XT[:], g.XT[:], Y[:], ALU.add)

        def act_part(act):
            act.wait_ge(vrd, 1)
            act.activation(S[:], Y[:], ACT.Square).then_inc(sq, 1)
            act.wait_ge(vrd, 2)
            act.activation(sdv[:], var[:], ACT.Sqrt, bias=g.eps[:, 0:1]).then_inc(rt, 1)

        return loads, {"dve": dve_part, "act": act_part}
    gnn_first(nc, g, "g0", g.adjT, g.L0_gnn_W, finish)


def l1_gnn(nc, g):
    def finish(ctx, Y):
        sb = lambda s, shape: ctx.enter_context(nc.sbuf_tensor(f"mn_{s}", shape, F32))
        sem = lambda s: nc.alloc_semaphore(f"mn_{s}")
        M, par, st = sb("M", [128, T]), sb("par", [128, 3]), sb("st", [128, 4])
        S = g.XNP[:, :, 0:N]
        y3, m3 = Y[:].rearrange("p (b n) -> p b n", n=N), M[:].rearrange("p (b n) -> p b n", n=N)
        pin, vrd, rt = sem("pin"), sem("vrd"), sem("rt")

        def loads(sp):
            for i, p in enumerate((g.L1_gnn_bias, g.L1_gnn_gamma, g.L1_gnn_beta)):
                sp.dma_start(par[:, i:i + 1], p.rearrange("(d a) -> d a", a=1), allow_slow_non_contiguous=True).then_inc(pin, 16)
            sp.dma_start(M[:], g.nodemask.rearrange("b n -> (b n)")[None, :].broadcast_to([128, T])).then_inc(pin, 16)

        def dve_part(dve):
            dve.wait_ge(pin, 64)
            step = [lambda: dve.tensor_scalar(Y[:], Y[:], par[:, 0:1], None, ALU.add),
                    lambda: dve.tensor_reduce(st[:, 0:1], M[:], AX.X, ALU.add),
                    lambda: dve.tensor_tensor(S, y3, m3, ALU.mult),
                    lambda: dve.tensor_reduce(st[:, 1:2], S, AX.XY, ALU.add),
                    lambda: dve.reciprocal(st[:, 0:1], st[:, 0:1]),
                    lambda: dve.tensor_tensor(st[:, 1:2], st[:, 1:2], st[:, 0:1], ALU.mult),
                    lambda: dve.tensor_scalar(Y[:], Y[:], st[:, 1:2], None, ALU.subtract),
                    lambda: dve.tensor_tensor(S, y3, y3, ALU.mult),
                    lambda: dve.tensor_tensor(S, S, m3, ALU.mult),
                    lambda: dve.tensor_reduce(st[:, 2:3], S, AX.XY, ALU.add)]
            for s in step:
                s()
                dve.drain()
            dve.tensor_tensor(st[:, 2:3], st[:, 2:3], st[:, 0:1], ALU.mult).then_inc(vrd, 1)
            dve.wait_ge(rt, 1)
            dve.reciprocal(st[:, 3:4], st[:, 3:4])
            dve.drain()
            dve.tensor_tensor(st[:, 3:4], st[:, 3:4], par[:, 1:2], ALU.mult)
            dve.drain()
            dve.tensor_scalar(Y[:], Y[:], st[:, 3:4], par[:, 2:3], ALU.mult, ALU.add)
            dve.drain()
            dve.tensor_tensor(Y[:], Y[:], M[:], ALU.mult)
            dve.drain()
            dve.scalar_tensor_tensor(g.XT[:], Y[:], 0.0, g.XT[:], ALU.max, ALU.add)

        def act_part(act):
            act.wait_ge(vrd, 1)
            act.activation(st[:, 3:4], st[:, 2:3], ACT.Sqrt, bias=g.eps[:, 0:1]).then_inc(rt, 1)

        return loads, {"dve": dve_part, "act": act_part}
    gnn_first(nc, g, "g1", g.adjT, g.L1_gnn_weight, finish)


def store_output(nc, g, dst=None):
    with nc.cleanup_on_exit(), ExitStack() as ctx:
        xo = ctx.enter_context(nc.sbuf_tensor("xo", [128, TT, D], F32))
        pst = [ctx.enter_context(nc.psum_tensor(f"pso{i}", [128, 4, 128], F32)) for i in range(2)]
        sem = lambda name: nc.alloc_semaphore(name)
        out_ps, out_sb, stored = sem("out_ps"), sem("out_sb"), sem("stored")
        block = ctx.enter_context(nc.Block())

        @block.tensor
        def _(pe):
            for c in range(TT // 4):
                if c >= 2:
                    pe.wait_ge(out_sb, c - 1)
                for k in range(4):
                    t = 4 * c + k
                    mm = pe.transpose(pst[c % 2][:, k, :], g.XT[:, t * 128:(t + 1) * 128], g.ident[:])
                mm.then_inc(out_ps, 1)

        @block.scalar
        def _(act):
            for c in range(TT // 4):
                act.wait_ge(out_ps, c + 1)
                act.activation(xo[:, 4 * c:4 * c + 4, :], pst[c % 2][:], ACT.Copy).then_inc(out_sb, 1)

        @block.sync
        def _(sp):
            sp.wait_ge(out_sb, TT // 4)
            sp.dma_start((g.out if dst is None else dst).rearrange("b n d -> (b n) d").rearrange("(t p) d -> p t d", p=128), xo[:]).then_inc(stored, 16)
            sp.wait_ge(stored, 16)


def chunk_view(g, c):
    return g.XNP[:, bass.ds(c * CHG, CHG), 0:N]


def chunk_cols(t, c):
    return t[:, bass.ds(c * CH, CH)]


def affine_xn(nc, g, gamma, beta):
    with nc.cleanup_on_exit(), ExitStack() as ctx:
        par = ctx.enter_context(nc.sbuf_tensor("aff_par", [128, 2], F32))
        pin = nc.alloc_semaphore("aff_in")
        block = ctx.enter_context(nc.Block())

        @block.sync
        def _(sp):
            for i, p in enumerate((gamma, beta)):
                sp.dma_start(par[:, i:i + 1], p.rearrange("(d a) -> d a", a=1), allow_slow_non_contiguous=True).then_inc(pin, 16)

        @block.vector
        def _(dve):
            dve.wait_ge(pin, 32)
            x = g.XNP[:, :, 0:N]
            dve.tensor_scalar(x, x, par[:, 0:1], par[:, 1:2], ALU.mult, ALU.add)


def top2(dve, S, R, C, G, E):
    for i in range(E):
        si = lambda n: S[:, :, i:i + 1].broadcast_to([128, TT, n])
        if i:
            dve.tensor_tensor(C[:, :, 0:i], S[:, :, 0:i], si(i), ALU.is_ge)
        if i < E - 1:
            dve.tensor_tensor(C[:, :, i + 1:E], S[:, :, i + 1:E], si(E - 1 - i), ALU.is_gt)
        dve.memset(C[:, :, i:i + 1], 0.0)
        dve.drain()
        dve.tensor_reduce(R[:, :, i:i + 1], C[:], AX.X, ALU.add)
        dve.drain()
    dve.tensor_scalar(G[:], R[:], 1.5, None, ALU.is_lt)
    dve.drain()


def softmax_top2_before(dve, S, st):
    E = S.shape[2]
    dve.tensor_reduce(st[:, :, 0:1], S[:], AX.X, ALU.max)
    dve.drain()
    dve.tensor_tensor(S[:], S[:], st[:, :, 0:1].broadcast_to([128, TT, E]), ALU.subtract)


def softmax_top2_after(dve, S, G, st):
    E = S.shape[2]
    dve.tensor_tensor(G[:], G[:], S[:], ALU.mult)
    dve.drain()
    dve.tensor_reduce(st[:, :, 0:1], G[:], AX.X, ALU.add)
    dve.drain()
    dve.reciprocal(st[:, :, 0:1], st[:, :, 0:1])
    dve.drain()
    dve.tensor_tensor(G[:], G[:], st[:, :, 0:1].broadcast_to([128, TT, E]), ALU.mult)
    dve.drain()


def router(nc, g, name, E, Wr, br, soft):
    with nc.cleanup_on_exit(), ExitStack() as ctx:
        sb = lambda s, shape: ctx.enter_context(nc.sbuf_tensor(f"{name}_{s}", shape, F32))
        sem = lambda s: nc.alloc_semaphore(f"{name}_{s}")
        wr, brt, LT = sb("wr", [D, E]), sb("brt", [E, 1]), sb("LT", [E, T])
        S, R, C, G, st = (sb(s, [128, TT, E]) for s in ("S", "R", "C", "G", "st"))
        G3 = sb("G3", [128, TT, 3, E])
        low = ctx.enter_context(nc.sbuf_tensor(f"{name}_low", [128, TT, E], BF16))
        psl = [ctx.enter_context(nc.psum_tensor(f"{name}_l{i}", [E, CH], F32)) for i in range(2)]
        pss = ctx.enter_context(nc.psum_tensor(f"{name}_s", [128, TT, E], F32))
        psg = [ctx.enter_context(nc.psum_tensor(f"{name}_g{i}", [3 * E, 512], F32)) for i in range(2)]
        w_in, l_ps, l_out, s_ps, shifted, expd, gated, g_ps, g_out = map(sem, (
            "w_in", "l_ps", "l_out", "s_ps", "shifted", "expd", "gated", "g_ps", "g_out"))
        block = ctx.enter_context(nc.Block())

        @block.sync
        def _(sp):
            sp.dma_start(wr[:], Wr).then_inc(w_in, 16)
            sp.dma_start(brt[:], br.rearrange("(e a) -> e a", a=1), allow_slow_non_contiguous=True).then_inc(w_in, 16)

        @block.tensor
        def _(pe):
            pe.wait_ge(w_in, 32)
            for c in range(NCH):
                if c >= 2:
                    pe.wait_ge(l_out, c - 1)
                pe.matmul(psl[c % 2][:], wr[:], chunk_view(g, c), start=True, stop=True).then_inc(l_ps, 1)
            pe.wait_ge(l_out, NCH)
            for t in range(TT):
                mm = pe.transpose(pss[:, t, :], LT[:, t * 128:(t + 1) * 128], g.ident[0:E, 0:E])
            mm.then_inc(s_ps, 1)
            pe.wait_ge(gated, 1)
            for c in range(TT // 4):
                if c >= 2:
                    pe.wait_ge(g_out, c - 1)
                for k in range(4):
                    mm = pe.transpose(psg[c % 2][:, k * 128:(k + 1) * 128], G3[:, 4 * c + k].rearrange("p i e -> p (i e)"), g.ident[:])
                mm.then_inc(g_ps, 1)

        @block.scalar
        def _(act):
            act.wait_ge(w_in, 32)
            for c in range(NCH):
                act.wait_ge(l_ps, c + 1)
                act.activation(LT[:, c * CH:(c + 1) * CH], psl[c % 2][:], ACT.Identity, bias=brt[:, 0:1]).then_inc(l_out, 1)
            if soft:
                act.wait_ge(shifted, 1)
                act.activation(S[:], S[:], ACT.Exp).then_inc(expd, 1)
            for c in range(TT // 4):
                act.wait_ge(g_ps, c + 1)
                act.activation(g.GT[0:3 * E, c * 512:(c + 1) * 512], psg[c % 2][:], ACT.Copy).then_inc(g_out, 1)

        @block.vector
        def _(dve):
            dve.wait_ge(s_ps, 1)
            dve.tensor_copy(S[:], pss[:])
            dve.drain()
            top2(dve, S, R, C, G, E)
            if soft:
                softmax_top2_before(dve, S, st)
                dve.drain()
                dve.nop().then_inc(shifted, 1)
                dve.wait_ge(expd, 1)
                softmax_top2_after(dve, S, G, st)
            split_parts(dve, G[:], [G3[:, :, i, :] for i in range(3)], G[:], low[:])
            dve.nop().then_inc(gated, 1)


def moe(nc, g, name, E, W1, b1, W2, b2):
    H2 = W1.shape[2] // 128
    with nc.cleanup_on_exit(), ExitStack() as ctx:
        sb = lambda s, shape: ctx.enter_context(nc.sbuf_tensor(f"{name}_{s}", shape, F32))
        sem = lambda s: nc.alloc_semaphore(f"{name}_{s}")
        w1, b1t, w2, b2t = sb("w1", [D, E, H2 * 128]), sb("b1t", [128, E * H2]), sb("w2", [128, E * H2, D]), sb("b2t", [3 * E, D])
        bsb = lambda s, shape: ctx.enter_context(nc.sbuf_tensor(f"{name}_{s}", shape, BF16))
        b2p, low = bsb("b2p", [3 * E, 3, D]), bsb("low", [3 * E, D])
        b1r = sb("b1r", [E * H2, 128])
        sel = bsb("sel", [3 * E, E, 128])
        hs, hg = sb("hs", [128, 2, H2, CH]), sb("hg", [128, 2, H2, CH])
        psg = [ctx.enter_context(nc.psum_tensor(f"{name}_pg{i}", [128, CH], F32)) for i in range(2)]
        psh = [[ctx.enter_context(nc.psum_tensor(f"{name}_ph{i}{k}", [128, CH], F32)) for k in range(H2)] for i in range(2)]
        pso = [ctx.enter_context(nc.psum_tensor(f"{name}_po{i}", [128, CH], F32)) for i in range(2)]
        w_in, b_in, b2_split, b_ps, b_out, sel0, sel_ready, h_ps, h_out, hg_ready, out_done, o_ps, o_out = map(sem, (
            "w_in", "b_in", "b2_split", "b_ps", "b_out", "sel0", "sel_ready", "h_ps", "h_out", "hg_ready", "out_done", "o_ps", "o_out"))
        block = ctx.enter_context(nc.Block())

        def chunks(eng, chunk):
            chunk(0, 0)
            with eng.Fori(0, (NCH - 2) // 2) as i:
                chunk(2 * i + 1, 1)
                chunk(2 * i + 2, 0)
            chunk(NCH - 1, 1)

        @block.sync
        def _(sp):
            sp.dma_start(b1r[:], b1.rearrange("e (k p) -> (e k) p", p=128)).then_inc(b_in, 16)
            sp.dma_start(w1[:], W1.rearrange("e d h -> d e h")).then_inc(w_in, 16)
            sp.dma_start(w2[:], W2.rearrange("e (k p) d -> p (e k) d", p=128)).then_inc(w_in, 16)
            for i in range(3):
                sp.dma_start(b2t[i * E:(i + 1) * E, :], b2).then_inc(w_in, 16)

        @block.gpsimd
        def _(pool):
            pool.memset(sel[:], 0.0).then_inc(sel0, 1)
            for i in range(3):
                pool.wait_ge(sel0, i + 1)
                pool.affine_select(out=sel[:], in_=sel[:], compare_op=ALU.not_equal, fill=1.0, base=-i * E,
                                   pattern=[[-1, E], [0, 128]], channel_multiplier=1).then_inc(sel0, 1)
            pool.wait_ge(sel0, 4)
            pool.nop().then_inc(sel_ready, 1)

        @block.tensor
        def _(pe):
            pe.wait_ge(b_in, 16)
            pe.transpose(psg[0][:, 0:E * H2], b1r[:], g.ident[0:E * H2, 0:E * H2]).then_inc(b_ps, 1)
            pe.wait_ge(b_out, 1)
            pe.wait_ge(w_in, 80)
            pe.wait_ge(b2_split, 1)
            pe.wait_ge(sel_ready, 1)

            def hidden(c, e, s):
                if not (isinstance(c, int) and s < 2):
                    pe.wait_ge(h_out, s - 1)
                    pe.wait_ge(hg_ready, s - 1)
                for k in range(H2):
                    pe.matmul(psh[e % 2][k][:], w1[:, e, k * 128:(k + 1) * 128], chunk_view(g, c), start=True, stop=True)
                mm = pe.matmul(psg[e % 2][:], sel[:, e, :], chunk_cols(g.GT[0:3 * E, :], c), start=True, stop=True)
                mm.then_inc(h_ps, 1)

            def chunk(c, par):
                for e in range(E):
                    s = c * E + e
                    if e < E - 1:
                        hidden(c, e + 1, s + 1)
                    elif not (isinstance(c, int) and c == NCH - 1):
                        hidden(c + 1, 0, s + 1)
                    if e == 0 and not (isinstance(c, int) and c < 2):
                        pe.wait_ge(o_out, c)
                    pe.wait_ge(hg_ready, s + 1)
                    for k in range(H2):
                        mm = pe.matmul(pso[par][:], w2[:, e * H2 + k, :], hg[:, e % 2, k, :], start=(e == 0 and k == 0), stop=False)
                    mm.then_inc(out_done, 1)
                for i in range(3):
                    mm = pe.matmul(pso[par][:], b2p[:, i, :], chunk_cols(g.GT[0:3 * E, :], c), start=False, stop=(i == 2))
                mm.then_inc(o_ps, 1)

            hidden(0, 0, 0)
            chunks(pe, chunk)

        @block.scalar
        def _(act):
            act.wait_ge(b_ps, 1)
            act.activation(b1t[:], psg[0][:, 0:E * H2], ACT.Copy).then_inc(b_out, 1)
            act.drain()

            def chunk(c, par):
                for e in range(E):
                    s = c * E + e
                    act.wait_ge(h_ps, s + 1)
                    if not (isinstance(c, int) and s < 2):
                        act.wait_ge(hg_ready, s - 1)
                    for k in range(H2):
                        ins = act.activation(hs[:, e % 2, k, :], psh[e % 2][k][:], ACT.Gelu, bias=b1t[:, e * H2 + k:e * H2 + k + 1])
                    ins.then_inc(h_out, 1)
            chunks(act, chunk)

        @block.vector
        def _(dve):
            def add(c, par):
                dve.wait_ge(o_ps, c + 1)
                x = chunk_cols(g.XT, c)
                dve.tensor_tensor(x, x, pso[par][:], ALU.add).then_inc(o_out, 1)

            def chunk(c, par):
                for e in range(E):
                    s = c * E + e
                    dve.wait_ge(h_out, s + 1)
                    if not (isinstance(c, int) and s < 2):
                        dve.wait_ge(out_done, s - 1)
                    for k in range(H2):
                        ins = dve.tensor_tensor(hg[:, e % 2, k, :], hs[:, e % 2, k, :], psg[e % 2][:], ALU.mult)
                    ins.then_inc(hg_ready, 1)
                    if e == 1 and not (isinstance(c, int) and c == 0):
                        add(c - 1, 1 - par)
            dve.wait_ge(w_in, 80)
            split_parts(dve, b2t[:], [b2p[:, i, :] for i in range(3)], b2t[:], low[:])
            dve.nop().then_inc(b2_split, 1)
            dve.sem_inc(o_out, 1)
            chunks(dve, chunk)
            add(NCH - 1, 1)


def l2_gnn(nc, g):
    with nc.cleanup_on_exit(), ExitStack() as ctx:
        sb = lambda s, shape: ctx.enter_context(nc.sbuf_tensor(f"g2_{s}", shape, F32))
        sem = lambda s: nc.alloc_semaphore(f"g2_{s}")
        w, inter = sb("w", [D, D]), sb("inter", [128, 2, CHG, SLOT])
        P, key, hide, st = sb("P", [128, PAIRS, N]), sb("key", [128, PAIRS, N]), sb("hide", [128, PAIRS, N]), sb("st", [128, PAIRS])
        w_in, key_in, i_ps, i_out, s_ps, s_out, shifted, expd = map(sem, (
            "w_in", "key_in", "i_ps", "i_out", "s_ps", "s_out", "shifted", "expd"))
        with ExitStack() as first:
            psi = [first.enter_context(nc.psum_tensor(f"g2_i{i}", [128, CHG, SLOT], F32)) for i in range(2)]
            pss = [first.enter_context(nc.psum_tensor(f"g2_s{i}", [128, CHP, N], F32)) for i in range(2)]
            block = first.enter_context(nc.Block())

            @block.sync
            def _(sp):
                sp.dma_start(w[:], g.L2_gnn_W).then_inc(w_in, 16)
                masks = g.nodemask.rearrange("(q j) m -> j q m", j=2)
                for j in range(2):
                    sp.dma_start(key[SLOT * j:SLOT * (j + 1), :, :], masks[j][None, :, :].broadcast_to([SLOT, PAIRS, N])).then_inc(key_in, 16)

            @block.tensor
            def _(pe):
                def scores(c):
                    pe.wait_ge(i_out, c + 1)
                    if c >= 2:
                        pe.wait_ge(s_out, c - 1)
                    for q in range(CHP):
                        for j in range(2):
                            mm = pe.matmul(pss[c % 2][SLOT * j:SLOT * (j + 1), q, :], inter[:, c % 2, 2 * q + j, :],
                                           g.XNP[:, c * CHG + 2 * q + j, 0:N], start=True, stop=True)
                    mm.then_inc(s_ps, 1)

                pe.wait_ge(w_in, 16)
                for c in range(NCH + 1):
                    if c < NCH:
                        if c >= 2:
                            pe.wait_ge(i_out, c - 1)
                        pe.matmul(psi[c % 2][:].rearrange("p b n -> p (b n)"), w[:],
                                  g.XNP[:, c * CHG:(c + 1) * CHG, :].rearrange("p b n -> p (b n)"), start=True, stop=True).then_inc(i_ps, 1)
                    if c >= 1:
                        scores(c - 1)

            @block.scalar
            def _(act):
                for c in range(NCH):
                    act.wait_ge(i_ps, c + 1)
                    if c >= 2:
                        act.wait_ge(s_ps, c - 1)
                    act.activation(inter[:, c % 2], psi[c % 2][:], ACT.Copy).then_inc(i_out, 1)
                act.wait_ge(shifted, 1)
                act.activation(P[:], P[:], ACT.Exp).then_inc(expd, 1)

            @block.vector
            def _(dve):
                dve.wait_ge(key_in, 32)
                dve.tensor_scalar(key[:], key[:], 0.0, None, ALU.not_equal)
                dve.drain()
                dve.tensor_scalar(hide[:], key[:], 1.0, 1e30, ALU.subtract, ALU.mult)
                for c in range(NCH):
                    dve.wait_ge(s_ps, c + 1)
                    o = slice(c * CHP, (c + 1) * CHP)
                    dve.tensor_tensor(P[:, o, :], pss[c % 2][:], g.adjG[:, o, :], ALU.mult).then_inc(s_out, 1)
                dve.drain()
                dve.tensor_tensor(P[:], P[:], key[:], ALU.mult)
                dve.drain()
                dve.tensor_tensor(P[:], P[:], hide[:], ALU.add)
                dve.drain()
                dve.tensor_reduce(st[:], P[:], AX.X, ALU.max)
                dve.drain()
                dve.tensor_tensor(P[:], P[:], st[:, :, None].broadcast_to([128, PAIRS, N]), ALU.subtract).then_inc(shifted, 1)
                dve.wait_ge(expd, 1)
                dve.tensor_reduce(st[:], P[:], AX.X, ALU.add)
                dve.drain()
                dve.reciprocal(st[:], st[:])
                dve.drain()
                dve.tensor_tensor(P[:], P[:], st[:, :, None].broadcast_to([128, PAIRS, N]), ALU.mult)

        PT = sb("PT", [128, 2, CHP, N])
        pst = [[ctx.enter_context(nc.psum_tensor(f"g2_t{i}{j}", [128, CHP, N], F32)) for j in range(2)] for i in range(2)]
        psz = [[ctx.enter_context(nc.psum_tensor(f"g2_z{i}{j}", [128, CHP, N], F32)) for j in range(2)] for i in range(2)]
        t_ps, t_out, z_ps, z_out = map(sem, ("t_ps", "t_out", "z_ps", "z_out"))
        block = ctx.enter_context(nc.Block())

        @block.tensor
        def _(pe):
            for c in range(NCH + 1):
                if c < NCH:
                    if c >= 2:
                        pe.wait_ge(t_out, c - 1)
                    for q in range(CHP):
                        for j in range(2):
                            mm = pe.matmul(pst[c % 2][j][rows(j), q, :], P[rows(j), c * CHP + q, :], g.ident[rows(j), rows(j)],
                                           start=True, stop=True)
                    mm.then_inc(t_ps, 1)
                if c >= 1:
                    k = c - 1
                    pe.wait_ge(t_out, k + 1)
                    if k >= 2:
                        pe.wait_ge(z_out, k - 1)
                    for q in range(CHP):
                        for j in range(2):
                            mm = pe.matmul(psz[k % 2][j][:, q, :], g.XNG[rows(j), k * CHP + q, :], PT[rows(j), k % 2, q, :],
                                           start=True, stop=True)
                    mm.then_inc(z_ps, 1)

        @block.scalar
        def _(act):
            for c in range(NCH):
                act.wait_ge(t_ps, c + 1)
                if c >= 2:
                    act.wait_ge(z_ps, c - 1)
                for j in range(2):
                    ins = act.activation(PT[rows(j), c % 2], pst[c % 2][j][rows(j)], ACT.Copy)
                ins.then_inc(t_out, 1)

        @block.vector
        def _(dve):
            for c in range(NCH):
                dve.wait_ge(z_ps, c + 1)
                x = g.XT[:, c * CH:(c + 1) * CH].rearrange("p (q j n) -> p q j n", j=2, n=N)
                for j in range(2):
                    ins = dve.tensor_tensor(x[:, :, j, :], x[:, :, j, :], psz[c % 2][j][:], ALU.add)
                ins.then_inc(z_out, 1)


def l3_gnn(nc, g):
    HD = 8
    NEG = -1000000000.0
    with nc.cleanup_on_exit(), ExitStack() as ctx:
        sb = lambda s, shape: ctx.enter_context(nc.sbuf_tensor(f"g3_{s}", shape, F32))
        sem = lambda s: nc.alloc_semaphore(f"g3_{s}")
        wc, wq, wk = sb("wc", [D, HD, D]), sb("wq", [D, HD]), sb("wk", [D, HD, SLOT])
        obias, Q, neg = sb("obias", [D, 1]), sb("Q", [128, PAIRS, HD]), sb("neg", [128, PAIRS, N])
        with ExitStack() as first:
            fsb = lambda s, shape: first.enter_context(nc.sbuf_tensor(f"g3_{s}", shape, F32))
            fc, fcT, fp = fsb("fc", [D, HD, D]), fsb("fcT", [D, HD, D]), fsb("fp", [D, HD, D])
            qk, krep, qkrep, fcb, fcbT = fsb("qk", [D, 2]), fsb("krep", [D, SLOT]), fsb("qkrep", [D, 128]), fsb("fcb", [HD, D]), fsb("fcbT", [D, HD])
            qkb, fpb, cst = fsb("qkb", [128, 2]), fsb("fpb", [D, 1]), fsb("cst", [128, HD])
            ps = [first.enter_context(nc.psum_tensor(f"g3_p{i}", [128, 4, 128], F32)) for i in range(2)]
            pq = first.enter_context(nc.psum_tensor("g3_pq", [128, HD], F32))
            pk = first.enter_context(nc.psum_tensor("g3_pk", [128, HD, SLOT], F32))
            pb = first.enter_context(nc.psum_tensor("g3_pb", [128, HD], F32))
            po = first.enter_context(nc.psum_tensor("g3_po", [128, 1], F32))
            pQ = first.enter_context(nc.psum_tensor("g3_pQ", [128, PAIRS, HD], F32))
            w_in, rep, t_ps, t_out, c_ps, s_ps, folded, q_ps = map(sem, ("w_in", "rep", "t_ps", "t_out", "c_ps", "s_ps", "folded", "q_ps"))
            block = first.enter_context(nc.Block())
            LOADS = 16 * 8

            @block.sync
            def _(sp):
                col = lambda t: t.rearrange("(d a) -> d a", a=1)
                sp.dma_start(fc[:], g.L3_gnn_fc_w.rearrange("f (h d) -> f h d", h=HD)).then_inc(w_in, 16)
                sp.dma_start(fp[:], g.L3_gnn_fp_w.rearrange("(h d) o -> d h o", h=HD)).then_inc(w_in, 16)
                sp.dma_start(fcb[:], g.L3_gnn_fc_b.rearrange("(h d) -> h d", h=HD)).then_inc(w_in, 16)
                sp.dma_start(qk[:, 0:1], g.L3_gnn_q_w, allow_slow_non_contiguous=True).then_inc(w_in, 16)
                sp.dma_start(qk[:, 1:2], g.L3_gnn_k_w, allow_slow_non_contiguous=True).then_inc(w_in, 16)
                sp.dma_start(qkb[:, 0:1], g.L3_gnn_q_b[None, :].broadcast_to([128, 1]), allow_slow_non_contiguous=True).then_inc(w_in, 16)
                sp.dma_start(qkb[:, 1:2], g.L3_gnn_k_b[None, :].broadcast_to([128, 1]), allow_slow_non_contiguous=True).then_inc(w_in, 16)
                sp.dma_start(fpb[:], col(g.L3_gnn_fp_b), allow_slow_non_contiguous=True).then_inc(w_in, 16)

            @block.vector
            def _(dve):
                dve.wait_ge(w_in, LOADS)
                dve.tensor_scalar(krep[:], g.ones[:, 0:SLOT], qk[:, 1:2], None, ALU.mult)
                dve.tensor_scalar(qkrep[:], g.ones[:], qk[:, 0:1], qk[:, 1:2], ALU.mult, ALU.add).then_inc(rep, 1)
                dve.tensor_scalar(neg[:], g.adjG[:], -1.0, 1.0, ALU.mult, ALU.add)
                dve.drain()
                dve.tensor_scalar(neg[:], neg[:], NEG, None, ALU.mult)
                for i in range(2):
                    dve.wait_ge(t_ps, i + 1)
                    dve.tensor_copy(fcT[:, 4 * i:4 * i + 4, :], ps[i][:]).then_inc(t_out, 1)
                dve.wait_ge(t_ps, 3)
                dve.tensor_copy(fcbT[:], pb[:]).then_inc(t_out, 1)
                for i in range(2):
                    dve.wait_ge(c_ps, i + 1)
                    dve.tensor_copy(wc[:, 4 * i:4 * i + 4, :], ps[i][:])
                dve.wait_ge(s_ps, 1)
                dve.tensor_copy(wq[:], pq[:])
                dve.tensor_copy(wk[:], pk[:])
                dve.tensor_scalar(cst[:], pb[:], qkb[:, 0:1], qkb[:, 1:2], ALU.add, ALU.add)
                dve.tensor_scalar(obias[:], po[:], fpb[:, 0:1], None, ALU.add).then_inc(folded, 1)
                dve.wait_ge(q_ps, 1)
                dve.drain()
                dve.tensor_tensor(Q[:], pQ[:], cst[:, None, :].broadcast_to([128, PAIRS, HD]), ALU.add)

            @block.tensor
            def _(pe):
                pe.wait_ge(w_in, LOADS)
                for i in range(2):
                    for k in range(4):
                        mm = pe.transpose(ps[i][:, k, :], fc[:, 4 * i + k, :], g.ident[:])
                    mm.then_inc(t_ps, 1)
                pe.transpose(pb[:], fcb[:], g.ident[0:HD, 0:HD]).then_inc(t_ps, 1)
                pe.wait_ge(rep, 1)
                for i in range(2):
                    pe.wait_ge(t_out, i + 1)
                    for k in range(4):
                        mm = pe.matmul(ps[i][:, k, :], fcT[:, 4 * i + k, :], fp[:, 4 * i + k, :], start=True, stop=True)
                    mm.then_inc(c_ps, 1)
                for h in range(HD):
                    pe.matmul(pq[:, h:h + 1], fcT[:, h, :], qk[:, 0:1], start=True, stop=True)
                    pe.matmul(pk[:, h, :], fcT[:, h, :], krep[:], start=True, stop=True)
                pe.wait_ge(t_out, 3)
                pe.matmul(pb[:], qkrep[:], fcbT[:], start=True, stop=True)
                for h in range(HD):
                    mm = pe.matmul(po[:], fp[:, h, :], fcbT[:, h:h + 1], start=(h == 0), stop=(h == HD - 1))
                mm.then_inc(s_ps, 1)
                pe.wait_ge(folded, 1)
                for q in range(PAIRS):
                    mm = pe.matmul(pQ[:, q, :], g.XNP[:, 2 * q:2 * q + 2, :].rearrange("p b n -> p (b n)"), wq[:], start=True, stop=True)
                mm.then_inc(q_ps, 1)

        P, st = sb("P", [128, 2, HD, CHP, N]), sb("st", [128, HD, CHP])
        PT, Z, so = sb("PT", [128, 2, HD, N]), sb("Z", [128, 2, HD, CHG, N]), sb("so", [128, 2, CH])
        GR = [range(0, 3), range(3, 6), range(6, 8)]
        psk = [ctx.enter_context(nc.psum_tensor(f"g3_k{i}", [128, 3, CHP, N], F32)) for i in range(3)]
        pst = [ctx.enter_context(nc.psum_tensor(f"g3_t{j}", [128, HD, N], F32)) for j in range(2)]
        psz = [ctx.enter_context(nc.psum_tensor(f"g3_z{j}", [128, HD, N], F32)) for j in range(2)]
        psy = ctx.enter_context(nc.psum_tensor("g3_y", [128, CH], F32))
        k_ps, k_out, shifted, expd, attn, pt_ps, pt_out, z_ps, z_out, y_ps, y_pre, y_sig = map(sem, (
            "k_ps", "k_out", "shifted", "expd", "attn", "pt_ps", "pt_out", "z_ps", "z_out", "y_ps", "y_pre", "y_sig"))
        block = ctx.enter_context(nc.Block())

        @block.tensor
        def _(pe):
            def keys(c):
                if c >= 1:
                    pe.wait_ge(k_out, c)
                for i, hs in enumerate(GR):
                    for h in hs:
                        for j in range(2):
                            rhs = g.XNP[:, c * CHG + j:c * CHG + CHG:2, 0:N]
                            mm = pe.matmul(psk[i][SLOT * j:SLOT * (j + 1), h - hs[0], :, :], wk[:, h, :], rhs, start=True, stop=True)
                mm.then_inc(k_ps, 1)

            def product(n):
                pe.wait_ge(pt_out, n + 1)
                if n >= 1:
                    pe.wait_ge(z_out, n)
                for j in range(2):
                    mm = pe.matmul(psz[j][:].rearrange("p h n -> p (h n)"), g.XNG[rows(j), n, :],
                                   PT[rows(j), n % 2].rearrange("p h n -> p (h n)"), start=True, stop=True)
                mm.then_inc(z_ps, 1)

            def project(c):
                pe.wait_ge(z_out, CHP * (c + 1))
                if c >= 1:
                    pe.wait_ge(y_pre, c)
                for h in range(HD):
                    mm = pe.matmul(psy[:], wc[:, h, :], Z[:, c % 2, h].rearrange("p b n -> p (b n)"), start=(h == 0), stop=(h == HD - 1))
                mm.then_inc(y_ps, 1)

            keys(0)
            for c in range(NCH):
                if c < NCH - 1:
                    keys(c + 1)
                pe.wait_ge(attn, c + 1)
                for q in range(CHP):
                    n = c * CHP + q
                    if n >= 1:
                        pe.wait_ge(pt_out, n)
                    for j in range(2):
                        for h in range(HD):
                            mm = pe.matmul(pst[j][rows(j), h, :], P[rows(j), c % 2, h, q, :], g.ident[rows(j), rows(j)], start=True, stop=True)
                    mm.then_inc(pt_ps, 1)
                    if n >= 1:
                        product(n - 1)
                    if q == 1 and c >= 1:
                        project(c - 1)
            product(PAIRS - 1)
            project(NCH - 1)

        @block.scalar
        def _(act):
            def z_evac(n):
                act.wait_ge(z_ps, n + 1)
                c, q = n // CHP, n % CHP
                if q == 0 and c >= 2:
                    act.wait_ge(y_ps, c - 1)
                for j in range(2):
                    ins = act.activation(Z[:, c % 2, :, 2 * q + j, :], psz[j][:], ACT.Copy)
                ins.then_inc(z_out, 1)

            def sig(c):
                act.wait_ge(y_pre, c + 1)
                act.activation(so[:, c % 2, :], so[:, c % 2, :], ACT.Exp, scale=-1.0).then_inc(y_sig, 1)

            def exps(c):
                act.wait_ge(shifted, c + 1)
                act.activation(P[:, c % 2], P[:, c % 2], ACT.Exp).then_inc(expd, 1)

            exps(0)
            for c in range(NCH):
                for q in range(CHP):
                    if q == 2 and c < NCH - 1:
                        exps(c + 1)
                    n = c * CHP + q
                    act.wait_ge(pt_ps, n + 1)
                    if n >= 2:
                        act.wait_ge(z_ps, n - 1)
                    for j in range(2):
                        ins = act.activation(PT[rows(j), n % 2], pst[j][rows(j)], ACT.Copy)
                    ins.then_inc(pt_out, 1)
                    if n >= 1:
                        z_evac(n - 1)
                    if q == 3 and c >= 1:
                        sig(c - 1)
            z_evac(PAIRS - 1)
            sig(NCH - 1)

        @block.vector
        def _(dve):
            def softmax(c):
                p = P[:, c % 2]
                o = slice(c * CHP, (c + 1) * CHP)
                dve.wait_ge(k_ps, c + 1)
                if c >= 2:
                    dve.wait_ge(pt_ps, CHP * (c - 1))
                for i, hs in enumerate(GR):
                    for h in hs:
                        ins = dve.tensor_tensor(p[:, h], psk[i][:, h - hs[0]], Q[:, o, h:h + 1].broadcast_to([128, CHP, N]), ALU.add)
                ins.then_inc(k_out, 1)
                dve.drain()
                m = neg[:, o, :].rearrange("p q m -> p (q m)")[:, None, :].broadcast_to([128, HD, CHP * N])
                p2 = p.rearrange("p h q m -> p h (q m)")
                dve.tensor_tensor(p2, p2, m, ALU.add)
                dve.drain()
                p1 = p.rearrange("p h q m -> p (h q m)")
                dve.scalar_tensor_tensor(p1, p1, 0.01, p1, ALU.mult, ALU.max)
                dve.drain()
                dve.tensor_reduce(st[:], p, AX.X, ALU.max)
                dve.drain()
                ph = p.rearrange("p h q m -> p (h q) m")
                sb_ = st[:].rearrange("p h q -> p (h q)")[:, :, None].broadcast_to([128, HD * CHP, N])
                dve.tensor_tensor(ph, ph, sb_, ALU.subtract).then_inc(shifted, 1)
                dve.wait_ge(expd, c + 1)
                dve.tensor_reduce(st[:], p, AX.X, ALU.add)
                dve.drain()
                dve.reciprocal(st[:], st[:])
                dve.drain()
                dve.tensor_tensor(ph, ph, sb_, ALU.mult).then_inc(attn, 1)

            def pre(c):
                dve.wait_ge(y_ps, c + 1)
                s3 = so[:, c % 2, :].rearrange("p (b n) -> p b n", n=N)
                dve.scalar_tensor_tensor(s3, psy[:].rearrange("p (b n) -> p b n", n=N), obias[:, 0:1],
                                         chunk_view(g, c), ALU.add, ALU.add).then_inc(y_pre, 1)

            def post(c):
                dve.wait_ge(y_sig, c + 1)
                s = so[:, c % 2, :]
                dve.tensor_scalar(s, s, 1.0, None, ALU.add)
                dve.drain()
                dve.reciprocal(s, s)
                dve.drain()
                x = g.XT[:, c * CH:(c + 1) * CH]
                dve.tensor_tensor(x, x, s, ALU.add)
                dve.drain()

            softmax(0)
            for c in range(NCH):
                if c < NCH - 1:
                    softmax(c + 1)
                if c >= 1:
                    pre(c - 1)
                    if c >= 2:
                        post(c - 2)
            pre(NCH - 1)
            post(NCH - 2)
            post(NCH - 1)


HEADS, EXP = 4, 4
HE = HEADS * EXP
V = HEADS + HE
EDGES = 524288
EC = EDGES // 128
VALID = 1 << 30
GRP = 8


def edge_keys(nc, g):
    with nc.cleanup_on_exit(), ExitStack() as ctx:
        sb = lambda s, shape, dt=F32: ctx.enter_context(nc.sbuf_tensor(f"ek_{s}", shape, dt))
        sem = lambda s: nc.alloc_semaphore(f"ek_{s}")
        lent = g.XNG[:].rearrange("p q d -> p (q d)").bitcast(I32)
        src, dst = lent[:, 0:EC], lent[:, EC:2 * EC]
        lent = g.XNP[:].rearrange("p b n -> p (b n)")
        keep, past = lent[:, 0:EC], lent[:, EC:2 * EC]
        mask = sb("mask", [128, EC], I32)
        HG = 16
        SEG, LO, HI = 128, 64, T // 64
        SEGS = EC // SEG
        KC = SEGS * GRP
        K, ki = sb("K", [128, KC]), sb("ki", [128, 3, KC], I32)
        dl, dh = sb("dl", [128, KC], BF16), sb("dh", [128, KC], BF16)
        iob = sb("iob", [128, 128], BF16)
        OL, OH, spelled = sb("OL", [128, 2, LO, HG], BF16), sb("OH", [128, 2, HI, HG], BF16), sb("spelled", [128, HI, HG], BF16)
        zero = sb("zero", [128, 128], BF16)
        seg, cnt, top = sb("seg", [128, SEGS]), sb("cnt", [128, 2]), sb("top", [1, 2])
        pc = ctx.enter_context(nc.psum_tensor("ek_pc", [1, 2, 128], F32))
        ph = ctx.enter_context(nc.psum_tensor("ek_ph", [LO, HI], F32))
        e_in, counted, c_ps, hot, sized, h_ps, io, zeroed = map(sem, ("e_in", "counted", "c_ps", "hot", "sized", "h_ps", "io", "zeroed"))
        block = ctx.enter_context(nc.Block())

        @block.sync
        def _(sp):
            sp.dma_start(src, g.L2_ffn_edge_index[0].rearrange("(p c) -> p c", p=128)).then_inc(e_in, 16)
            sp.dma_start(dst, g.L2_ffn_edge_index[1].rearrange("(p c) -> p c", p=128)).then_inc(e_in, 16)

        @block.gpsimd
        def _(pool):
            pool.iota(iob[:], pattern=[[1, 128]], base=0, channel_multiplier=0, allow_small_or_imprecise_dtypes=True)
            pool.iota(g.iof[:], pattern=[[1, 128]], base=0, channel_multiplier=0, allow_small_or_imprecise_dtypes=True).then_inc(io, 1)
            pool.memset(g.ones[:], 1.0)
            pool.memset(zero[:], 0.0).then_inc(zeroed, 1)

        @block.vector
        def _(dve):
            dve.wait_ge(e_in, 32)
            w = g.work[:].bitcast(I32)
            dve.tensor_scalar(w, dst, 13, VALID, ALU.logical_shift_left, ALU.bitwise_or)
            dve.tensor_scalar(past, src, float(T - 1), None, ALU.is_ge)
            dve.tensor_scalar(keep, dst, float(T), None, ALU.is_lt)
            dve.drain()
            dve.tensor_tensor(w, w, src, ALU.bitwise_or)
            dve.tensor_tensor(past, past, keep, ALU.mult)
            dve.drain()
            dve.tensor_tensor(keep, keep, past, ALU.subtract)
            dve.tensor_reduce(seg[:], past.rearrange("p (s c) -> p s c", c=SEG), AX.X, ALU.add)
            dve.drain()
            dve.tensor_copy(mask[:], keep)
            dve.tensor_reduce(cnt[:, 0:1], keep, AX.X, ALU.add)
            dve.tensor_reduce(cnt[:, 1:2], seg[:], AX.X, ALU.max)
            dve.drain()
            dve.nop().then_inc(counted, 1)
            dve.tensor_scalar(mask[:], mask[:], 31, 31, ALU.logical_shift_left, ALU.arith_shift_right)
            dve.tensor_scalar(keep, dst, 1.0, float(SEG), ALU.add, ALU.mult)
            dve.wait_ge(io, 1)
            dve.tensor_copy(spelled[:], iob[:, 0:HI, None].broadcast_to([128, HI, HG]))
            dve.drain()
            dve.tensor_tensor(w, w, mask[:], ALU.bitwise_and)
            k3 = keep.rearrange("p (s c) -> p s c", c=SEG)
            dve.tensor_tensor(k3, k3, g.iof[:, None, :].broadcast_to([128, SEGS, SEG]), ALU.add)
            dve.drain()
            dve.tensor_tensor(keep, keep, past, ALU.mult)
            dve.wait_ge(c_ps, 1)
            dve.tensor_reduce(top[:], pc[:], AX.X, ALU.max)
            dve.drain()
            dve.tensor_scalar(g.turns[:, 0:1], top[:, 0:1], float(2 * GRP - 1), float(2 * GRP), ALU.add, ALU.max)
            dve.tensor_scalar(g.turns[:, 1:2], top[:, 1:2], float(GRP - 1), float(GRP), ALU.add, ALU.max)
            dve.drain()
            dve.tensor_scalar(g.turns[:, 0:1], g.turns[:, 0:1], 4, None, ALU.logical_shift_right)
            dve.tensor_scalar(g.turns[:, 1:2], g.turns[:, 1:2], 3, None, ALU.logical_shift_right)
            dve.drain()
            dve.nop().then_inc(sized, 1)
            dve.wait_ge(sized, 1)
            n = dve.value_load(g.turns[0:1, 1:2], min_val=1, max_val=SEG // GRP)
            with dve.Fori(0, n) as r:
                for i in range(SEGS):
                    dve.max(K[:, i * GRP:(i + 1) * GRP], keep[:, i * SEG:(i + 1) * SEG])
                dve.drain()
                for i in range(SEGS):
                    s = keep[:, i * SEG:(i + 1) * SEG]
                    dve.match_replace(s, K[:, i * GRP:(i + 1) * GRP], s, 0.0)
                dve.tensor_copy(ki[:, 0], K[:])
                dve.drain()
                dve.tensor_scalar(ki[:, 0], ki[:, 0], 7, None, ALU.logical_shift_right)
                dve.drain()
                dve.tensor_scalar(ki[:, 0], ki[:, 0], 1.0, None, ALU.subtract)
                dve.drain()
                dve.tensor_scalar(ki[:, 1], ki[:, 0], LO - 1, None, ALU.bitwise_and)
                dve.tensor_scalar(ki[:, 2], ki[:, 0], 6, None, ALU.arith_shift_right)
                dve.drain()
                dve.tensor_copy(dl[:], ki[:, 1])
                dve.tensor_copy(dh[:], ki[:, 2])
                dve.drain()
                for c in range(KC // HG):
                    b = c % 2
                    cols = slice(c * HG, (c + 1) * HG)
                    dve.wait_ge(h_ps, r * (KC // HG) + c + 1)
                    dve.tensor_tensor(OL[:, b], spelled[:, 0:LO], dl[:, None, cols].broadcast_to([128, LO, HG]), ALU.is_equal)
                    dve.tensor_tensor(OH[:, b], spelled[:], dh[:, None, cols].broadcast_to([128, HI, HG]), ALU.is_equal).then_inc(hot, 1)
            dve.wait_ge(h_ps, n * (KC // HG) + 3)
            for i in range(2):
                dve.tensor_copy(g.cntB[i * LO:(i + 1) * LO, :], ph[:].rearrange("p (t i) -> p i t", i=2)[:, i])
            dve.memset(g.XNP[:], 0.0)

        @block.tensor
        def _(pe):
            pe.wait_ge(counted, 1)
            for i in range(2):
                mm = pe.transpose(pc[:, i, :], cnt[:, i:i + 1], g.ident[:])
            mm.then_inc(c_ps, 1)
            pe.wait_ge(zeroed, 1)
            pe.wait_ge(sized, 1)
            pe.matmul(ph[:], zero[:, 0:LO], zero[:, 0:HI], start=True, stop=False, skip_group_check=True).then_inc(h_ps, 2)
            n = pe.value_load(g.turns[0:1, 1:2], min_val=1, max_val=SEG // GRP)
            with pe.Fori(0, n) as r:
                for c in range(KC // HG):
                    pe.wait_ge(hot, r * (KC // HG) + c + 1)
                    for k in range(HG):
                        mm = pe.matmul(ph[:], OL[:, c % 2, :, k], OH[:, c % 2, :, k], start=False, stop=False, skip_group_check=True)
                    mm.then_inc(h_ps, 1)
            pe.matmul(ph[:], zero[:, 0:LO], zero[:, 0:HI], start=False, stop=True, skip_group_check=True).then_inc(h_ps, 1)


def leaky(dve, t, slope):
    dve.scalar_tensor_tensor(t, t, slope, t, ALU.mult, ALU.max)
    dve.drain()


def edge_router(nc, g):
    with nc.cleanup_on_exit(), ExitStack() as ctx:
        sb = lambda s, shape, dt=F32: ctx.enter_context(nc.sbuf_tensor(f"er_{s}", shape, dt))
        sem = lambda s: nc.alloc_semaphore(f"er_{s}")
        TS, TD, TM = sb("TS", [128, V, TT]), sb("TD", [128, HEADS, TT]), sb("TM", [128, HEADS, TT])
        amax = sb("amax", [128, HEADS])
        last = sb("last", [128, V])
        att0 = sb("att0", [128, HE])
        with ExitStack() as first:
            fsb = lambda s, shape: first.enter_context(nc.sbuf_tensor(f"er_{s}", shape, F32))
            wg, HT = fsb("wg", [D, HE]), fsb("HT", [HE, T])
            H, pr, att = fsb("H", [128, TT, HE]), fsb("pr", [128, TT, HE]), fsb("att", [128, 2, HE])
            mx, m4, dg, sel = fsb("mx", [128, HEADS]), fsb("m4", [HEADS, 1]), fsb("dg", [HEADS, HEADS]), fsb("sel", [128, 128])
            psl = [first.enter_context(nc.psum_tensor(f"er_l{i}", [HE, CH], F32)) for i in range(2)]
            psh = [first.enter_context(nc.psum_tensor(f"er_h{i}", [128, TT // 2, HE], F32)) for i in range(2)]
            psm = first.enter_context(nc.psum_tensor("er_m", [HEADS, 128], F32))
            psa = first.enter_context(nc.psum_tensor("er_a", [128, HEADS], F32))
            psv = first.enter_context(nc.psum_tensor("er_v", [128, V], F32))
            w_in, l_ps, l_out, h_ps, mxd, m_ps, dgd, a_ps, selr = map(sem, ("w_in", "l_ps", "l_out", "h_ps", "mxd", "m_ps", "dgd", "a_ps", "selr"))
            block = first.enter_context(nc.Block())

            @block.sync
            def _(sp):
                sp.dma_start(wg[:], g.L2_ffn_W_gat).then_inc(w_in, 16)
                for i, a in enumerate((g.L2_ffn_att_src, g.L2_ffn_att_dst)):
                    sp.dma_start(att[:, i, :], a.rearrange("h e -> (h e)")[None, :].broadcast_to([128, HE])).then_inc(w_in, 16)

            @block.gpsimd
            def _(pool):
                pool.affine_select(out=sel[:], in_=g.ones[:], compare_op=ALU.is_ge, fill=0.0, base=-127,
                                   pattern=[[0, 128]], channel_multiplier=1).then_inc(selr, 1)

            @block.tensor
            def _(pe):
                pe.wait_ge(w_in, 48)
                for c in range(NCH):
                    if c >= 2:
                        pe.wait_ge(l_out, c - 1)
                    pe.matmul(psl[c % 2][:], wg[:], chunk_view(g, c), start=True, stop=True).then_inc(l_ps, 1)
                pe.wait_ge(l_out, NCH)
                for t in range(TT):
                    mm = pe.transpose(psh[t // 20][:, t % 20, :], HT[:, t * 128:(t + 1) * 128], g.ident[0:HE, 0:HE])
                mm.then_inc(h_ps, 1)
                pe.wait_ge(mxd, 1)
                pe.transpose(psm[:], mx[:], g.ident[:]).then_inc(m_ps, 1)
                pe.wait_ge(dgd, 1)
                pe.wait_ge(selr, 1)
                pe.matmul(psv[:], sel[:], TS[:, :, TT - 1], start=True, stop=True)
                pe.matmul(psa[:], g.ones[0:HEADS, :], dg[:], start=True, stop=True).then_inc(a_ps, 1)

            @block.scalar
            def _(act):
                for c in range(NCH):
                    act.wait_ge(l_ps, c + 1)
                    act.activation(HT[:, c * CH:(c + 1) * CH], psl[c % 2][:], ACT.Copy).then_inc(l_out, 1)

            @block.vector
            def _(dve):
                dve.wait_ge(h_ps, 1)
                dve.tensor_copy(att0[:], att[:, 0, :])
                for i in range(2):
                    dve.tensor_copy(H[:, i * 20:(i + 1) * 20, :], psh[i][:])
                dve.drain()
                dve.tensor_copy(TS[:, HEADS:V, :].rearrange("p v t -> p t v"), H[:])
                for i, o in enumerate((TS[:, 0:HEADS, :], TD[:])):
                    dve.tensor_tensor(pr[:], H[:], att[:, i, None, :].broadcast_to([128, TT, HE]), ALU.mult)
                    dve.drain()
                    dve.tensor_reduce(o.rearrange("p h t -> p t h"), pr[:].rearrange("p t (h e) -> p t h e", h=HEADS), AX.X, ALU.add)
                    dve.drain()
                dve.tensor_reduce(mx[:], TS[:, 0:HEADS, :], AX.X, ALU.max).then_inc(mxd, 1)
                dve.wait_ge(m_ps, 1)
                dve.tensor_reduce(m4[:], psm[:], AX.X, ALU.max)
                dve.drain()
                dve.tensor_scalar(dg[:], g.ident[0:HEADS, 0:HEADS], m4[:, 0:1], None, ALU.mult).then_inc(dgd, 1)
                dve.wait_ge(a_ps, 1)
                dve.tensor_copy(amax[:], psa[:])
                dve.tensor_copy(last[:], psv[:])
                dve.drain()
                dve.tensor_tensor(TM[:], TD[:], amax[:, :, None].broadcast_to([128, HEADS, TT]), ALU.add)
                dve.drain()
                leaky(dve, TM[:], 0.2)

        k8, ki = sb("k8", [128, GRP]), sb("ki", [128, 4, GRP], I32)
        idx = sb("idx", [128, 4, GRP])
        OS, OD = sb("OS", [128, GRP, 128], BF16), sb("OD", [128, 2, GRP, 128])
        TP, low = sb("TP", [128, 3, V, TT], BF16), sb("low", [128, V, TT], BF16)
        identb = sb("identb", [128, 128], BF16)
        M = sb("M", [128, 2, GRP, 2, TT])
        OT = sb("OT", [128, 2, 2, 128], BF16)
        HALF, XBUF = GRP // 2, 4
        lent = g.XNG[:].rearrange("p q d -> p (q d)")
        SEL = lent[:, 0:HALF * V * TT].rearrange("p (u v t) -> p u v t", u=HALF, v=V)
        X = lent[:, HALF * V * TT:(HALF + XBUF) * V * TT].rearrange("p (u v t) -> p u v t", u=XBUF, v=V)
        VV, VW = sb("VV", [128, GRP, V]), sb("VW", [128, GRP, V])
        VA, SC, S4 = sb("VA", [128, GRP, HE]), sb("SC", [128, GRP, 2, HEADS]), sb("S4", [128, GRP, HEADS])
        zero = sb("zero", [128, 128])
        A = sb("A", [128, V, TT])
        VH = V // 2
        VB = 12
        pst = [ctx.enter_context(nc.psum_tensor(f"er_t{i}", [128, 2, 128], F32)) for i in range(2)]
        psg = [[ctx.enter_context(nc.psum_tensor(f"er_g{i}{j}", [128, n, TT], F32)) for j, n in enumerate((VB, V - VB))] for i in range(2)]
        acc = [ctx.enter_context(nc.psum_tensor(f"er_c{i}", [128, VH, TT], F32)) for i in range(2)]
        hot, picked, t_ps, t_out, g_ps, scored, expd, weighted, x_ready, x_used, closed = map(sem, (
            "hot", "picked", "t_ps", "t_out", "g_ps", "scored", "expd", "weighted", "x_ready", "x_used", "closed"))

        def loop(eng, turn, last):
            n = eng.value_load(g.turns[0:1, 0:1], min_val=1, max_val=EC // GRP // 2)
            with eng.Fori(0, n) as r:
                turn(2 * r, 0)
                turn(2 * r + 1, 1)
            last(2 * n)

        with nc.Block() as block:
            @block.vector
            def _(dve):
                dve.memset(VV[:], 0.0)
                dve.memset(M[:, 1], 0.0)
                dve.memset(OD[:, 1], 0.0)
                dve.memset(zero[:], 0.0)
                dve.tensor_copy(identb[:], g.ident[:])
                rest = SEL[:, 0]
                dve.tensor_copy(rest[:, 0:HE], TS[:, HEADS:V, :])
                dve.tensor_copy(rest[:, HE:V], TD[:])
                dve.drain()
                split_parts(dve, rest, [TP[:, i] for i in range(3)], rest, low[:])
                dve.nop().then_inc(closed, 1)

                def weigh(r):
                    dve.wait_ge(x_used, GRP * r + GRP)
                    dve.wait_ge(expd, r + 1)
                    dve.tensor_copy(VW[:, :, 0:HEADS], S4[:])
                    hv = VV[:, :, 0:HE].rearrange("p u (h e) -> p u h e", h=HEADS)
                    ov = VW[:, :, HEADS:V].rearrange("p u (h e) -> p u h e", h=HEADS)
                    dve.tensor_tensor(ov, hv, S4[:, :, :, None].broadcast_to([128, GRP, HEADS, EXP]), ALU.mult)
                    dve.drain()
                    dve.nop().then_inc(weighted, 1)

                def turn(r, par):
                    dve.max(k8[:], g.work[:])
                    dve.drain()
                    dve.match_replace(g.work[:], k8[:], g.work[:], 0.0)
                    weigh(r)
                    kb = k8[:].bitcast(I32)
                    dve.tensor_scalar(ki[:, 0], kb, 127, None, ALU.bitwise_and)
                    dve.tensor_scalar(ki[:, 1], kb, 7, 63, ALU.logical_shift_right, ALU.bitwise_and)
                    dve.tensor_scalar(ki[:, 2], kb, 13, 127, ALU.logical_shift_right, ALU.bitwise_and)
                    dve.tensor_scalar(ki[:, 3], kb, 20, None, ALU.logical_shift_right)
                    dve.drain()
                    dve.tensor_copy(idx[:], ki[:])
                    dve.drain()
                    dve.tensor_scalar(idx[:, 3], idx[:, 3], float(VALID >> 20), None, ALU.subtract)
                    for u in range(GRP):
                        dve.tensor_scalar(OS[:, u], g.iof[:], idx[:, 0, u:u + 1], None, ALU.is_equal)
                        dve.tensor_scalar(OD[:, par, u], g.iof[:], idx[:, 2, u:u + 1], None, ALU.is_equal).then_inc(hot, 1)
                    dve.drain()
                    io = g.iof[:, None, 0:TT].broadcast_to([128, GRP, TT])
                    for i in range(2):
                        dve.tensor_tensor(M[:, par, :, i, :], io, idx[:, 1 + 2 * i, :, None].broadcast_to([128, GRP, TT]), ALU.is_equal)
                    dve.drain()
                    for u in range(GRP):
                        dve.wait_ge(g_ps, r * GRP + u + 1)
                        k = u % HALF
                        dve.tensor_tensor(SEL[:, k, 0:VB], psg[u % 2][0][:], M[:, par, u, 0:1, :].broadcast_to([128, VB, TT]), ALU.mult)
                        two = lambda t: t.rearrange("p (i v) t -> p i v t", i=2)
                        dve.tensor_tensor(two(SEL[:, k, VB:V]), two(psg[u % 2][1][:]),
                                          M[:, par, u, :, None, :].broadcast_to([128, 2, HEADS, TT]), ALU.mult).then_inc(picked, 1)
                        if k == HALF - 1:
                            dve.drain()
                            dve.tensor_reduce(VV[:, u - k:u + 1, :], SEL, AX.X, ALU.add)
                            dve.drain()
                    dve.tensor_tensor(VA[:], VV[:, :, 0:HE], att0[:, None, :].broadcast_to([128, GRP, HE]), ALU.mult)
                    dve.tensor_tensor(SC[:, :, 1], VV[:, :, HE:V], amax[:, None, :].broadcast_to([128, GRP, HEADS]), ALU.add)
                    dve.drain()
                    dve.tensor_reduce(SC[:, :, 0], VA[:].rearrange("p u (h e) -> p u h e", h=HEADS), AX.X, ALU.add)
                    dve.drain()
                    dve.tensor_tensor(SC[:, :, 0], SC[:, :, 0], VV[:, :, HE:V], ALU.add)
                    dve.drain()
                    leaky(dve, SC[:], 0.2)
                    dve.tensor_tensor(S4[:], SC[:, :, 0], SC[:, :, 1], ALU.subtract).then_inc(scored, 1)
                loop(dve, turn, weigh)

            @block.gpsimd
            def _(pool):
                def spread(r, par):
                    pool.wait_ge(weighted, r + 1)
                    for u in range(GRP):
                        pool.wait_ge(x_used, GRP * r + u + 5)
                        pool.tensor_tensor(X[:, u % XBUF], VW[:, u, :, None].broadcast_to([128, V, TT]),
                                           M[:, 1 - par, u, 1:2, :].broadcast_to([128, V, TT]), ALU.mult).then_inc(x_ready, 1)
                        pool.wait_ge(x_ready, GRP * r + u + 1)
                loop(pool, spread, lambda r: spread(r, 0))

            @block.scalar
            def _(act):
                act.wait_ge(closed, 1)
                act.activation(S4[:], VV[:, :, 0:HEADS], ACT.Copy).then_inc(expd, 1)

                def turn(r, par):
                    for u in range(GRP):
                        s = r * GRP + u
                        act.wait_ge(t_ps, s + 1)
                        if u >= 2:
                            act.wait_ge(g_ps, s - 1)
                        act.activation(OT[:, u % 2], pst[u % 2][:], ACT.Copy).then_inc(t_out, 1)
                    act.wait_ge(scored, r + 1)
                    act.activation(S4[:], S4[:], ACT.Exp).then_inc(expd, 1)
                loop(act, turn, lambda r: None)

            @block.tensor
            def _(pe):
                pe.wait_ge(closed, 1)
                flat = lambda t: t.rearrange("p v t -> p (v t)")
                for i in range(2):
                    mm = pe.matmul(flat(acc[i][:]), zero[:], flat(TS[:, 0:VH, :]), start=True, stop=False, skip_group_check=True)
                mm.then_inc(x_used, GRP)

                def turn(r, par):
                    def turned(u):
                        s = r * GRP + u
                        pe.wait_ge(hot, s + 1)
                        if u >= 2:
                            pe.wait_ge(t_out, s - 1)
                        pe.matmul(pst[u % 2][:, 0, :], OS[:, u], identb[:], start=True, stop=True)
                        pe.transpose(pst[u % 2][:, 1, :], OD[:, par, u], g.ident[:]).then_inc(t_ps, 1)

                    def gather(u):
                        s = r * GRP + u
                        pe.wait_ge(t_out, s + 1)
                        if u >= 2:
                            pe.wait_ge(picked, s - 1)
                        a, b = psg[u % 2]
                        src, dst = OT[:, u % 2, 0, :], OT[:, u % 2, 1, :]
                        for o, w, lo, hi in ((a[:], src, 0, VB), (b[:, 0:HE - VB, :], src, VB, HE), (b[:, HE - VB:, :], dst, HE, V)):
                            for i in range(3):
                                mm = pe.matmul(flat(o), w, flat(TP[:, i, lo:hi, :]), start=(i == 0), stop=(i == 2))
                        mm.then_inc(g_ps, 1)

                    turned(0)
                    for u in range(GRP):
                        if u + 1 < GRP:
                            turned(u + 1)
                        gather(u)
                    total(r, par)

                def total(r, par):
                    for u in range(GRP):
                        pe.wait_ge(x_ready, r * GRP + u + 1)
                        for i in range(2):
                            mm = pe.matmul(flat(acc[i][:]), OD[:, 1 - par, u], flat(X[:, u % XBUF, i * VH:(i + 1) * VH, :]),
                                           start=False, stop=False, skip_group_check=True)
                        mm.then_inc(x_used, 1)
                loop(pe, turn, lambda r: total(r, 0))
                for i in range(2):
                    mm = pe.matmul(flat(acc[i][:]), zero[:], flat(TS[:, 0:VH, :]), start=False, stop=True, skip_group_check=True)
                mm.then_inc(closed, 1)

        W2_, bg, lg, lb = sb("W2", [128, 2, HEADS, TT]), sb("bg", [128, HE]), sb("lg", [128, HE]), sb("lb", [128, HE])
        tmp, st = sb("tmp", [128, HE, TT]), sb("st", [128, TT, 2])
        S, R, C, G = (sb(s, [128, TT, EXP]) for s in ("S", "R", "C", "G"))
        st4 = sb("st4", [128, TT, EXP])
        G3, low4 = sb("G3", [128, TT, 3, EXP]), sb("low4", [128, TT, EXP], BF16)
        p_in, e1, e2, rt, rtd, sh, ex, gated, g_ps2, g_out = map(sem, ("p_in", "e1", "e2", "rt", "rtd", "sh", "ex", "gated", "gp2", "g_out"))
        block = ctx.enter_context(nc.Block())
        psr = [t[0][:].rearrange("p a b -> p (a b)") for t in psg]

        @block.sync
        def _(sp):
            for t, p in ((bg, g.L2_ffn_b_gat), (lg, g.L2_ffn_ln_gamma), (lb, g.L2_ffn_ln_beta)):
                sp.dma_start(t[:], p[None, :].broadcast_to([128, HE])).then_inc(p_in, 16)

        @block.vector
        def _(dve):
            bct = lambda t: t[:, :, None].broadcast_to([128, HE, TT])
            dve.tensor_tensor(W2_[:, 0], TS[:, 0:HEADS, :], TD[:], ALU.add)
            dve.tensor_tensor(W2_[:, 1], TD[:], last[:, 0:HEADS, None].broadcast_to([128, HEADS, TT]), ALU.add)
            for i in range(2):
                dve.tensor_copy(A[:, i * VH:(i + 1) * VH, :], acc[i][:])
            dve.drain()
            leaky(dve, W2_[:], 0.2)
            for i in range(2):
                dve.tensor_tensor(W2_[:, i], W2_[:, i], TM[:], ALU.subtract)
            dve.drain()
            dve.nop().then_inc(e1, 1)
            dve.wait_ge(e2, 1)
            dve.tensor_tensor(W2_[:, 1], W2_[:, 1], g.cntB[:, None, :].broadcast_to([128, HEADS, TT]), ALU.mult)
            dve.drain()
            t4 = tmp[:].rearrange("p (h e) t -> p h e t", h=HEADS)
            for i in range(2):
                dve.tensor_tensor(A[:, 0:HEADS, :], A[:, 0:HEADS, :], W2_[:, i], ALU.add)
                for h in range(HEADS):
                    w = W2_[:, i, h, None, :].broadcast_to([128, EXP, TT])
                    if i == 0:
                        v = TS[:, HEADS + h * EXP:HEADS + (h + 1) * EXP, :]
                    else:
                        v = last[:, HEADS + h * EXP:HEADS + (h + 1) * EXP, None].broadcast_to([128, EXP, TT])
                    dve.tensor_tensor(t4[:, h], v, w, ALU.mult)
                dve.drain()
                dve.tensor_tensor(A[:, HEADS:V, :], A[:, HEADS:V, :], tmp[:], ALU.add)
                dve.drain()
            dve.tensor_scalar(A[:, 0:HEADS, :], A[:, 0:HEADS, :], 1e-30, None, ALU.add)
            dve.drain()
            dve.reciprocal(A[:, 0:HEADS, :], A[:, 0:HEADS, :])
            dve.drain()
            M = A[:, HEADS:V, :]
            for h in range(HEADS):
                mh = A[:, HEADS + h * EXP:HEADS + (h + 1) * EXP, :]
                dve.tensor_tensor(mh, mh, A[:, h:h + 1, :].broadcast_to([128, EXP, TT]), ALU.mult)
            dve.wait_ge(p_in, 48)
            dve.drain()
            dve.tensor_tensor(M, M, bct(bg), ALU.add)
            dve.drain()
            bst = lambda k: st[:, :, k:k + 1].rearrange("p t a -> p a t").broadcast_to([128, HE, TT])
            dve.tensor_reduce(st[:, :, 0:1], M.rearrange("p v t -> p t v"), AX.X, ALU.add)
            dve.drain()
            dve.tensor_scalar(st[:, :, 0:1], st[:, :, 0:1], 1.0 / HE, None, ALU.mult)
            dve.drain()
            dve.tensor_tensor(M, M, bst(0), ALU.subtract)
            dve.drain()
            dve.tensor_tensor(tmp[:], M, M, ALU.mult)
            dve.drain()
            dve.tensor_reduce(st[:, :, 1:2], tmp[:].rearrange("p v t -> p t v"), AX.X, ALU.add)
            dve.drain()
            dve.tensor_scalar(st[:, :, 1:2], st[:, :, 1:2], 1.0 / HE, None, ALU.mult)
            dve.drain()
            dve.nop().then_inc(rt, 1)
            dve.wait_ge(rtd, 1)
            dve.reciprocal(st[:, :, 1:2], st[:, :, 1:2])
            dve.drain()
            dve.tensor_tensor(M, M, bst(1), ALU.mult)
            dve.drain()
            dve.tensor_tensor(M, M, bct(lg), ALU.mult)
            dve.drain()
            dve.tensor_tensor(M, M, bct(lb), ALU.add)
            dve.drain()
            dve.tensor_reduce(S[:], M.rearrange("p (h e) t -> p t e h", h=HEADS), AX.X, ALU.add)
            dve.drain()
            dve.tensor_scalar(S[:], S[:], 1.0 / HEADS, None, ALU.mult)
            dve.drain()
            top2(dve, S, R, C, G, EXP)
            softmax_top2_before(dve, S, st4)
            dve.drain()
            dve.nop().then_inc(sh, 1)
            dve.wait_ge(ex, 1)
            softmax_top2_after(dve, S, G, st4)
            split_parts(dve, G[:], [G3[:, :, i, :] for i in range(3)], G[:], low4[:])
            dve.nop().then_inc(gated, 1)

        @block.scalar
        def _(act):
            act.wait_ge(e1, 1)
            act.activation(W2_[:], W2_[:], ACT.Exp).then_inc(e2, 1)
            act.wait_ge(rt, 1)
            act.activation(st[:, :, 1:2], st[:, :, 1:2], ACT.Sqrt, bias=g.eps[:, 0:1]).then_inc(rtd, 1)
            act.wait_ge(sh, 1)
            act.activation(S[:], S[:], ACT.Exp).then_inc(ex, 1)
            for c in range(TT // 2):
                act.wait_ge(g_ps2, c + 1)
                act.activation(g.GT[0:3 * EXP, c * 256:(c + 1) * 256], psr[c % 2][0:3 * EXP, 0:256], ACT.Copy).then_inc(g_out, 1)

        @block.tensor
        def _(pe):
            pe.wait_ge(gated, 1)
            for c in range(TT // 2):
                if c >= 2:
                    pe.wait_ge(g_out, c - 1)
                for k in range(2):
                    mm = pe.transpose(psr[c % 2][0:3 * EXP, k * 128:(k + 1) * 128], G3[:, 2 * c + k].rearrange("p i e -> p (i e)"), g.ident[:])
                mm.then_inc(g_ps2, 1)


SH_, SP_, SG = 8, 64, 64
DI = SH_ * SP_
KT = DI // 128
SEQ = SG
CW = CHG * SG
XB = KT + 1
DTR = 40
SPW = 128 + SH_
IPM = 2 * KT + 2


def l0_ffn(nc, g):
    with nc.cleanup_on_exit(), ExitStack() as ctx:
        sb = lambda s, shape: ctx.enter_context(nc.sbuf_tensor(f"hy_{s}", shape, F32))
        sem = lambda s: nc.alloc_semaphore(f"hy_{s}")
        wfx, wlg, bfx, blg = sb("wfx", [D, DI]), sb("wlg", [D, DI]), sb("bfx", [128, DI]), sb("blg", [128, DI])
        win, wdt = sb("win", [128, KT, 2 * DI + 128]), sb("wdt", [128, KT, DTR])
        wo, wout, wfd = sb("wo", [128, KT, DI]), sb("wout", [128, KT, D]), sb("wfd", [128, KT, SH_])
        spread = sb("spread", [128, KT - 1, SPW])
        cw, cb = sb("cw", [128, XB, 3]), sb("cb", [128, XB])
        dtb, negA, outb, Dp = sb("dtb", [DTR, 1]), sb("negA", [DTR, 1]), sb("outb", [128, 1]), sb("Dp", [128, SH_])
        delta, selS, selB = sb("delta", [128, SEQ]), sb("selS", [128, CHP, CHG]), sb("selB", [DTR, CHG, 128])
        PS = [ctx.enter_context(nc.psum_tensor(f"hy_ps{i}", [128, 512], F32)) for i in range(8)]
        dA_dram = nc.dram_tensor("hy_decays", [2, 2, SH_, CHP, SEQ], F32).ap()

        with ExitStack() as first:
            fsb = lambda s, shape: first.enter_context(nc.sbuf_tensor(f"hy_{s}", shape, F32))
            raw_in, raw_dt = fsb("raw_in", [128, 2 * KT + 1, DI]), fsb("raw_dt", [DTR, DI])
            raw_o, raw_out, raw_fd = fsb("raw_o", [128, KT, DI]), fsb("raw_out", [128, DI]), fsb("raw_fd", [SH_, DI])
            raw_fx, raw_x, raw_sl = fsb("raw_fx", [128, KT, D]), fsb("raw_x", [128, KT, D]), fsb("raw_sl", [SG, SP_])
            slT, bx, bxr = fsb("slT", [128, SG]), fsb("bx", [128, KT]), fsb("bxr", [128, KT, 128])
            nw, tmp, bsl, sl2 = fsb("nw", [128, KT]), fsb("tmp", [128, SH_]), fsb("bsl", [128, SG]), fsb("sl2", [SG, 128])
            ws = {s: nc.alloc_semaphore(f"hyw_{s}") for s in ("w_in", "z", "sel", "t_ps", "t_out", "ready", "c_ps", "a1", "a2", "sl")}
            block = first.enter_context(nc.Block())
            slow = dict(allow_slow_non_contiguous=True)
            col = lambda t: t.rearrange("(d a) -> d a", a=1)
            tiles = lambda t: t.rearrange("(k p) -> p k", p=128)
            NLOAD = 26

            @block.sync
            def _(sp):
                def ld(dst, src, **kw):
                    sp.dma_start(dst, src, **kw).then_inc(ws["w_in"], 16)
                sp.wait_ge(ws["z"], 1)
                W = g.L0_ffn_hy_in_w
                ld(raw_in[:], W[0:2 * DI + 128, :].rearrange("(m p) k -> p m k", p=128))
                ld(raw_dt[0:SH_, :], W[2 * DI + 128:2 * DI + 128 + SH_, :])
                ld(raw_dt[32:32 + SH_, :], W[2 * DI + 128 + SH_:, :])
                ld(raw_o[:], g.L0_ffn_hy_out_w.rearrange("(m p) k -> p m k", p=128))
                ld(raw_out[:], g.L0_ffn_out_w)
                ld(raw_fd[:], g.L0_ffn_hy_fcD_w)
                ld(raw_fx[:], g.L0_ffn_W_fx.rearrange("(m p) k -> p m k", p=128))
                ld(raw_x[:], g.L0_ffn_W_x.rearrange("(m p) k -> p m k", p=128))
                ld(raw_sl[:], g.L0_ffn_W_slice)
                ld(bx[:], tiles(g.L0_ffn_b_x), **slow)
                ld(nw[:], tiles(g.L0_ffn_hy_norm_w), **slow)
                ld(bsl[:], g.L0_ffn_b_slice[None, :].broadcast_to([128, SG]))
                ld(bfx[:], g.L0_ffn_b_fx[None, :].broadcast_to([128, DI]))
                ld(tmp[:], g.L0_ffn_temperature.rearrange("a h b c -> a (h b c)").broadcast_to([128, SH_]))
                for i in range(3):
                    ld(cw[:, :, i], g.L0_ffn_hy_conv_w[:, i].rearrange("(k p) -> p k", p=128), **slow)
                ld(cb[:], tiles(g.L0_ffn_hy_conv_b), **slow)
                ld(dtb[0:SH_, :], col(g.L0_ffn_hy_dt_bias), **slow)
                ld(dtb[32:32 + SH_, :], col(g.L0_ffn_hy_dt_bias), **slow)
                ld(negA[0:SH_, :], col(g.L0_ffn_hy_A_log), **slow)
                ld(negA[32:32 + SH_, :], col(g.L0_ffn_hy_A_log), **slow)
                ld(outb[:], col(g.L0_ffn_out_b), **slow)
                ld(Dp[:], g.L0_ffn_hy_D[None, :].broadcast_to([128, SH_]))
                ld(sl2[:, 0:SP_], g.L0_ffn_W_slice)
                ld(sl2[:, SP_:], g.L0_ffn_W_slice)

            @block.gpsimd
            def _(pool):
                made = [0]

                def step(ins):
                    made[0] += 1
                    ins.then_inc(ws["sel"], 1)
                    pool.wait_ge(ws["sel"], made[0])

                step(pool.memset(delta[:], 0.0))
                step(pool.memset(selS[:], 1.0))
                step(pool.memset(selB[:], 0.0))
                for j in range(2):
                    h = slice(SLOT * j, SLOT * (j + 1))
                    step(pool.affine_select(out=delta[h, :], in_=delta[h, :], compare_op=ALU.not_equal, fill=1.0, base=0,
                                            pattern=[[-1, SEQ]], channel_multiplier=1))
                    step(pool.affine_select(out=selS[h], in_=selS[h], compare_op=ALU.is_ge, fill=0.0, base=N - 1,
                                            pattern=[[0, CHP], [0, CHG]], channel_multiplier=-1))
                    step(pool.affine_select(out=selS[h], in_=selS[h], compare_op=ALU.is_equal, fill=0.0, base=j,
                                            pattern=[[2, CHP], [-1, CHG]], channel_multiplier=0))
                    r = slice(32 * j, 32 * j + CHG)
                    o = selB[r, :, SLOT * j:SLOT * (j + 1)]
                    step(pool.affine_select(out=o, in_=o, compare_op=ALU.not_equal, fill=1.0, base=0,
                                            pattern=[[-1, CHG], [0, SLOT]], channel_multiplier=1))

            srcs = []
            for m in range(2 * KT + 1):
                srcs.append(([raw_in[:, m, k * 128:(k + 1) * 128] for k in range(KT)], 128, win[:, :, m * 128:(m + 1) * 128]))
            for m in range(KT):
                srcs.append(([raw_o[:, m, k * 128:(k + 1) * 128] for k in range(KT)], 128, wo[:, :, m * 128:(m + 1) * 128]))
            srcs.append(([raw_out[:, k * 128:(k + 1) * 128] for k in range(KT)], 128, wout[:]))
            srcs.append(([raw_fx[:, k, :] for k in range(KT)], 128, wfx[:].rearrange("p (k n) -> p k n", k=KT)))
            srcs.append(([raw_fd[:, k * 128:(k + 1) * 128] for k in range(KT)], SH_, wfd[:]))
            srcs.append(([raw_dt[:, k * 128:(k + 1) * 128] for k in range(KT)], DTR, wdt[:]))
            srcs.append(([sl2[:]], SG, slT[:, None, :]))
            NT = len(srcs)

            @block.tensor
            def _(pe):
                pe.wait_ge(ws["w_in"], 16 * NLOAD)
                for n, (ins_, w, _) in enumerate(srcs):
                    if n >= 2:
                        pe.wait_ge(ws["t_out"], n - 1)
                    for k, s in enumerate(ins_):
                        mm = pe.transpose(PS[n % 2][:, k * w:(k + 1) * w], s, g.ident[0:w, 0:w])
                    mm.then_inc(ws["t_ps"], 1)
                pe.wait_ge(ws["t_out"], NT)
                pe.wait_ge(ws["ready"], 1)
                for h in range(SH_):
                    r = slice(SLOT * (h % 2), SLOT * (h % 2) + SLOT)
                    o = slice((h // 2) * SG, (h // 2 + 1) * SG)
                    pe.matmul(PS[2 + h % 2][:, o], raw_x[r, h // 2, :], slT[r, :], start=True, stop=True)
                    mm = pe.matmul(PS[4 + h % 2][:, o], bxr[r, h // 2, :], slT[r, :], start=True, stop=True)
                mm.then_inc(ws["c_ps"], 1)

            @block.scalar
            def _(act):
                act.wait_ge(ws["a1"], 1)
                act.activation(negA[:], negA[:], ACT.Exp).then_inc(ws["a2"], 1)

            @block.vector
            def _(dve):
                dve.memset(raw_dt[:], 0.0)
                dve.memset(dtb[:], 0.0)
                dve.memset(negA[:], 0.0).then_inc(ws["z"], 1)
                dve.wait_ge(ws["w_in"], 16 * NLOAD)
                dve.tensor_scalar(negA[:], negA[:], 88.0, None, ALU.min).then_inc(ws["a1"], 1)
                dve.tensor_copy(spread[:, :, 0:128], g.ident[:, None, :].broadcast_to([128, KT - 1, 128]))
                for n, (ins_, w, dst) in enumerate(srcs):
                    dve.wait_ge(ws["t_ps"], n + 1)
                    dve.tensor_copy(dst, PS[n % 2][:, 0:len(ins_) * w].rearrange("p (k n) -> p k n", n=w)).then_inc(ws["t_out"], 1)
                dve.drain()
                dve.tensor_copy(spread[:, :, 128:SPW], wfd[:, 0:KT - 1, :])
                for k in range(KT):
                    dve.tensor_scalar(bxr[:, k, :], g.mean_w[:], bx[:, k:k + 1], float(D), ALU.mult, ALU.mult)
                    dve.tensor_scalar(wo[:, k, :], wo[:, k, :], nw[:, k:k + 1], None, ALU.mult)
                dve.tensor_scalar(tmp[:], tmp[:], 1e-6, None, ALU.max)
                dve.drain()
                dve.reciprocal(tmp[:], tmp[:])
                dve.wait_ge(ws["a2"], 1)
                dve.tensor_scalar(negA[:], negA[:], -1.0, None, ALU.mult)
                dve.drain()
                dve.nop().then_inc(ws["ready"], 1)
                dve.wait_ge(ws["c_ps"], 1)
                for par in range(2):
                    heads = lambda t: t[:].rearrange("p (k a n) -> p a k n", a=2, n=SG)[:, par]
                    ps = lambda i: PS[i + par][:, 0:KT * SG].rearrange("p (k n) -> p k n", k=KT)
                    it = tmp[:].rearrange("p (k a) -> p a k", a=2)[:, par][:, :, None].broadcast_to([128, KT, SG])
                    dve.tensor_tensor(heads(wlg), ps(2), it, ALU.mult)
                    dve.tensor_tensor(heads(blg), ps(4), bsl[:, None, :].broadcast_to([128, KT, SG]), ALU.add)
                    dve.drain()
                    dve.tensor_tensor(heads(blg), heads(blg), it, ALU.mult)

        lent = g.XNG[:].rearrange("p q d -> p (q d)")
        HQT = SH_ * CHP * SEQ
        dAb = lent[:, 0:2 * HQT].rearrange("p (a n) -> p a n", a=2)
        L = lent[:, 2 * HQT:4 * HQT].rearrange("p (a n) -> p a n", a=2)
        lent = g.XNP[:].rearrange("p b n -> p (b n)")
        zs = lent[:, 0:2 * KT * CW].rearrange("p (a k n) -> p a k n", a=2, k=KT)
        xt, ot = (lent[:, (2 + i) * KT * CW:(3 + i) * KT * CW].rearrange("p (q n) -> p q n", q=CHP) for i in range(2))
        xn_dram = nc.dram_tensor("hy_xn", [NCH, 128, CW], F32).ap()
        XC, fx, sw, sst = sb("XC", [128, CW]), sb("fx", [128, CHP, DI]), sb("sw", [128, CHP, DI]), sb("sst", [128, CHP * SH_])
        rn, rb, uT, swT = sb("rn", [DTR, KT * SG]), sb("rb", [128, 2, 512]), sb("uT", [128, KT, CW]), sb("swT", [128, 2, CHP, SH_, N])
        xr, yg = sb("xr", [128, XB, CHG, SEQ + 2]), sb("yg", [128, KT, CW])
        xs, Cs = sb("xs", [128, XB, CW]), sb("Cs", [64, CW])
        dtv, dA = sb("dtv", [DTR, CW]), sb("dA", [DTR, CW])
        dtc, Dc = sb("dtc", [128, 2, SH_, CHP]), sb("Dc", [128, SH_, CHP])
        share = sb("share", [128, CHP, KT - 1, SH_])
        E, W, rr, dt1, sq = fx[:].rearrange("p q n -> p (q n)"), dAb[:, 0].rearrange("p (h q t) -> p h q t", q=CHP, t=SEQ), rb[:, 0], dA, uT
        oT = uT[:].rearrange("p k n -> p (k n)")[:, 0:KT * CH].rearrange("p (k q j n) -> p k q j n", q=CHP, j=2, n=N)
        s = {n: sem(n) for n in ("xn_st", "xc", "lf_ps", "lg_out", "smx", "sme", "smd", "sn_ps", "rn", "st_ps", "rb_out", "u_out", "sT_ps", "sT_out",
                                 "ip_ps", "ip_out", "cv", "xs", "dtln", "dt_rdy", "da_exp", "da_rdy", "da_ld", "xt_ps", "xt_out",
                                 "g_ps", "w_rdy", "y_ps", "yg1", "sq", "sq_sum", "r_ps", "rt", "yg2", "ot_ps", "ot_out", "o_ps", "oT_out", "f_ps", "init", "settled")}
        da_st = [sem(f"da_st{i}") for i in range(2)]
        half = lambda j: slice(SLOT * j, SLOT * (j + 1))
        ORDER = [IPM - 1] + list(range(KT, 2 * KT + 1)) + list(range(KT))

        with nc.Block() as spill:
            @spill.sync
            def _(sp):
                sp.dma_start(xn_dram.rearrange("c p n -> p c n"), g.XNP[:].rearrange("p (c b) n -> p c (b n)", b=CHG)).then_inc(s["xn_st"], 16)
                sp.wait_ge(s["xn_st"], 16)

        def there(k):
            return not isinstance(k, int) or 0 <= k < NCH

        def wait(eng, sem, value):
            if not isinstance(value, int) or value > 0:
                eng.wait_ge(sem, value)

        def all_turns(eng, turn):
            turn(-2, 0)
            turn(-1, 1)
            with eng.Fori(0, (NCH - 2) // 2) as i:
                turn(2 * i, 0)
                turn(2 * i + 1, 1)
            turn(NCH - 2, 0)
            turn(NCH - 1, 1)

        block = ctx.enter_context(nc.Block())

        @block.sync
        def _(sp):
            def load_xn(k):
                wait(sp, s["lf_ps"], 4 * k)
                src = xn_dram[bass.ds(k, 1)] if not isinstance(k, int) else xn_dram[k:k + 1]
                sp.dma_start(XC[:], src.rearrange("c p n -> p (c n)")).then_inc(s["xc"], 16)

            def spread_decays(k):
                sp.wait_ge(s["da_rdy"], k + 1)
                for a in range(2):
                    src = dA[32 * a:32 * a + SH_, :].rearrange("h (q j t) -> h q j t", j=2, t=SEQ)
                    for j in range(2):
                        sp.dma_start(dA_dram[j, a], src[:, :, j, :]).then_inc(da_st[j], 16)
                wait(sp, s["y_ps"], 2 * k)
                for j in range(2):
                    sp.wait_ge(da_st[j], 32 * k + 32)
                    src = dA_dram[j].rearrange("a h q t -> (a h q t)")[None, :].broadcast_to([SLOT, 2 * HQT])
                    sp.dma_start(dAb[half(j)].rearrange("p a n -> p (a n)"), src).then_inc(s["da_ld"], 16)

            def turn(c, par):
                if there(c + 2):
                    load_xn(c + 2)
                if there(c + 1):
                    spread_decays(c + 1)
            all_turns(sp, turn)

        @block.tensor
        def _(pe):
            def settle(sem, value):
                if not isinstance(value, int) or value > 0:
                    pe.wait_ge(sem, value)
                    pe.sem_inc(s["settled"], 1)

            def logits(k):
                pe.wait_ge(s["xc"], 16 * k + 16)
                wait(pe, s["sT_out"], 4 * k)
                for q in range(CHP):
                    if q >= 2:
                        pe.wait_ge(s["lg_out"], 4 * k + q - 1)
                    x = XC[:, q * 128:(q + 1) * 128]
                    pe.matmul(PS[q % 2][:], x, wlg[:], start=True, stop=True)
                    pe.matmul(PS[2 + q % 2][:], x, wfx[:], start=True, stop=True).then_inc(s["lf_ps"], 1)

            def slices(k):
                pe.wait_ge(s["smd"], k + 1)
                wait(pe, s["xt_out"], 4 * k)
                for par in range(2):
                    for q in range(CHP):
                        rhs = sw[:, q, :].rearrange("p (k a n) -> p a k n", a=2, n=SG)[:, par]
                        mm = pe.matmul(PS[4][32 * par:32 * par + CHG, 0:KT * SG].rearrange("p (k n) -> p k n", k=KT), selS[:, q, :], rhs,
                                       start=(q == 0), stop=(q == CHP - 1))
                mm.then_inc(s["sn_ps"], 1)

                def transposed(q):
                    if q >= 2:
                        settle(s["u_out"], 4 * k + q + 1)
                    for t in range(KT):
                        mm = pe.transpose(PS[2 * (q % 2)][:, t * 128:(t + 1) * 128], sw[:, q, t * 128:(t + 1) * 128], g.ident[:])
                    mm.then_inc(s["sT_ps"], 1)

                transposed(0)
                transposed(1)
                for q in range(CHP):
                    if q < 2:
                        settle(s["sT_out"], 4 * k + q + 1)
                    else:
                        settle(s["u_out"], 4 * k + q - 1)
                    for j in range(2):
                        for h in range(SH_):
                            o = (h // 2) * SG
                            pe.matmul(PS[2 * (q % 2) + j][half(h % 2), o:o + SG], fx[rows(j), q, h * 64:(h + 1) * 64],
                                      sw[rows(j), q, h * 64:(h + 1) * 64], start=True, stop=True)
                    if q == 0:
                        pe.wait_ge(s["rn"], k + 1)
                    for j in range(2):
                        mm = pe.matmul(PS[5 + q % 2][:, j * 256:(j + 1) * 256], selB[:, 2 * q + j, :], rn[:], start=True, stop=True)
                    mm.then_inc(s["st_ps"], 1)
                transposed(2)
                transposed(3)

            def input_projection(k):
                pe.wait_ge(s["u_out"], 4 * k + 4)
                for i, m in enumerate(ORDER):
                    if i >= 3:
                        pe.wait_ge(s["ip_out"], IPM * k + i - 2)
                    p = PS[4 + i % 3]
                    for t in range(KT):
                        if m < IPM - 1:
                            mm = pe.matmul(p[:], win[:, t, m * 128:(m + 1) * 128], uT[:, t, :], start=(t == 0), stop=(t == KT - 1))
                        else:
                            mm = pe.matmul(p[0:DTR, :], wdt[:, t, :], uT[:, t, :], start=(t == 0), stop=(t == KT - 1))
                    mm.then_inc(s["ip_ps"], 1)

            def steps_down(k):
                pe.wait_ge(s["xs"], XB * k + XB)
                pe.wait_ge(s["ip_out"], IPM * k + IPM)
                for q in range(CHP):
                    if q >= 2:
                        pe.wait_ge(s["xt_out"], 4 * k + q - 1)
                    for t in range(KT - 1):
                        pe.matmul(PS[4 + q % 2][:, t * SPW:(t + 1) * SPW], xs[:, t, q * 128:(q + 1) * 128], spread[:, t, :], start=True, stop=True)
                    mm = pe.transpose(PS[6][:, q * 128:(q + 1) * 128], xs[:, KT - 1, q * 128:(q + 1) * 128], g.ident[:])
                    mm.then_inc(s["xt_ps"], 1)

            def gains(k):
                for q in range(CHP):
                    for j in range(2):
                        b = slice((2 * q + j) * SEQ, (2 * q + j + 1) * SEQ)
                        pe.matmul(PS[7][half(j), q * SEQ:(q + 1) * SEQ], xs[0:64, KT, b], Cs[:, b], start=True, stop=True)
                    pe.matmul(PS[7][:, 256 + 8 * q:264 + 8 * q], xs[:, KT - 1, q * 128:(q + 1) * 128], wfd[:, KT - 1, :], start=True, stop=True)

            def dt_down(k):
                settle(s["dt_rdy"], k + 1)
                for q in range(CHP):
                    mm = pe.transpose(PS[7][:, 288 + DTR * q:288 + DTR * (q + 1)], dtv[:, q * 128:(q + 1) * 128], g.ident[0:DTR, 0:DTR])
                mm.then_inc(s["g_ps"], 1)

            def mix(k):
                pe.wait_ge(s["w_rdy"], k + 1)
                pe.wait_ge(s["xt_out"], 4 * k + 4)
                settle(s["sT_out"], 4 * (k + 2) if there(k + 1) else 4 * (k + 1))
                for q in range(CHP):
                    for j in range(2):
                        for h in range(SH_):
                            o = (h // 2) * 128 + (q % 2) * SEQ
                            mm = pe.matmul(PS[2 * (q // 2) + j][half(h % 2), o:o + SEQ], xt[half(j), q, h * 64:(h + 1) * 64],
                                           W[half(j), h, q, :], start=True, stop=True)
                    if q % 2:
                        mm.then_inc(s["y_ps"], 1)

            def squares(k):
                pe.wait_ge(s["sq_sum"], k + 1)
                if there(k + 1):
                    pe.wait_ge(s["xt_out"], 4 * k + 8)
                pe.matmul(PS[6][:], g.mean_w[:], sq[:, 0, :], start=True, stop=True).then_inc(s["r_ps"], 1)

            def output_projection(k):
                pe.wait_ge(s["yg2"], k + 1)
                if there(k + 1):
                    pe.wait_ge(s["xt_out"], 4 * k + 8)
                for q in range(CHP):
                    if q >= 2:
                        pe.wait_ge(s["ot_out"], 4 * k + q - 1)
                    for t in range(KT):
                        mm = pe.matmul(PS[4 + q % 2][:], yg[:, t, q * 128:(q + 1) * 128], wo[:, t, :], start=(t == 0), stop=(t == KT - 1))
                    mm.then_inc(s["ot_ps"], 1)

            def back_to_nodes(k, par):
                for q in range(CHP):
                    if q == 0 and there(k + 2):
                        settle(s["lg_out"], 4 * k + 12)
                    settle(s["ot_out"], 4 * k + q + 1)
                    if q >= 2:
                        settle(s["oT_out"], 4 * k + q - 1)
                    for j in range(2):
                        for h in range(SH_):
                            o = (h // 2) * N
                            mm = pe.matmul(PS[2 * (q % 2) + j][half(h % 2), o:o + N], ot[half(j), q, h * 64:(h + 1) * 64],
                                           swT[half(j), par, q, h, :], start=True, stop=True)
                    mm.then_inc(s["o_ps"], 1)
                pe.wait_ge(s["oT_out"], 4 * k + 4)
                for t in range(KT):
                    mm = pe.matmul(PS[6][:, 0:CH], wout[:, t, :], oT[:, t].rearrange("p q j n -> p (q j n)"), start=(t == 0), stop=(t == KT - 1))
                mm.then_inc(s["f_ps"], 1)

            def turn(c, par):
                if there(c + 1):
                    slices(c + 1)
                    input_projection(c + 1)
                if there(c):
                    mix(c)
                if there(c + 1):
                    steps_down(c + 1)
                if there(c):
                    squares(c)
                if there(c + 1):
                    gains(c + 1)
                if there(c + 2):
                    logits(c + 2)
                if there(c):
                    output_projection(c)
                    back_to_nodes(c, par)
                if there(c + 1):
                    dt_down(c + 1)
            all_turns(pe, turn)

        @block.scalar
        def _(act):
            act.wait_ge(s["init"], 1)

            def exps(k):
                act.wait_ge(s["smx"], k + 1)
                act.activation(sw[:], sw[:], ACT.Exp).then_inc(s["sme"], 1)

            def slices(k, par):
                def transposed(q):
                    act.wait_ge(s["sT_ps"], 4 * k + q + 1)
                    for j in range(2):
                        for a in range(2):
                            o = swT[half(j), par, q].rearrange("p (k a) n -> p k a n", a=2)[:, :, a, :]
                            p = PS[2 * (q % 2)][half(a), :].rearrange("p (k j n) -> p k j n", j=2, n=SLOT)
                            ins = act.activation(o, p[:, :, j, 0:N], ACT.Copy)
                    ins.then_inc(s["sT_out"], 1)

                transposed(0)
                transposed(1)
                for q in range(CHP):
                    act.wait_ge(s["st_ps"], 4 * k + q + 1)
                    if q >= 2:
                        act.wait_ge(s["u_out"], 4 * k + q - 1)
                    act.activation(rb[:, q % 2], PS[5 + q % 2][:], ACT.Copy).then_inc(s["rb_out"], 1)
                transposed(2)
                transposed(3)

            def projected(k, par):
                for i, m in enumerate(ORDER):
                    act.wait_ge(s["ip_ps"], IPM * k + i + 1)
                    p = PS[4 + i % 3]
                    if m < KT:
                        act.activation(zs[:, par, m, :], p[:], ACT.Silu).then_inc(s["ip_out"], 1)
                    elif m < IPM - 1:
                        if i == 1:
                            wait(act, s["cv"], XB * k)
                        act.activation(xr[:, m - KT, :, 2:], p[:].rearrange("p (b t) -> p b t", t=SEQ), ACT.Copy).then_inc(s["ip_out"], 1)
                    else:
                        wait(act, s["da_ld"], 32 * k)
                        act.activation(dt1[:], p[0:DTR, :], ACT.Abs, bias=dtb[:, 0:1])
                        act.activation(dtv[:], p[0:DTR, :], ACT.Identity, bias=dtb[:, 0:1]).then_inc(s["ip_out"], 1)
                        act.drain()
                        act.activation(dt1[:], dt1[:], ACT.Exp, scale=-1.0)
                        act.drain()
                        act.activation(dt1[:], dt1[:], ACT.Ln, bias=1.0).then_inc(s["dtln"], 1)
                    if i == XB:
                        act.wait_ge(s["dt_rdy"], k + 1)
                        act.activation(dA[:], dtv[:], ACT.Exp, scale=negA[:, 0:1]).then_inc(s["da_exp"], 1)

            def convolved(k):
                for i in range(KT):
                    act.wait_ge(s["cv"], XB * k + i + 1)
                    act.activation(xs[:, i, :], xs[:, i, :], ACT.Silu).then_inc(s["xs"], 1)
                act.wait_ge(s["cv"], XB * k + XB)
                act.activation(Cs[:], xs[64:128, KT, :], ACT.Silu)
                act.activation(xs[0:64, KT, :], xs[0:64, KT, :], ACT.Silu).then_inc(s["xs"], 1)

            def steps_down(k):
                for q in range(CHP):
                    act.wait_ge(s["xt_ps"], 4 * k + q + 1)
                    p = PS[4 + q % 2][:, 0:(KT - 1) * SPW].rearrange("p (t n) -> p t n", n=SPW)
                    act.activation(xt[:, q, 0:(KT - 1) * 128].rearrange("p (t n) -> p t n", n=128), p[:, :, 0:128], ACT.Copy)
                    ins = act.activation(share[:, q], p[:, :, 128:SPW], ACT.Copy)
                    if q == CHP - 1:
                        ins = act.activation(xt[:, :, (KT - 1) * 128:], PS[6][:].rearrange("p (q n) -> p q n", n=128), ACT.Copy)
                    ins.then_inc(s["xt_out"], 1)

            def squares(k):
                act.wait_ge(s["yg1"], k + 1)
                act.activation(sq[:], yg[:], ACT.Square).then_inc(s["sq"], 1)

            def root(k):
                act.wait_ge(s["r_ps"], k + 1)
                act.activation(rr, PS[6][:], ACT.Sqrt, bias=g.eps[:, 0:1], scale=D / DI).then_inc(s["rt"], 1)

            def out_copy(k, q):
                act.wait_ge(s["ot_ps"], 4 * k + q + 1)
                act.activation(ot[:, q, :], PS[4 + q % 2][:], ACT.Copy).then_inc(s["ot_out"], 1)

            def turn(c, par):
                if there(c + 1):
                    slices(c + 1, 1 - par)
                    projected(c + 1, 1 - par)
                    convolved(c + 1)
                if there(c):
                    squares(c)
                if there(c + 1):
                    steps_down(c + 1)
                if there(c):
                    root(c)
                    out_copy(c, 0)
                if there(c + 2):
                    exps(c + 2)
                if there(c):
                    for q in range(1, CHP):
                        out_copy(c, q)
            all_turns(act, turn)

        @block.vector
        def _(dve):
            dve.memset(rn[:], 0.0)
            dve.memset(xr[:], 0.0)
            dve.drain()
            dve.nop().then_inc(s["init"], 1)

            def softmax(k):
                for q in range(CHP):
                    dve.wait_ge(s["lf_ps"], 4 * k + q + 1)
                    dve.tensor_tensor(sw[:, q, :], PS[q % 2][:], blg[:], ALU.add)
                    dve.tensor_tensor(fx[:, q, :], PS[2 + q % 2][:], bfx[:], ALU.add).then_inc(s["lg_out"], 1)
                dve.drain()
                sw3 = sw[:].rearrange("p q (h n) -> p (q h) n", n=SG)
                bc = sst[:, :, None].broadcast_to([128, CHP * SH_, SG])
                dve.tensor_reduce(sst[:], sw3, AX.X, ALU.max)
                dve.drain()
                dve.tensor_tensor(sw3, sw3, bc, ALU.subtract).then_inc(s["smx"], 1)
                dve.wait_ge(s["sme"], k + 1)
                dve.tensor_reduce(sst[:], sw3, AX.X, ALU.add)
                dve.drain()
                dve.reciprocal(sst[:], sst[:])
                dve.drain()
                dve.tensor_tensor(sw3, sw3, bc, ALU.mult).then_inc(s["smd"], 1)

            def states(k):
                dve.wait_ge(s["sn_ps"], k + 1)
                for par in range(2):
                    r = slice(32 * par, 32 * par + CHG)
                    dve.tensor_scalar(rn[r, :], PS[4][r, 0:KT * SG], 1e-5, None, ALU.add)
                dve.drain()
                dve.reciprocal(rn[0:CHG, :], rn[0:CHG, :])
                dve.reciprocal(rn[32:32 + CHG, :], rn[32:32 + CHG, :]).then_inc(s["rn"], 1)
                for q in range(CHP):
                    dve.wait_ge(s["rb_out"], 4 * k + q + 1)
                    for j in range(2):
                        o = uT[:, :, (2 * q + j) * SG:(2 * q + j + 1) * SG]
                        v = lambda t: t.rearrange("p (k n) -> p k n", n=SG)
                        ins = dve.tensor_tensor(o, v(PS[2 * (q % 2) + j][:, 0:256]), v(rb[:, q % 2, j * 256:(j + 1) * 256]), ALU.mult)
                    ins.then_inc(s["u_out"], 1)

            dlt = delta[:, None, :].broadcast_to([128, SH_ * CHP, SEQ])
            per = lambda t: t.rearrange("p h q -> p (h q)")[:, :, None].broadcast_to([128, SH_ * CHP, SEQ])

            def decayed(k, a):
                dve.tensor_tensor(E.rearrange("p (r t) -> p r t", t=SEQ), dlt, per(dtc[:, a]), ALU.mult)
                dve.drain()
                if a == 0:
                    dve.wait_ge(s["da_ld"], 32 * k + 32)
                st = slice(None) if a == 0 else slice(None, None, -1)
                dve.tensor_tensor_scan(L[:, a][:, st], dAb[:, a][:, st], E[:, st], 0.0, ALU.mult, ALU.add)
                dve.drain()
                G = PS[7][:, None, 0:CHP * SEQ].broadcast_to([128, SH_, CHP * SEQ])
                l3 = L[:, a].rearrange("p (h n) -> p h n", h=SH_)
                dve.tensor_tensor(l3, l3, G, ALU.mult)

            def weights(k):
                W3 = W.rearrange("p h q t -> p (h q) t")
                dve.tensor_tensor(W3, dlt, per(Dc[:]), ALU.mult)
                dve.drain()
                L3 = lambda a: L[:, a].rearrange("p (r t) -> p r t", t=SEQ)
                dve.tensor_tensor(W3[:, :, 1:], W3[:, :, 1:], L3(0)[:, :, :SEQ - 1], ALU.add)
                dve.drain()
                dve.tensor_tensor(W3[:, :, :SEQ - 1], W3[:, :, :SEQ - 1], L3(1)[:, :, 1:], ALU.add).then_inc(s["w_rdy"], 1)

            def dt_ready(k):
                dve.wait_ge(s["dtln"], k + 1)
                dve.scalar_tensor_tensor(dtv[:], dtv[:], 0.0, dt1[:], ALU.max, ALU.add).then_inc(s["dt_rdy"], 1)

            def convolve(k):
                for i in range(XB):
                    dve.wait_ge(s["ip_out"], IPM * k + i + 2)
                    o = xs[:, i, :].rearrange("p (b t) -> p b t", t=SEQ)
                    dve.tensor_scalar(o, xr[:, i, :, 2:], cw[:, i, 2:3], cb[:, i:i + 1], ALU.mult, ALU.add)
                    dve.drain()
                    dve.scalar_tensor_tensor(o, xr[:, i, :, 1:SEQ + 1], cw[:, i, 1:2], o, ALU.mult, ALU.add)
                    dve.drain()
                    dve.scalar_tensor_tensor(o, xr[:, i, :, 0:SEQ], cw[:, i, 0:1], o, ALU.mult, ALU.add).then_inc(s["cv"], 1)
                    if i == 0:
                        dve.wait_ge(s["da_exp"], k + 1)
                        d4 = dA[:].rearrange("p (b t) -> p b t", t=SEQ)
                        dve.memset(d4[0:SH_, :, 0:1], 0.0)
                        dve.memset(d4[32:32 + SH_, :, SEQ - 1:SEQ], 0.0).then_inc(s["da_rdy"], 1)

            def gate(k, par):
                dve.wait_ge(s["ip_out"], IPM * k + IPM)
                y5 = yg[:].rearrange("p k (q j t) -> p k q j t", j=2, t=SEQ)
                z5 = zs[:, par].rearrange("p k (q j t) -> p k q j t", j=2, t=SEQ)
                for f in range(2):
                    dve.wait_ge(s["y_ps"], 2 * k + f + 1)
                    for q in range(2 * f, 2 * f + 2):
                        for j in range(2):
                            p = PS[2 * f + j][:].rearrange("p (k q t) -> p k q t", k=KT, q=2)[:, :, q % 2, :]
                            ins = dve.tensor_tensor(y5[:, :, q, j, :], p, z5[:, :, q, j, :], ALU.mult)
                ins.then_inc(s["yg1"], 1)

            def rms(k):
                dve.wait_ge(s["sq"], k + 1)
                dve.tensor_tensor(sq[:, 0:2], sq[:, 0:2], sq[:, 2:4], ALU.add)
                dve.drain()
                dve.tensor_tensor(sq[:, 0], sq[:, 0], sq[:, 1], ALU.add).then_inc(s["sq_sum"], 1)
                dve.wait_ge(s["rt"], k + 1)
                dve.reciprocal(rr, rr)
                dve.drain()
                dve.tensor_tensor(yg[:], yg[:], rr[:, None, :].broadcast_to([128, KT, CW]), ALU.mult).then_inc(s["yg2"], 1)

            def out(k):
                for q in range(CHP):
                    dve.wait_ge(s["o_ps"], 4 * k + q + 1)
                    for j in range(2):
                        p = PS[2 * (q % 2) + j][:, 0:160].rearrange("p (k n) -> p k n", n=N)
                        ins = dve.tensor_copy(oT[:, :, q, j, :], p)
                    ins.then_inc(s["oT_out"], 1)
                dve.wait_ge(s["f_ps"], k + 1)
                x = chunk_cols(g.XT, k)
                dve.scalar_tensor_tensor(x, PS[6][:, 0:CH], outb[:, 0:1], x, ALU.add, ALU.add)

            def columns(k):
                dve.wait_ge(s["g_ps"], k + 1)
                dts = PS[7][:, 288:288 + CHP * DTR].rearrange("p (q r) -> p r q", r=DTR)
                for a in range(2):
                    dve.tensor_copy(dtc[:, a], dts[:, 32 * a:32 * a + SH_, :])
                dve.wait_ge(s["xt_out"], 4 * k + 4)
                dve.tensor_reduce(Dc[:].rearrange("p h q -> p q h"), share[:].rearrange("p q t h -> p q h t"), AX.X, ALU.add)
                dve.drain()
                dve.tensor_tensor(Dc[:], Dc[:], PS[7][:, 256:256 + CHP * SH_].rearrange("p (q h) -> p h q", h=SH_), ALU.add)
                dve.drain()
                dve.tensor_tensor(Dc[:], Dc[:], Dp[:, :, None].broadcast_to([128, SH_, CHP]), ALU.add)
                dve.drain()

            def turn(c, par):
                if there(c + 1):
                    states(c + 1)
                if there(c):
                    decayed(c, 0)
                if there(c + 1):
                    dt_ready(c + 1)
                if there(c):
                    dve.drain()
                    decayed(c, 1)
                    weights(c)
                if there(c + 1):
                    convolve(c + 1)
                if there(c):
                    gate(c, par)
                    rms(c)
                if there(c + 2):
                    softmax(c + 2)
                if there(c):
                    out(c)
                if there(c + 1):
                    columns(c + 1)
            all_turns(dve, turn)


def graph_network(nc, g):
    with ExitStack() as ctx:
        sb = lambda name, shape, dt=F32: ctx.enter_context(nc.sbuf_tensor(name, shape, dt))
        g.XT, g.XNP, g.XNG = sb("XT", [128, T]), sb("XNP", [128, B, SLOT]), sb("XNG", [128, PAIRS, D])
        g.ident, g.mean_w, g.eps = sb("ident", [128, 128]), sb("mean_w", [128, 128]), sb("eps", [128, 1])
        g.mean_row, g.row = sb("mean_row", [128, LNR, LNR]), sb("row", [96, LNR, 128], BF16)
        g.inv = sb("inv", [96, 2, CH], BF16)
        load_x(nc, g)
        with nc.sbuf_tensor("adjG0", [128, PAIRS, N], F32) as adjG, nc.sbuf_tensor("adjT0", [128, PAIRS, N], F32) as adjT, \
                nc.sbuf_tensor("betaT", [128, 4, N], F32) as betaT:
            g.adjG, g.adjT, g.betaT = adjG, adjT, betaT
            load_adjacency(nc, g, "a0", True)
            layer_norm(nc, g, g.XT, True, "n0")
            l0_gnn(nc, g)
        layer_norm(nc, g, g.XT, False, "n1")
        l0_ffn(nc, g)

        g.GT, g.iof, g.work = sb("GT", [24, T], BF16), sb("iof", [128, 128]), sb("work", [128, EC])
        g.ones = sb("ones", [128, 128])
        g.turns, g.cntB = sb("turns", [1, 2], I32), sb("cntB", [128, TT])
        edge_keys(nc, g)
        g.adjG, g.adjT = sb("adjG", [128, PAIRS, N]), sb("adjT", [128, PAIRS, N])
        load_adjacency(nc, g, "a1", False)
        layer_norm(nc, g, g.XT, True, "n2")
        l1_gnn(nc, g)
        layer_norm(nc, g, g.XT, False, "n3")
        layer_norm(nc, g, g.XNP, False, "n4")
        affine_xn(nc, g, g.L1_ffn_gamma, g.L1_ffn_beta)
        router(nc, g, "r1", 8, g.L1_ffn_Wr, g.L1_ffn_br, True)
        moe(nc, g, "f1", 8, g.L1_ffn_W1, g.L1_ffn_b1, g.L1_ffn_W2, g.L1_ffn_b2)
        layer_norm(nc, g, g.XT, True, "n5")
        l2_gnn(nc, g)
        layer_norm(nc, g, g.XT, False, "n6")
        edge_router(nc, g)
        moe(nc, g, "f2", EXP, g.L2_ffn_W1, g.L2_ffn_b1, g.L2_ffn_W2, g.L2_ffn_b2)
        layer_norm(nc, g, g.XT, True, "n7")
        l3_gnn(nc, g)
        layer_norm(nc, g, g.XT, False, "n8")
        router(nc, g, "r3", 8, g.L3_ffn_Wg, g.L3_ffn_bg, False)
        moe(nc, g, "f3", 8, g.L3_ffn_W1, g.L3_ffn_b1, g.L3_ffn_W2, g.L3_ffn_b2)
        store_output(nc, g)


def build(nc, x, adj, nodemask, L0_gnn_W, L0_gnn_bn_gamma, L0_gnn_bn_beta, L0_ffn_W_fx, L0_ffn_b_fx, L0_ffn_W_x, L0_ffn_b_x, L0_ffn_W_slice, L0_ffn_b_slice, L0_ffn_temperature, L0_ffn_hy_in_w, L0_ffn_hy_conv_w, L0_ffn_hy_conv_b, L0_ffn_hy_dt_bias, L0_ffn_hy_A_log, L0_ffn_hy_D, L0_ffn_hy_fcD_w, L0_ffn_hy_norm_w, L0_ffn_hy_out_w, L0_ffn_out_w, L0_ffn_out_b, L1_gnn_weight, L1_gnn_bias, L1_gnn_gamma, L1_gnn_beta, L1_ffn_gamma, L1_ffn_beta, L1_ffn_Wr, L1_ffn_br, L1_ffn_W1, L1_ffn_b1, L1_ffn_W2, L1_ffn_b2, L2_gnn_W, L2_ffn_W_gat, L2_ffn_att_src, L2_ffn_att_dst, L2_ffn_b_gat, L2_ffn_ln_gamma, L2_ffn_ln_beta, L2_ffn_W1, L2_ffn_b1, L2_ffn_W2, L2_ffn_b2, L2_ffn_edge_index, L3_gnn_fc_w, L3_gnn_fc_b, L3_gnn_q_w, L3_gnn_q_b, L3_gnn_k_w, L3_gnn_k_b, L3_gnn_fp_w, L3_gnn_fp_b, L3_ffn_Wg, L3_ffn_bg, L3_ffn_W1, L3_ffn_b1, L3_ffn_W2, L3_ffn_b2, out):
    g = Buffers()
    g.x, g.adj, g.nodemask, g.L0_gnn_W = x, adj, nodemask, L0_gnn_W
    g.L0_gnn_bn_gamma, g.L0_gnn_bn_beta, g.L0_ffn_W_fx, g.L0_ffn_b_fx = L0_gnn_bn_gamma, L0_gnn_bn_beta, L0_ffn_W_fx, L0_ffn_b_fx
    g.L0_ffn_W_x, g.L0_ffn_b_x, g.L0_ffn_W_slice, g.L0_ffn_b_slice = L0_ffn_W_x, L0_ffn_b_x, L0_ffn_W_slice, L0_ffn_b_slice
    g.L0_ffn_temperature, g.L0_ffn_hy_in_w, g.L0_ffn_hy_conv_w, g.L0_ffn_hy_conv_b = L0_ffn_temperature, L0_ffn_hy_in_w, L0_ffn_hy_conv_w, L0_ffn_hy_conv_b
    g.L0_ffn_hy_dt_bias, g.L0_ffn_hy_A_log, g.L0_ffn_hy_D, g.L0_ffn_hy_fcD_w = L0_ffn_hy_dt_bias, L0_ffn_hy_A_log, L0_ffn_hy_D, L0_ffn_hy_fcD_w
    g.L0_ffn_hy_norm_w, g.L0_ffn_hy_out_w, g.L0_ffn_out_w, g.L0_ffn_out_b = L0_ffn_hy_norm_w, L0_ffn_hy_out_w, L0_ffn_out_w, L0_ffn_out_b
    g.L1_gnn_weight, g.L1_gnn_bias, g.L1_gnn_gamma, g.L1_gnn_beta = L1_gnn_weight, L1_gnn_bias, L1_gnn_gamma, L1_gnn_beta
    g.L1_ffn_gamma, g.L1_ffn_beta, g.L1_ffn_Wr, g.L1_ffn_br = L1_ffn_gamma, L1_ffn_beta, L1_ffn_Wr, L1_ffn_br
    g.L1_ffn_W1, g.L1_ffn_b1, g.L1_ffn_W2, g.L1_ffn_b2 = L1_ffn_W1, L1_ffn_b1, L1_ffn_W2, L1_ffn_b2
    g.L2_gnn_W, g.L2_ffn_W_gat, g.L2_ffn_att_src, g.L2_ffn_att_dst = L2_gnn_W, L2_ffn_W_gat, L2_ffn_att_src, L2_ffn_att_dst
    g.L2_ffn_b_gat, g.L2_ffn_ln_gamma, g.L2_ffn_ln_beta, g.L2_ffn_W1 = L2_ffn_b_gat, L2_ffn_ln_gamma, L2_ffn_ln_beta, L2_ffn_W1
    g.L2_ffn_b1, g.L2_ffn_W2, g.L2_ffn_b2, g.L2_ffn_edge_index = L2_ffn_b1, L2_ffn_W2, L2_ffn_b2, L2_ffn_edge_index
    g.L3_gnn_fc_w, g.L3_gnn_fc_b, g.L3_gnn_q_w, g.L3_gnn_q_b = L3_gnn_fc_w, L3_gnn_fc_b, L3_gnn_q_w, L3_gnn_q_b
    g.L3_gnn_k_w, g.L3_gnn_k_b, g.L3_gnn_fp_w, g.L3_gnn_fp_b = L3_gnn_k_w, L3_gnn_k_b, L3_gnn_fp_w, L3_gnn_fp_b
    g.L3_ffn_Wg, g.L3_ffn_bg, g.L3_ffn_W1, g.L3_ffn_b1 = L3_ffn_Wg, L3_ffn_bg, L3_ffn_W1, L3_ffn_b1
    g.L3_ffn_W2, g.L3_ffn_b2 = L3_ffn_W2, L3_ffn_b2
    g.out = out
    graph_network(nc, g)


_INS = ['x', 'adj', 'nodemask', 'L0_gnn_W', 'L0_gnn_bn_gamma', 'L0_gnn_bn_beta', 'L0_ffn_W_fx', 'L0_ffn_b_fx', 'L0_ffn_W_x', 'L0_ffn_b_x', 'L0_ffn_W_slice', 'L0_ffn_b_slice', 'L0_ffn_temperature', 'L0_ffn_hy_in_w', 'L0_ffn_hy_conv_w', 'L0_ffn_hy_conv_b', 'L0_ffn_hy_dt_bias', 'L0_ffn_hy_A_log', 'L0_ffn_hy_D', 'L0_ffn_hy_fcD_w', 'L0_ffn_hy_norm_w', 'L0_ffn_hy_out_w', 'L0_ffn_out_w', 'L0_ffn_out_b', 'L1_gnn_weight', 'L1_gnn_bias', 'L1_gnn_gamma', 'L1_gnn_beta', 'L1_ffn_gamma', 'L1_ffn_beta', 'L1_ffn_Wr', 'L1_ffn_br', 'L1_ffn_W1', 'L1_ffn_b1', 'L1_ffn_W2', 'L1_ffn_b2', 'L2_gnn_W', 'L2_ffn_W_gat', 'L2_ffn_att_src', 'L2_ffn_att_dst', 'L2_ffn_b_gat', 'L2_ffn_ln_gamma', 'L2_ffn_ln_beta', 'L2_ffn_W1', 'L2_ffn_b1', 'L2_ffn_W2', 'L2_ffn_b2', 'L2_ffn_edge_index', 'L3_gnn_fc_w', 'L3_gnn_fc_b', 'L3_gnn_q_w', 'L3_gnn_q_b', 'L3_gnn_k_w', 'L3_gnn_k_b', 'L3_gnn_fp_w', 'L3_gnn_fp_b', 'L3_ffn_Wg', 'L3_ffn_bg', 'L3_ffn_W1', 'L3_ffn_b1', 'L3_ffn_W2', 'L3_ffn_b2']
_OUTS = [((B, N, D), "float32")]


def kernel(**inputs):
    import numpy as _np
    import concourse.bacc as _bacc
    from concourse import mybir as _mybir
    from concourse.bass_utils import run_bass_kernel_spmd as _run

    nc = _bacc.Bacc("TRN2", target_bir_lowering=False, num_devices=1)
    arrays, args = {}, []
    for name in _INS:
        a = _np.ascontiguousarray(inputs[name])
        arrays[f"in_{name}_dram"] = a
        args.append(nc.dram_tensor(f"in_{name}_dram", a.shape, _mybir.dt.from_np(a.dtype), kind="ExternalInput").ap())
    for i, (shape, dtype) in enumerate(_OUTS):
        dt = _mybir.dt.from_np(_np.dtype(dtype))
        args.append(nc.dram_tensor(f"out_{i}_dram", shape, dt, kind="ExternalOutput").ap())
    build(nc, *args)
    r = _run(nc, [arrays], core_ids=[0])
    return r.results[0]["out_0_dram"]
```
